# Optimizing a Trainium2 kernel written in Bass

```python
import numpy as np
import jax
import jax.numpy as jnp

def _softmax(x, axis=-1):
    return jax.nn.softmax(x, axis=axis)

def _gelu(x):
    return jax.nn.gelu(x, approximate=True)

def _silu(x):
    return jax.nn.silu(x)

def _sigmoid(x):
    return jax.nn.sigmoid(x)

def _layernorm(x, axis=-1, eps=1e-05):
    m = jnp.mean(x, axis=axis, keepdims=True)
    v = jnp.var(x, axis=axis, keepdims=True)
    return (x - m) / jnp.sqrt(v + eps)

def _scatter_add(tgt, idx, src, axis=0):
    return tgt.at[idx].add(src)

def _segment_sum(src, seg, n):
    return jax.ops.segment_sum(src, seg, n)
kernel_name = 'mk_adaln_d1_jaxref_r8_56bee1'

def setup_inputs(seed: int=0):
    np.random.seed(seed)
    _w = jnp.asarray

    def _L0_attn_setup():
        import jax, jax.numpy as jnp
        import numpy as np
        EPS = 1e-05
        H = 16

        def rms(x, w=None):
            y = x * jax.lax.rsqrt(jnp.mean(jnp.square(x), axis=-1, keepdims=True) + EPS)
            return y * w if w is not None else y

        def rotate_every_two(x):
            x1 = x[..., ::2]
            x2 = x[..., 1::2]
            return jnp.stack([-x2, x1], axis=-1).reshape(x.shape)

        def theta_shift(x, sin, cos):
            return x * cos + rotate_every_two(x) * sin

        def retnet_rel_pos(S, Dh):
            angle = 1.0 / 10000.0 ** jnp.linspace(0.0, 1.0, Dh // 2)
            angle = jnp.repeat(angle, 2)
            idx = jnp.arange(S, dtype=jnp.float32)
            sin = jnp.sin(idx[:, None] * angle[None, :])
            cos = jnp.cos(idx[:, None] * angle[None, :])
            decay = jnp.log(1.0 - 2.0 ** (-5.0 - jnp.arange(H, dtype=jnp.float32)))
            i = jnp.arange(S)[:, None]
            j = jnp.arange(S)[None, :]
            expnt = jnp.where(i >= j, (i - j).astype(jnp.float32)[None, :, :] * decay[:, None, None], -jnp.inf)
            mask = jnp.exp(expnt)
            mask = jnp.nan_to_num(mask)
            mask = mask / jnp.sqrt(jnp.sum(mask, axis=-1, keepdims=True))
            return (sin, cos, mask)
        key = jax.random.key(seed)
        B, S, E, F = (4, 128, 256, 1024)
        ks = jax.random.split(key, 12)
        sE = 1.0 / np.sqrt(E)
        sF = 1.0 / np.sqrt(F)
        return {'x': jax.random.normal(ks[0], (B, S, E), jnp.float32), 'q_w': jax.random.normal(ks[1], (E, E), jnp.float32) * sE, 'k_w': jax.random.normal(ks[2], (E, E), jnp.float32) * sE, 'v_w': jax.random.normal(ks[3], (E, E), jnp.float32) * sE, 'g_w': jax.random.normal(ks[4], (E, E), jnp.float32) * sE, 'out_w': jax.random.normal(ks[5], (E, E), jnp.float32) * sE, 'fc1_w': jax.random.normal(ks[6], (E, F), jnp.float32) * sE, 'fc1_b': jnp.zeros((F,), jnp.float32), 'fc2_w': jax.random.normal(ks[7], (F, E), jnp.float32) * sF, 'fc2_b': jnp.zeros((E,), jnp.float32), 'retn_norm_w': jnp.ones((E,), jnp.float32), 'final_norm_w': jnp.ones((E,), jnp.float32)}
    _L0_attn_in = _L0_attn_setup()

    def _L0_ffn_setup():
        import jax, jax.numpy as jnp
        import numpy as np
        B, S, H = (4, 128, 256)
        E, K, I, SI = (16, 4, 176, 704)

        def _silu_mul(gu, inter):
            return jax.nn.silu(gu[:, :inter]) * gu[:, inter:]
        key = jax.random.key(seed)
        ks = jax.random.split(key, 7)
        s = 0.02
        return {'hidden_states': jax.random.normal(ks[0], (B, S, H), jnp.float32), 'gate_w': jax.random.normal(ks[1], (E, H), jnp.float32) * s, 'expert_gate_up': jax.random.normal(ks[2], (E, 2 * I, H), jnp.float32) * s, 'expert_down': jax.random.normal(ks[3], (E, H, I), jnp.float32) * s, 'shared_gate_up': jax.random.normal(ks[4], (2 * SI, H), jnp.float32) * s, 'shared_down': jax.random.normal(ks[5], (H, SI), jnp.float32) * s, 'shared_gate_vec': jax.random.normal(ks[6], (1, H), jnp.float32) * s}
    _L0_ffn_in = _L0_ffn_setup()
    _L0_c = _w((lambda *s: np.random.randn(*s).astype(np.float32) * 0.05)(1, 256))
    _L0_wmod = _w((lambda *s: np.random.randn(*s).astype(np.float32) * 0.05)(256, 6 * 256) * 256 ** (-0.5))
    _d = {'L0_attn_x': _L0_attn_in['x'], 'L0_attn_q_w': _L0_attn_in['q_w'], 'L0_attn_k_w': _L0_attn_in['k_w'], 'L0_attn_v_w': _L0_attn_in['v_w'], 'L0_attn_g_w': _L0_attn_in['g_w'], 'L0_attn_out_w': _L0_attn_in['out_w'], 'L0_attn_fc1_w': _L0_attn_in['fc1_w'], 'L0_attn_fc1_b': _L0_attn_in['fc1_b'], 'L0_attn_fc2_w': _L0_attn_in['fc2_w'], 'L0_attn_fc2_b': _L0_attn_in['fc2_b'], 'L0_attn_retn_norm_w': _L0_attn_in['retn_norm_w'], 'L0_attn_final_norm_w': _L0_attn_in['final_norm_w'], 'L0_ffn_gate_w': _L0_ffn_in['gate_w'], 'L0_ffn_expert_gate_up': _L0_ffn_in['expert_gate_up'], 'L0_ffn_expert_down': _L0_ffn_in['expert_down'], 'L0_ffn_shared_gate_up': _L0_ffn_in['shared_gate_up'], 'L0_ffn_shared_down': _L0_ffn_in['shared_down'], 'L0_ffn_shared_gate_vec': _L0_ffn_in['shared_gate_vec'], 'L0_c': _L0_c, 'L0_wmod': _L0_wmod}
    _x0 = _d['L0_attn_x']
    _d['L0_attn_x'] = jax.random.normal(jax.random.fold_in(jax.random.key(seed), 1), (1, 2048, 256), dtype=_x0.dtype)
    del _x0
    return _d

def reference(L0_attn_x, L0_attn_q_w, L0_attn_k_w, L0_attn_v_w, L0_attn_g_w, L0_attn_out_w, L0_attn_fc1_w, L0_attn_fc1_b, L0_attn_fc2_w, L0_attn_fc2_b, L0_attn_retn_norm_w, L0_attn_final_norm_w, L0_ffn_gate_w, L0_ffn_expert_gate_up, L0_ffn_expert_down, L0_ffn_shared_gate_up, L0_ffn_shared_down, L0_ffn_shared_gate_vec, L0_c, L0_wmod):

    def _L0_attn_ref(x, q_w, k_w, v_w, g_w, out_w, fc1_w, fc1_b, fc2_w, fc2_b, retn_norm_w, final_norm_w):
        import jax, jax.numpy as jnp
        import numpy as np
        EPS = 1e-05
        H = 16

        def rms(x, w=None):
            y = x * jax.lax.rsqrt(jnp.mean(jnp.square(x), axis=-1, keepdims=True) + EPS)
            return y * w if w is not None else y

        def rotate_every_two(x):
            x1 = x[..., ::2]
            x2 = x[..., 1::2]
            return jnp.stack([-x2, x1], axis=-1).reshape(x.shape)

        def theta_shift(x, sin, cos):
            return x * cos + rotate_every_two(x) * sin

        def retnet_rel_pos(S, Dh):
            angle = 1.0 / 10000.0 ** jnp.linspace(0.0, 1.0, Dh // 2)
            angle = jnp.repeat(angle, 2)
            idx = jnp.arange(S, dtype=jnp.float32)
            sin = jnp.sin(idx[:, None] * angle[None, :])
            cos = jnp.cos(idx[:, None] * angle[None, :])
            decay = jnp.log(1.0 - 2.0 ** (-5.0 - jnp.arange(H, dtype=jnp.float32)))
            i = jnp.arange(S)[:, None]
            j = jnp.arange(S)[None, :]
            expnt = jnp.where(i >= j, (i - j).astype(jnp.float32)[None, :, :] * decay[:, None, None], -jnp.inf)
            mask = jnp.exp(expnt)
            mask = jnp.nan_to_num(mask)
            mask = mask / jnp.sqrt(jnp.sum(mask, axis=-1, keepdims=True))
            return (sin, cos, mask)
        B, S, E = x.shape
        Dh = E // H
        scaling = Dh ** (-0.5)
        sin, cos, mask = retnet_rel_pos(S, Dh)
        residual = x
        h = rms(x, retn_norm_w)
        q = h @ q_w
        k = h @ k_w * scaling
        v = h @ v_w
        g = h @ g_w

        def split_heads(t):
            return t.reshape(B, S, H, Dh).transpose(0, 2, 1, 3)
        q, k, v_h = (split_heads(q), split_heads(k), split_heads(v))
        qr = theta_shift(q, sin, cos)
        kr = theta_shift(k, sin, cos)
        qk = jnp.einsum('bhsd,bhtd->bhst', qr, kr) * mask
        denom = jnp.clip(jnp.abs(jax.lax.stop_gradient(jnp.sum(qk, axis=-1, keepdims=True))), 1.0, None)
        qk = qk / denom
        o = jnp.einsum('bhst,bhtd->bhsd', qk, v_h)
        o = o.transpose(0, 2, 1, 3)
        o = rms(o)
        o = o.reshape(B, S, E)
        o = jax.nn.silu(g) * o
        o = o @ out_w
        x = residual + o
        residual = x
        h = rms(x, final_norm_w)
        h = jax.nn.gelu(h @ fc1_w + fc1_b)
        h = h @ fc2_w + fc2_b
        return residual + h

    def _L0_ffn_ref(hidden_states, gate_w, expert_gate_up, expert_down, shared_gate_up, shared_down, shared_gate_vec):
        import jax, jax.numpy as jnp
        import numpy as np
        B, S, H = (4, 128, 256)
        E, K, I, SI = (16, 4, 176, 704)

        def _silu_mul(gu, inter):
            return jax.nn.silu(gu[:, :inter]) * gu[:, inter:]
        orig_shape = hidden_states.shape
        x = hidden_states.reshape(-1, H)
        router_logits = x @ gate_w.T
        routing_probs = jax.nn.softmax(router_logits.astype(jnp.float32), axis=-1)
        topk_w, topk_idx = jax.lax.top_k(routing_probs, K)
        topk_w = topk_w / topk_w.sum(axis=-1, keepdims=True)
        topk_w = topk_w.astype(x.dtype)
        combine = (jax.nn.one_hot(topk_idx, E, dtype=x.dtype) * topk_w[..., None]).sum(1)
        shared = _silu_mul(x @ shared_gate_up.T, SI) @ shared_down.T
        shared = shared * jax.nn.sigmoid(x @ shared_gate_vec.T)

        def step(acc, ew):
            w_gu, w_d, cw = ew
            h = _silu_mul(x @ w_gu.T, I)
            return (acc + h @ w_d.T * cw[:, None], None)
        acc0 = jnp.zeros_like(x)
        sparse, _ = jax.lax.scan(step, acc0, (expert_gate_up, expert_down, combine.T))
        return (shared + sparse).reshape(orig_shape)
    x = L0_attn_x
    mod = (_silu(L0_c) @ L0_wmod).reshape(L0_c.shape[0], 6, 1, -1)
    sa, ca, ga, sb, cb, gb = (mod[:, 0], mod[:, 1], mod[:, 2], mod[:, 3], mod[:, 4], mod[:, 5])
    ga = (2 * (ga >= 0) - 1) * jnp.maximum(jnp.abs(ga), 0.25)
    gb = (2 * (gb >= 0) - 1) * jnp.maximum(jnp.abs(gb), 0.25)
    h = _layernorm(x, axis=-1) * (1 + ca) + sa
    x = x + ga * _L0_attn_ref(h, L0_attn_q_w, L0_attn_k_w, L0_attn_v_w, L0_attn_g_w, L0_attn_out_w, L0_attn_fc1_w, L0_attn_fc1_b, L0_attn_fc2_w, L0_attn_fc2_b, L0_attn_retn_norm_w, L0_attn_final_norm_w)
    h = _layernorm(x, axis=-1) * (1 + cb) + sb
    x = x + gb * _L0_ffn_ref(h, L0_ffn_gate_w, L0_ffn_expert_gate_up, L0_ffn_expert_down, L0_ffn_shared_gate_up, L0_ffn_shared_down, L0_ffn_shared_gate_vec)
    return x

_drawn_inputs = setup_inputs


def setup_inputs(seed=0):
    import zlib

    import numpy as np

    out = dict(_drawn_inputs(seed))
    spreads = {'L0_attn_fc1_b': (0.0, 0.507),
     'L0_attn_fc2_b': (0.0, 0.317),
     'L0_attn_retn_norm_w': (1.0, 0.2),
     'L0_attn_final_norm_w': (1.0, 0.537)}
    factors = {'L0_ffn_gate_w': 8.0,
     'L0_ffn_expert_gate_up': 8.0,
     'L0_ffn_expert_down': 8.0,
     'L0_ffn_shared_gate_up': 8.0,
     'L0_ffn_shared_down': 8.0,
     'L0_ffn_shared_gate_vec': 8.0}
    for name, (base, spread) in spreads.items():
        noise = np.random.default_rng([zlib.crc32(name.encode()), seed]).standard_normal(out[name].shape)
        drawn = base * np.exp(spread * noise) if base else spread * noise
        out[name] = jnp.asarray(drawn.astype(out[name].dtype))
    for name, factor in factors.items():
        out[name] = (out[name] * factor).astype(out[name].dtype)
    return out
```

```python
from contextlib import ExitStack

import numpy as np
import concourse.bass as bass
from concourse import mybir

F32 = mybir.dt.float32
F32R = mybir.dt.float32r
ALU = mybir.AluOpType
ACT = mybir.ActivationFunctionType
AX = mybir.AxisListType

P = 128
N = 2048
E = 256
KB = E // P
NT = N // P
H = 16
DH = E // H
PAIRS = H // 2
STRIP = 32
F = 1024
FB = F // P
NX = 16
NR = NX + 1
TOPK = 4
I = 176
IT = I - P
GU = 2 * I
SI = 704
SBLOCKS = [(0, 128), (128, 128), (256, 128), (384, 128), (512, 96), (608, 96)]
ETILES = N * TOPK // P + NX
ROW = E + 4
SPARE = N * TOPK
G = 512
NG = N // G
TPG = G // P
EPS = 1e-5


def shape_tables():
    f32 = np.float32
    angle = (f32(1.0) / f32(10000.0) ** np.linspace(0.0, 1.0, DH // 2, dtype=f32)).astype(f32)
    phase = (np.arange(N, dtype=f32)[:, None] * angle[None, :]).astype(f32)
    cos = np.repeat(np.cos(phase), 2, axis=1).astype(f32)
    sin = np.repeat(np.sin(phase), 2, axis=1).astype(f32)
    sin[:, 0::2] *= -1
    tiled = lambda a: np.ascontiguousarray(a.reshape(NT, P, -1).transpose(1, 0, 2)).astype(f32)
    log_gamma = np.log(f32(1.0) - f32(2.0) ** (f32(-5.0) - np.arange(H, dtype=f32))).astype(np.float64)
    s = np.arange(P)
    dist = s[None, :] - s[:, None]
    decay = np.where(dist[:, None, :] >= 0, np.exp(np.maximum(dist, 0)[:, None, :] * log_gamma[None, :, None]), 0.0)
    q_decay = np.exp((s[:, None] + 1) * log_gamma[None, :])
    v_decay = np.exp((P - 1 - s[:, None]) * log_gamma[None, :])
    norm = np.sqrt(np.cumsum(np.exp(np.arange(N)[:, None] * log_gamma[None, :]), axis=0))
    chunk = np.exp(P * log_gamma)
    same = (np.arange(P)[:, None] // DH == np.arange(H)[None, :] % (H // 2)).astype(f32)
    state_mask = np.broadcast_to(same[:, :, None], (P, H, DH + 1))
    state_decay = np.broadcast_to(chunk[None, :, None], (P, H, DH + 1))
    return {
        "t_cos": tiled(cos), "t_sin": tiled(sin), "t_norm": tiled(norm),
        "t_decay": decay.astype(f32).reshape(P, H * P), "t_qdecay": q_decay.astype(f32), "t_vdecay": v_decay.astype(f32),
        "t_smask": np.ascontiguousarray(state_mask).astype(f32), "t_sdecay": np.ascontiguousarray(state_decay).astype(f32),
        "t_ident": np.eye(P, dtype=f32),
        "t_before": np.ascontiguousarray(np.broadcast_to(np.tril(np.ones((NX, NX), f32), -1)[None], (P, NX, NX))),
        "t_later": np.triu(np.ones((P, P), f32), 1),
        "t_steps": np.ascontiguousarray(np.broadcast_to((P * np.arange(NX, dtype=f32))[None], (P, NX))),
        "t_tiles": np.ascontiguousarray(np.broadcast_to(np.arange(ETILES, dtype=f32)[None], (P, ETILES))),
        "t_dest": (np.arange(TOPK)[None, :, None] * N + np.arange(NT)[None, None, :] * P + s[:, None, None]).astype(np.int32),
        "t_spare": (SPARE + np.arange(4)[None, :] * P + s[:, None]).astype(np.int32),
    }


def per(count, t):
    return t * count + count


def upto(t):
    return min(t + 1, NT) if isinstance(t, int) else t + 1


def build(nc, io, out):
    ctx = ExitStack()
    dram = {n: nc.dram_tensor(n, shape, F32, kind="Internal").ap() for n, shape in (
        ("dispatched", (ETILES * P, ROW)), ("results", (N * TOPK + 4 * P, E)), ("x3_rows", (N, E)), ("x4_rows", (N, E)))}
    with ctx:
        scopes = [ctx]

        def sb(name, shape, dt=F32, side="left"):
            return scopes[-1].enter_context(nc.sbuf_tensor(name, shape, dt, side=side))

        phase_sems = []

        def sem(name):
            phase_sems.append(nc.alloc_semaphore(name))
            return phase_sems[-1]

        def release_sems():
            nc.clear_and_free_semaphores(phase_sems)
            nc.all_engine_barrier()
            phase_sems.clear()

        def alone(eng):
            eng.nop(nofuse=True)

        def wait(eng, s, value):
            if isinstance(value, int) and value <= 0:
                return
            eng.wait_ge(s, value)

        bank = [ctx.enter_context(nc.psum_tensor(f"bank{b}", [P, 512], F32)) for b in range(8)]

        ident = sb("ident", [P, P])
        neghalf, eps = sb("neghalf", [P, H]), sb("eps", [P, H])
        gb = sb("gb", [P, E])
        weights = sb("weights", [P, TOPK, NT])
        tile_expert = sb("tile_expert", [P, ETILES], mybir.dt.int32)
        s_filled = nc.alloc_semaphore("filled")

        with ExitStack() as routed:
            with ExitStack() as attended:
                scopes.append(attended)
                modb = sb("modb", [P, 6, E])
                h_all = sb("h_all", [P, NT, E])
                x2T = [sb(f"x2T_{n}", [P, KB, N], F32R) for n in ("hi", "lo")]
                wf1 = [sb(f"wf1_{n}", [P, KB, F], F32R) for n in ("hi", "lo")]
                wf2 = [sb(f"wf2_{n}", [P, FB, E], F32R) for n in ("hi", "lo")]
                setup_and_attention(nc, io, scopes, sb, sem, wait, alone, bank, ident, neghalf, eps, modb, gb,
                                    h_all, x2T, wf1, wf2)
                release_sems()
                scopes.append(routed)
                h3T = [sb(f"h3T_{n}", [P, KB, N], F32R, side="right") for n in ("hi", "lo")]
                rows = sb("rows", [P, NT, ROW], side="right")
                logits = sb("logits", [P, NT, NR], side="right")
                order = sb("order", [P, NT, NX], side="right")
                chosen = sb("chosen", [P, NT, NX], side="right")
                before_tile = sb("before_tile", [P, NT + 1, NX], side="right")
                ebefore = sb("ebefore", [P, NX, NX], side="right")
                scopes.pop()
                mlp(nc, io, scopes, sb, sem, wait, alone, bank, ident, neghalf, eps, modb, h_all, x2T, wf1, wf2, h3T,
                    rows, logits, order, chosen, before_tile, ebefore, dram, s_filled)
                release_sems()
                scopes.pop()
            wgu = [sb(f"wgu_{n}", [P, KB, NX, GU], F32R) for n in ("hi", "lo")]
            shared_and_dispatch(nc, io, scopes, sb, sem, wait, alone, bank, gb, weights, tile_expert, h3T, rows, logits,
                                order, chosen, before_tile, ebefore, wgu, dram, s_filled)
            release_sems()
        experts(nc, io, scopes, sb, sem, wait, alone, bank, ident, gb, weights, tile_expert, wgu, dram, out)


def setup_and_attention(nc, io, scopes, sb, sem, wait, alone, bank, ident, neghalf, eps, modb, gb, h_all, x2T, wf1, wf2):
    with ExitStack() as local:
        scopes.append(local)
        cos, sin = sb("cos", [P, NT, DH]), sb("sin", [P, NT, DH])
        norm = sb("norm", [P, NT, H])
        decay = sb("decay", [P, H, P])
        qdecay, vdecay = sb("qdecay", [P, H]), sb("vdecay", [P, H])
        smask, sdecay = sb("smask", [P, H, DH + 1]), sb("sdecay", [P, H, DH + 1])
        rw, fw = sb("rw", [P, KB]), sb("fw", [P, KB])
        rwk = sb("rwk", [P, KB])
        ccol, scol = sb("ccol", [P, KB]), sb("scol", [P, KB])
        wmod = sb("wmod", [P, KB, 6 * E])
        sign = sb("sign", [P, E])
        rot1, rot2 = sb("rot1", [P, 2 * H, DH]), sb("rot2", [P, 2 * H, DH])
        wo32 = rot1[:, :, :].rearrange("p (k h) d -> p k (h d)", k=KB)
        probs = sb("probs", [P, H, P])
        wq32 = probs[:, :, :].rearrange("p (k n) s -> p k (n s)", k=KB)
        w1_32 = h_all[:, 0:NT // 2, :].rearrange("p (k n) e -> p k (n e)", k=KB)
        w2_32 = h_all[:, NT // 2:NT, :]
        wq = [sb(f"wq_{n}", [P, KB, 4 * E], F32R) for n in ("hi", "lo")]
        wo = [sb(f"wo_{n}", [P, KB, E], F32R) for n in ("hi", "lo")]
        xt = sb("xt", [P, 2, E])
        st6, mv, ve, rstd = sb("st6", [P, 2, 6]), sb("mv", [P, 2, 2]), sb("ve", [P, 2, 1]), sb("rstd", [P, 2, 1])
        xn, hm = sb("xn", [P, 2, E]), sb("hm", [P, E])
        junk = sign
        ssq, ssq2 = sb("ssq", [P, 2, 1]), sb("ssq2", [P, 2, 1])
        mse, mse2 = sb("mse", [P, 2, 1]), sb("mse2", [P, 2, 1])
        rms, rms2 = sb("rms", [P, 2, 1]), sb("rms2", [P, 2, 1])
        hr, x2r = sb("hr", [P, 2, E]), sb("x2r", [P, 2, E])
        hT = [sb(f"hT_{n}", [P, 2, KB, P], F32R) for n in ("hi", "lo")]
        qk = sb("qk", [P, 2, 2 * H, DH])
        qk2 = sb("qk2", [P, 2 * H, 4, DH], F32R)
        q_parts, k_parts = qk2[:, 0:H, :, :], qk2[:, H:2 * H, :, :]
        HI, LO = (q_parts[:, :, 0:2, :], k_parts[:, :, 0::2, :]), (q_parts[:, :, 2:4, :], k_parts[:, :, 1::2, :])

        def twice(heads):
            return heads.unsqueeze(2).broadcast_to([P, H, 2, DH])

        qs = sb("qs", [P, E])
        vpad = sb("vpad", [P, 2, H, STRIP])
        vs = sb("vs", [P, 2, H, DH + 1])
        sg = sb("sg", [P, 2, E])
        qbd = sb("qbd", [P, PAIRS, 2 * P], F32R)
        kT = sb("kT", [P, PAIRS, P], F32R)
        qsT = sb("qsT", [P, KB, P])
        state = sb("state", [P, H, STRIP])
        state_new, state_old = sb("state_new", [P, H, DH + 1]), sb("state_old", [P, H, DH + 1])
        oT = sb("oT", [P, 4, P])
        rabs, den, rden = sb("rabs", [P, H]), sb("den", [P, H]), sb("rden", [P, H])
        on, osq, og = sb("on", [P, H, DH]), sb("osq", [P, H, DH]), sb("og", [P, H, DH])
        oms, omse, orms = sb("oms", [P, H]), sb("omse", [P, H]), sb("orms", [P, H])
        y = sb("y", [P, 2, E])
        yT = [sb(f"yT_{n}", [P, KB, P], F32R) for n in ("hi", "lo")]

        b_hT, b_qk, b_vg, b_o = bank[0], bank[1], bank[2], bank[7]
        b_s = bank[3:7]

        names = """eps tables wload vecs wmod_in x_in0 x_in1 silu_c mod_ps mod_sb sgn gates prep wprep init
            st6 mv ve rstd xn hm h ssq mse rms hr hT_ps hT_hi hT_lo qk_ps vg_ps rope qk qk_hi qk_lo qs v sg vs
            qT_ps kT_ps q_ev k_ev qsT_ps qsT sc_ps probs inter o_ps st_ps st_new st_old state oT oTT_ps
            rabs den rden on osq og oms omse orms y yT_ps yT_hi yT_lo out_ps x2 ssq2 mse2 rms2 x2r x2T_ps x2_hi x2_lo""".split()
        S = {n: sem("s_" + n) for n in names}

        block = local.enter_context(nc.Block())
        x_tiles = io["L0_attn_x"].rearrange("a (t p) e -> (a t) p e", p=P)
        LAGS = 3

        def pipeline(eng, body):
            for t in range(6):
                body(t, t % 2, lambda lag, t=t: t - lag >= 0)
            with eng.Fori(3, NT // 2) as j:
                for p in range(2):
                    body(j * 2 + p, p, lambda lag: True)
            for t in range(NT, NT + LAGS):
                body(t, t % 2, lambda lag, t=t: t - lag < NT)

        @block.sync
        def _(sp):
            sp.dma_start(ccol[:, :], io["L0_c"]).then_inc(S["vecs"], 16)
            sp.dma_start(rw[:, :], io["L0_attn_retn_norm_w"]).then_inc(S["vecs"], 16)
            sp.dma_start(fw[:, :], io["L0_attn_final_norm_w"]).then_inc(S["vecs"], 16)
            sp.dma_start(wmod[:, :, :], io["L0_wmod"].rearrange("(k p) n -> p k n", p=P)).then_inc(S["wmod_in"], 16)
            for n, w in enumerate(("q", "k", "v", "g")):
                sp.dma_start(wq32[:, :, n * E:(n + 1) * E], io[f"L0_attn_{w}_w"].rearrange("(k p) n -> p k n", p=P)).then_inc(S["wload"], 16)
            sp.dma_start(wo32[:, :, :], io["L0_attn_out_w"].rearrange("(k p) n -> p k n", p=P)).then_inc(S["wload"], 16)
            sp.dma_start(w1_32[:, :, :], io["L0_attn_fc1_w"].rearrange("(k p) n -> p k n", p=P)).then_inc(S["wload"], 16)
            sp.dma_start(w2_32[:, :, :], io["L0_attn_fc2_w"].rearrange("(k p) n -> p k n", p=P)).then_inc(S["wload"], 16)

            def load_x(t, p):
                wait(sp, S["xn"], per(1, t - 2))
                sp.dma_start(xt[:, p, :], x_tiles[t, :, :]).then_inc(S[f"x_in{p}"], 16)

            load_x(0, 0)
            load_x(1, 1)
            with sp.Fori(1, NT // 2) as j:
                load_x(j * 2, 0)
                load_x(j * 2 + 1, 1)

        TABLES = [(ident, "t_ident"), (cos, "t_cos"), (sin, "t_sin"), (norm, "t_norm"), (qdecay, "t_qdecay"),
                  (vdecay, "t_vdecay"), (smask, "t_smask"), (sdecay, "t_sdecay"), (decay, "t_decay")]
        ALL_TABLES, ALL_W, PREP = 16 * len(TABLES), 16 * 7, 6
        W_SPLIT = 1 + 2 * (4 * KB + 1 + KB + 1)

        @block.scalar
        def _(act):
            for dst, name in TABLES:
                src = io[name]
                act.dma_start(dst[tuple([slice(None)] * len(dst.shape))],
                              src if len(src.shape) == len(dst.shape) else src.rearrange("p (h s) -> p h s", h=H)).then_inc(S["tables"], 16)
            act.wait_ge(S["vecs"], 48)
            nc.scalar.activation(scol[:, :], ccol[:, :], ACT.Silu).then_inc(S["silu_c"], 1)
            for c in range(3):
                act.wait_ge(S["mod_ps"], c + 1)
                nc.scalar.copy(modb[:, 2 * c:2 * c + 2, :], bank[c][:, :]).then_inc(S["mod_sb"], 1)
            act.wait_ge(S["init"], 1)
            act.wait_ge(S["prep"], PREP)

            def square_h(t, p):
                act.wait_ge(S["h"], per(1, t))
                wait(act, S["mse"], per(1, t - 2))
                nc.scalar.activation(junk[:, :], h_all[:, t, :], ACT.Square, scale=E ** -0.5, accum_out=ssq[:, p, :]).then_inc(S["ssq"], 1)

            def split_hT(t, p):
                act.wait_ge(S["hT_ps"], per(1, t))
                wait(act, S["vg_ps"], per(1, t - 2))
                nc.scalar.copy(hT[0][:, p, :, :], b_hT[:, 0:E]).then_inc(S["hT_hi"], 1)

            def split_qk(t, p):
                act.wait_ge(S["qk"], per(1, t))
                wait(act, S["kT_ps"], per(2, t - 1))
                for n in range(2):
                    nc.scalar.copy(HI[n], twice(qk[:, p, n * H:n * H + H, :])).then_inc(S["qk_hi"], 1)

            def value_gate(t, p):
                act.wait_ge(S["vg_ps"], per(1, t))
                wait(act, S["o_ps"], per(1, t - 2))
                wait(act, S["vs"], per(1, t - 2))
                nc.scalar.copy(vpad[:, p, :, 0:DH], b_vg[:, 0:E].rearrange("p (h d) -> p h d", d=DH)).then_inc(S["v"], 1)
                wait(act, S["og"], per(1, t - 2))
                nc.scalar.activation(sg[:, p, :], b_vg[:, E:2 * E], ACT.Silu).then_inc(S["sg"], 1)

            def evacuate_q(t, p):
                wait(act, S["sc_ps"], per(4, t - 1))
                for b in range(2):
                    act.wait_ge(S["qT_ps"], per(2, t) - 1 + b)
                    for half in range(2):
                        rows = slice(64 * half, 64 * half + 64)
                        nc.scalar.copy(qbd[rows, 4 * b:4 * b + 4, P * half:P * half + P],
                                       b_s[b][rows, :].rearrange("p (j s) -> p j s", s=P)).then_inc(S["q_ev"], 1)

            def evacuate_qsT(t, p):
                act.wait_ge(S["qsT_ps"], per(1, t))
                wait(act, S["inter"], per(1, t - 1))
                nc.scalar.copy(qsT[:, :, :], b_qk[:, 0:E]).then_inc(S["qsT"], 1)

            def evacuate_oT(t, p):
                act.wait_ge(S["o_ps"], per(1, t))
                wait(act, S["oTT_ps"], per(1, t - 1))
                nc.scalar.copy(oT[:, :, :], b_o[:, :]).then_inc(S["oT"], 1)

            def square_o(t, p):
                act.wait_ge(S["on"], per(1, t))
                wait(act, S["oms"], per(1, t - 1))
                nc.scalar.activation(osq[:, :, :], on[:, :, :], ACT.Square, scale=DH ** -0.5).then_inc(S["osq"], 1)

            def split_yT(t, p):
                act.wait_ge(S["yT_ps"], per(1, t))
                wait(act, S["out_ps"], per(1, t - 1))
                nc.scalar.copy(yT[0][:, :, :], b_vg[:, 0:E]).then_inc(S["yT_hi"], 1)

            def square_x2(t, p):
                act.wait_ge(S["x2"], per(1, t))
                wait(act, S["mse2"], per(1, t - 2))
                nc.scalar.activation(junk[:, :], h_all[:, t, :], ACT.Square, scale=E ** -0.5, accum_out=ssq2[:, p, :]).then_inc(S["ssq2"], 1)

            def split_x2T(t, p):
                act.wait_ge(S["x2T_ps"], per(1, t))
                nc.scalar.copy(x2T[0][:, :, bass.ds(t * P, P)], b_hT[:, 0:E].rearrange("p (k s) -> p k s", s=P)).then_inc(S["x2_hi"], 1)

            def body(t, p, live):
                q = 1 - p
                if live(1): value_gate(t - 1, q)
                if live(1): split_qk(t - 1, q)
                if live(0): square_h(t, p)
                if live(2): evacuate_oT(t - 2, p)
                if live(1): evacuate_q(t - 1, q)
                if live(1): evacuate_qsT(t - 1, q)
                if live(0): split_hT(t, p)
                if live(3): split_yT(t - 3, q)
                if live(2): square_o(t - 2, p)
                if live(3): square_x2(t - 3, q)
                if live(3): split_x2T(t - 3, q)

            pipeline(nc.scalar, body)

        @block.gpsimd
        def _(pool):
            nc.gpsimd.memset(neghalf[:, :], -0.5).then_inc(S["prep"], 1)
            nc.gpsimd.memset(eps[:, :], EPS).then_inc(S["eps"], 1)
            nc.gpsimd.memset(vpad[:, :, :, :], 0.0).then_inc(S["prep"], 1)
            nc.gpsimd.memset(state[:, :, :], 0.0).then_inc(S["prep"], 1)
            pool.wait_ge(S["eps"], 1)
            pool.wait_ge(S["prep"], 3)
            nc.gpsimd.memset(vpad[:, :, :, DH:DH + 1], 1.0).then_inc(S["prep"], 1)
            pool.wait_ge(S["tables"], ALL_TABLES)
            for p in range(2):
                nc.gpsimd.tensor_copy(vs[:, p, :, DH:DH + 1], vdecay[:, :].unsqueeze(2)).then_inc(S["prep"], 1)
            pool.wait_ge(S["prep"], PREP)
            pool.wait_ge(S["mod_sb"], 3)
            pool.wait_ge(S["sgn"], 1)
            pool.wait_ge(S["wprep"], W_SPLIT)

            def rms_scale(src, ready, tmp, tmp_name, dst, dst_name, t, p, reader):
                pool.wait_ge(S[ready], per(1, t))
                nc.gpsimd.tensor_tensor(tmp, src, eps[:, 0:tmp.shape[1]], ALU.add).then_inc(S[tmp_name], 1)
                pool.wait_ge(S[tmp_name], per(1, t))
                wait(pool, S[reader], per(1, t - 2))
                nc.gpsimd.tensor_tensor(dst, tmp, neghalf[:, 0:tmp.shape[1]], ALU.pow).then_inc(S[dst_name], 1)

            def rstd_x(t, p):
                pool.wait_ge(S["ve"], per(1, t))
                nc.gpsimd.tensor_tensor(rstd[:, p, :], ve[:, p, :], neghalf[:, 0:1], ALU.pow).then_inc(S["rstd"], 1)

            def modulate(t, p):
                pool.wait_ge(S["xn"], per(1, t))
                wait(pool, S["h"], per(1, t - 1))
                nc.gpsimd.tensor_tensor(hm[:, :], xn[:, p, :], modb[:, 1, :], ALU.mult).then_inc(S["hm"], 1)
                pool.wait_ge(S["hm"], per(1, t))
                nc.gpsimd.tensor_tensor(h_all[:, t, :], hm[:, :], modb[:, 0, :], ALU.add).then_inc(S["h"], 1)

            def rms_h(t, p):
                rms_scale(ssq[:, p, :], "ssq", mse[:, p, :], "mse", rms[:, p, :], "rms", t, p, "hr")

            def rope_add(t, p):
                pool.wait_ge(S["rope"], per(3, t))
                wait(pool, S["st_ps"], per(1, t - 2))
                nc.gpsimd.tensor_tensor(qk[:, p, :, :], rot1[:, :, :], rot2[:, :, :], ALU.add).then_inc(S["qk"], 1)

            def decay_q(t, p):
                pool.wait_ge(S["qk"], per(1, t))
                wait(pool, S["qsT_ps"], per(1, t - 1))
                nc.gpsimd.tensor_tensor(qs[:, :].rearrange("p (h d) -> p h d", d=DH), qk[:, p, 0:H, :],
                                        qdecay[:, :].unsqueeze(2).broadcast_to([P, H, DH]), ALU.mult).then_inc(S["qs"], 1)

            def decay_v(t, p):
                pool.wait_ge(S["v"], per(1, t))
                wait(pool, S["st_ps"], per(1, t - 2))
                nc.gpsimd.tensor_tensor(vs[:, p, :, 0:DH], vpad[:, p, :, 0:DH],
                                        vdecay[:, :].unsqueeze(2).broadcast_to([P, H, DH]), ALU.mult).then_inc(S["vs"], 1)

            def decay_state(t, p):
                wait(pool, S["state"], per(1, t - 1))
                nc.gpsimd.tensor_tensor(state_old[:, :, :], state[:, :, 0:DH + 1], sdecay[:, :, :], ALU.mult).then_inc(S["st_old"], 1)

            def gate_o(t, p):
                pool.wait_ge(S["on"], per(1, t))
                pool.wait_ge(S["sg"], per(1, t))
                wait(pool, S["y"], per(1, t - 1))
                nc.gpsimd.tensor_tensor(og[:, :, :], on[:, :, :], sg[:, p, :].rearrange("p (h d) -> p h d", d=DH), ALU.mult).then_inc(S["og"], 1)

            def rms_o(t, p):
                pool.wait_ge(S["oms"], per(1, t))
                nc.gpsimd.tensor_tensor(omse[:, :], oms[:, :], eps[:, :], ALU.add).then_inc(S["omse"], 1)
                pool.wait_ge(S["omse"], per(1, t))
                wait(pool, S["y"], per(1, t - 1))
                nc.gpsimd.tensor_tensor(orms[:, :], omse[:, :], neghalf[:, :], ALU.pow).then_inc(S["orms"], 1)

            def scale_o(t, p):
                pool.wait_ge(S["orms"], per(1, t))
                pool.wait_ge(S["og"], per(1, t))
                wait(pool, S["yT_ps"], per(1, t - 2))
                nc.gpsimd.tensor_tensor(y[:, p, :].rearrange("p (h d) -> p h d", d=DH), og[:, :, :],
                                        orms[:, :].unsqueeze(2).broadcast_to([P, H, DH]), ALU.mult).then_inc(S["y"], 1)

            def rms_x2(t, p):
                rms_scale(ssq2[:, p, :], "ssq2", mse2[:, p, :], "mse2", rms2[:, p, :], "rms2", t, p, "x2r")

            def body(t, p, live):
                q = 1 - p
                if live(0): rstd_x(t, p)
                if live(1): rope_add(t - 1, q)
                if live(1): decay_q(t - 1, q)
                if live(0): modulate(t, p)
                if live(1): decay_v(t - 1, q)
                if live(2): decay_state(t - 2, p)
                if live(0): rms_h(t, p)
                if live(2): gate_o(t - 2, p)
                if live(3): rms_x2(t - 3, q)
                if live(2): rms_o(t - 2, p)
                if live(2): scale_o(t - 2, p)

            pipeline(nc.gpsimd, body)

        @block.vector
        def _(dve):
            count = {}

            def step(name, ins):
                count[name] = count.get(name, 0) + 1
                ins.then_inc(S[name], 1)
                dve.wait_ge(S[name], count[name])

            nc.vector.memset(qbd[:, :, :].bitcast(F32), 0.0).then_inc(S["init"], 1)
            dve.wait_ge(S["mod_sb"], 3)
            ca1 = modb[:, 1, :]
            step("sgn", nc.vector.tensor_scalar(ca1, ca1, 1.0, None, ALU.add))
            for g, gated in ((modb[:, 2, :], modb[:, 2, :]), (modb[:, 5, :], gb[:, :])):
                step("sgn", nc.vector.tensor_scalar(sign[:, :], g, 0.0, 2.0, ALU.is_ge, ALU.mult))
                step("sgn", nc.vector.tensor_scalar(sign[:, :], sign[:, :], 1.0, None, ALU.subtract))
                step("sgn", nc.vector.tensor_tensor(g, g, sign[:, :], ALU.mult))
                step("gates", nc.vector.scalar_tensor_tensor(gated, g, 0.25, sign[:, :], ALU.max, ALU.mult))
            nc.vector.tensor_scalar(modb[:, 4, :], modb[:, 4, :], 1.0, None, ALU.add).then_inc(S["gates"], 1)
            dve.wait_ge(S["vecs"], 48)
            step("wprep", nc.vector.tensor_scalar(rwk[:, :], rw[:, :], float(DH) ** -0.5, None, ALU.mult))
            dve.wait_ge(S["wload"], ALL_W)

            def split(dst, src, scale):
                if scale is None:
                    step("wprep", nc.vector.tensor_copy(dst[0], src))
                    nc.vector.tensor_tensor(dst[1], src, dst[0].bitcast(F32), ALU.subtract).then_inc(S["wprep"], 1)
                else:
                    step("wprep", nc.vector.tensor_scalar(dst[0], src, scale, None, ALU.mult))
                    nc.vector.scalar_tensor_tensor(dst[1], src, scale, dst[0].bitcast(F32), ALU.mult, ALU.subtract).then_inc(S["wprep"], 1)
                count["wprep"] += 1

            for k in range(KB):
                for n in range(4):
                    cols = slice(n * E, (n + 1) * E)
                    split([w[:, k, cols] for w in wq], wq32[:, k, cols], (rwk if n == 1 else rw)[:, k:k + 1])
            split([w[:, :, :] for w in wo], wo32[:, :, :], None)
            for k in range(KB):
                split([w[:, k, :] for w in wf1], w1_32[:, k, :], fw[:, k:k + 1])
            split([w[:, :, :] for w in wf2], w2_32[:, :, :], None)
            dve.wait_ge(S["tables"], ALL_TABLES)
            dve.wait_ge(S["prep"], PREP)

            def stats(t, p):
                dve.wait_ge(S[f"x_in{p}"], (t - p) * 8 + 16)
                nc.vector.bn_stats(st6[:, p, :], xt[:, p, :]).then_inc(S["st6"], 1)
                dve.wait_ge(S["st6"], per(1, t))
                alone(dve)
                nc.vector.bn_aggr(mv[:, p, :], st6[:, p, :]).then_inc(S["mv"], 1)
                dve.wait_ge(S["mv"], per(1, t))
                wait(dve, S["rstd"], per(1, t - 2))
                nc.vector.tensor_scalar(ve[:, p, :], mv[:, p, 1:2], EPS, None, ALU.add).then_inc(S["ve"], 1)

            def normalise(t, p):
                dve.wait_ge(S["rstd"], per(1, t))
                wait(dve, S["hm"], per(1, t - 2))
                nc.vector.tensor_scalar(xn[:, p, :], xt[:, p, :], mv[:, p, 0:1], rstd[:, p, :], ALU.subtract, ALU.mult).then_inc(S["xn"], 1)

            def scale_h(t, p):
                dve.wait_ge(S["rms"], per(1, t))
                wait(dve, S["hT_ps"], per(1, t - 2))
                nc.vector.tensor_scalar(hr[:, p, :], h_all[:, t, :], rms[:, p, :], None, ALU.mult).then_inc(S["hr"], 1)

            def split_hT(t, p):
                dve.wait_ge(S["hT_hi"], per(1, t))
                wait(dve, S["vg_ps"], per(1, t - 2))
                nc.vector.tensor_tensor(hT[1][:, p, :, :].rearrange("p k s -> p (k s)"), b_hT[:, 0:E],
                                        hT[0][:, p, :, :].bitcast(F32).rearrange("p k s -> p (k s)"), ALU.subtract).then_inc(S["hT_lo"], 1)

            def rope(t, p):
                dve.wait_ge(S["qk_ps"], per(1, t))
                wait(dve, S["qk"], per(1, t - 1))
                heads = b_qk[:, :].rearrange("p (h d) -> p h d", d=DH)
                odd_even = b_qk[:, :].rearrange("p (h d two) -> p h d two", d=DH // 2, two=2)
                r2 = rot2[:, :, :].rearrange("p h (d two) -> p h d two", two=2)
                nc.vector.tensor_tensor(rot1[:, :, :], heads, cos[:, t, :].unsqueeze(1).broadcast_to([P, 2 * H, DH]), ALU.mult).then_inc(S["rope"], 1)
                sn = sin[:, t, :].rearrange("p (d two) -> p d two", two=2)
                for e in range(2):
                    nc.vector.tensor_tensor(r2[:, :, :, e], odd_even[:, :, :, 1 - e],
                                            sn[:, :, e].unsqueeze(1).broadcast_to([P, 2 * H, DH // 2]), ALU.mult).then_inc(S["rope"], 1)

            def split_qk(t, p):
                for n in range(2):
                    dve.wait_ge(S["qk_hi"], per(2, t) - 1 + n)
                    nc.vector.tensor_tensor(LO[n], twice(qk[:, p, n * H:n * H + H, :]), HI[n].bitcast(F32), ALU.subtract).then_inc(S["qk_lo"], 1)

            def evacuate_k(t, p):
                wait(dve, S["sc_ps"], per(4, t - 1))
                for b in range(2):
                    dve.wait_ge(S["kT_ps"], per(2, t) - 1 + b)
                    nc.vector.tensor_copy(kT[:, 4 * b:4 * b + 4, :], b_s[2 + b][:, :].rearrange("p (j s) -> p j s", s=P)).then_inc(S["k_ev"], 1)

            def mask(t, p):
                wait(dve, S["o_ps"], per(1, t - 1))
                for b in range(4):
                    dve.wait_ge(S["sc_ps"], per(4, t) - 3 + b)
                    nc.vector.tensor_tensor(probs[:, 4 * b:4 * b + 4, :], b_s[b][:, :].rearrange("p (h s) -> p h s", s=P),
                                            decay[:, 4 * b:4 * b + 4, :], ALU.mult).then_inc(S["probs"], 1)

            def update_state(t, p):
                dve.wait_ge(S["st_ps"], per(1, t))
                nc.vector.tensor_tensor(state_new[:, :, :], b_vg[:, 0:H * (DH + 1)].rearrange("p (h d) -> p h d", d=DH + 1),
                                        smask[:, :, :], ALU.mult).then_inc(S["st_new"], 1)
                dve.wait_ge(S["st_new"], per(1, t))
                dve.wait_ge(S["st_old"], per(1, t))
                dve.wait_ge(S["inter"], per(1, t))
                nc.vector.tensor_tensor(state[:, :, 0:DH + 1], state_new[:, :, :], state_old[:, :, :], ALU.add).then_inc(S["state"], 1)

            def normalise_o(t, p):
                dve.wait_ge(S["oTT_ps"], per(1, t))
                o = b_hT[:, :].rearrange("p (h d) -> p h d", d=STRIP)
                nc.vector.tensor_reduce(rabs[:, :], o[:, :, DH:DH + 1], AX.X, ALU.max, apply_absolute_value=True).then_inc(S["rabs"], 1)
                dve.wait_ge(S["rabs"], per(1, t))
                nc.vector.tensor_tensor(den[:, :], rabs[:, :], norm[:, t, :], ALU.max).then_inc(S["den"], 1)
                dve.wait_ge(S["den"], per(1, t))
                nc.vector.reciprocal(rden[:, :], den[:, :]).then_inc(S["rden"], 1)
                dve.wait_ge(S["rden"], per(1, t))
                wait(dve, S["og"], per(1, t - 1))
                wait(dve, S["osq"], per(1, t - 1))
                nc.vector.tensor_tensor(on[:, :, :], o[:, :, 0:DH], rden[:, :].unsqueeze(2).broadcast_to([P, H, DH]), ALU.mult).then_inc(S["on"], 1)

            def mean_square_o(t, p):
                dve.wait_ge(S["osq"], per(1, t))
                wait(dve, S["omse"], per(1, t - 1))
                nc.vector.tensor_reduce(oms[:, :], osq[:, :, :], AX.X, ALU.add).then_inc(S["oms"], 1)

            def split_yT(t, p):
                dve.wait_ge(S["yT_hi"], per(1, t))
                wait(dve, S["out_ps"], per(1, t - 1))
                nc.vector.tensor_tensor(yT[1][:, :, :].rearrange("p k s -> p (k s)"), b_vg[:, 0:E],
                                        yT[0][:, :, :].bitcast(F32).rearrange("p k s -> p (k s)"), ALU.subtract).then_inc(S["yT_lo"], 1)

            def residual(t, p):
                dve.wait_ge(S["out_ps"], per(1, t))
                nc.vector.tensor_tensor(h_all[:, t, :], b_qk[:, 0:E], h_all[:, t, :], ALU.add).then_inc(S["x2"], 1)

            def scale_x2(t, p):
                dve.wait_ge(S["rms2"], per(1, t))
                wait(dve, S["x2T_ps"], per(1, t - 2))
                nc.vector.tensor_scalar(x2r[:, p, :], h_all[:, t, :], rms2[:, p, :], None, ALU.mult).then_inc(S["x2r"], 1)

            def split_x2T(t, p):
                dve.wait_ge(S["x2_hi"], per(1, t))
                cols = bass.ds(t * P, P)
                nc.vector.tensor_tensor(x2T[1][:, :, cols], b_hT[:, 0:E].rearrange("p (k s) -> p k s", s=P),
                                        x2T[0][:, :, cols].bitcast(F32), ALU.subtract).then_inc(S["x2_lo"], 1)

            def body(t, p, live):
                q = 1 - p
                if live(0): stats(t, p)
                if live(1): rope(t - 1, q)
                if live(2): mask(t - 2, p)
                if live(0): normalise(t, p)
                if live(1): split_qk(t - 1, q)
                if live(2): update_state(t - 2, p)
                if live(0): scale_h(t, p)
                if live(1): evacuate_k(t - 1, q)
                if live(0): split_hT(t, p)
                if live(3): split_yT(t - 3, q)
                if live(2): normalise_o(t - 2, p)
                if live(3): residual(t - 3, q)
                if live(2): mean_square_o(t - 2, p)
                if live(3): scale_x2(t - 3, q)
                if live(3): split_x2T(t - 3, q)

            pipeline(nc.vector, body)

        @block.tensor
        def _(pe):
            pe.wait_ge(S["silu_c"], 1)
            pe.wait_ge(S["wmod_in"], 16)
            for c in range(3):
                for k in range(KB):
                    mm = nc.tensor.matmul(bank[c][:, :], scol[:, k:k + 1].broadcast_to([P, P]), wmod[:, k, 512 * c:512 * c + 512],
                                          start=(k == 0), stop=(k == KB - 1))
                mm.then_inc(S["mod_ps"], 1)
            pe.wait_ge(S["mod_sb"], 3)
            pe.wait_ge(S["wprep"], W_SPLIT)
            pe.wait_ge(S["tables"], ALL_TABLES)
            pe.wait_ge(S["prep"], PREP)

            def product3(dst, lhs, rhs, start, stop):
                nc.tensor.matmul(dst, lhs[0], rhs[0], start=start, stop=False)
                nc.tensor.matmul(dst, lhs[0], rhs[1], start=False, stop=False)
                return nc.tensor.matmul(dst, lhs[1], rhs[0], start=False, stop=stop)

            def transpose_h(t, p):
                pe.wait_ge(S["hr"], per(1, t))
                wait(pe, S["hT_lo"], per(1, t - 1))
                wait(pe, S["x2_lo"], per(1, t - 4))
                wait(pe, S["on"], per(1, t - 3))
                for k in range(KB):
                    tr = nc.tensor.transpose(b_hT[:, k * P:k * P + P], hr[:, p, k * P:k * P + P], ident[:, :])
                tr.then_inc(S["hT_ps"], 1)

            def project(t, p):
                pe.wait_ge(S["hT_lo"], per(1, t))
                wait(pe, S["rope"], per(3, t - 1))
                wait(pe, S["qsT"], per(1, t - 1))
                wait(pe, S["x2"], per(1, t - 3))
                for k in range(KB):
                    mm = product3(b_qk[:, :], [a[:, p, k, :] for a in hT], [w[:, k, 0:512] for w in wq], k == 0, k == KB - 1)
                mm.then_inc(S["qk_ps"], 1)
                wait(pe, S["sg"], per(1, t - 1))
                wait(pe, S["st_new"], per(1, t - 2))
                wait(pe, S["yT_lo"], per(1, t - 3))
                for k in range(KB):
                    mm = product3(b_vg[:, :], [a[:, p, k, :] for a in hT], [w[:, k, 512:1024] for w in wq], k == 0, k == KB - 1)
                mm.then_inc(S["vg_ps"], 1)

            def transpose_qk(t, p):
                wait(pe, S["probs"], per(4, t - 1))
                for n, done in enumerate(("qT_ps", "kT_ps")):
                    pe.wait_ge(S["qk_lo"], per(2, t) - 1 + n)
                    for j in range(PAIRS):
                        src = qk2[:, n * H + 2 * j:n * H + 2 * j + 2, :, :].bitcast(F32).rearrange("p h part d -> p (h part d)")
                        tr = nc.tensor.transpose(b_s[2 * n + j // 4][:, (j % 4) * P:(j % 4) * P + P], src, ident[:, :])
                        if j % 4 == 3:
                            tr.then_inc(S[done], 1)

            def transpose_qs(t, p):
                pe.wait_ge(S["qs"], per(1, t))
                pe.wait_ge(S["rope"], per(3, t))
                for k in range(KB):
                    tr = nc.tensor.transpose(b_qk[:, k * P:k * P + P], qs[:, k * P:k * P + P], ident[:, :])
                tr.then_inc(S["qsT_ps"], 1)

            def scores(t, p):
                pe.wait_ge(S["q_ev"], per(4, t))
                pe.wait_ge(S["k_ev"], per(2, t))
                for b in range(4):
                    for j in (2 * b, 2 * b + 1):
                        mm = nc.tensor.matmul(b_s[b][:, (j % 2) * 2 * P:(j % 2) * 2 * P + 2 * P], kT[:, j, :], qbd[:, j, :], start=True, stop=True)
                    mm.then_inc(S["sc_ps"], 1)

            def retain(t, p):
                wait(pe, S["oT"], per(1, t - 1))
                pe.wait_ge(S["qsT"], per(1, t))
                wait(pe, S["state"], per(1, t - 1))
                for g in range(4):
                    mm = nc.tensor.matmul(b_o[:, g * P:g * P + P], state[:, 4 * g:4 * g + 4, :], qsT[:, g // 2, :],
                                          start=(g == 0), stop=(g == 3), skip_group_check=True)
                mm.then_inc(S["inter"], 1)
                pe.wait_ge(S["v"], per(1, t))
                for h in range(H):
                    if h % 4 == 0:
                        pe.wait_ge(S["probs"], per(4, t) - 3 + h // 4)
                    r = STRIP * (h % 4)
                    mm = nc.tensor.matmul(b_o[r:r + STRIP, (h // 4) * P:(h // 4) * P + P], vpad[:, p, h, :], probs[:, h, :],
                                          start=False, stop=(h == H - 1), skip_group_check=True)
                mm.then_inc(S["o_ps"], 1)

            def state_update(t, p):
                pe.wait_ge(S["vs"], per(1, t))
                pe.wait_ge(S["sg"], upto(t + 1))
                for a in range(2):
                    mm = nc.tensor.matmul(b_vg[:, a * 8 * (DH + 1):(a + 1) * 8 * (DH + 1)],
                                          qk[:, p, H + 8 * a:H + 8 * a + 8, :], vs[:, p, 8 * a:8 * a + 8, :], start=True, stop=True)
                mm.then_inc(S["st_ps"], 1)

            def transpose_o(t, p):
                pe.wait_ge(S["oT"], per(1, t))
                pe.wait_ge(S["hT_lo"], upto(t + 2))
                wait(pe, S["x2_lo"], per(1, t - 2))
                for g in range(4):
                    tr = nc.tensor.transpose(b_hT[:, g * P:g * P + P], oT[:, g, :], ident[:, :])
                tr.then_inc(S["oTT_ps"], 1)

            def transpose_y(t, p):
                pe.wait_ge(S["y"], per(1, t))
                pe.wait_ge(S["st_new"], upto(t + 1))
                for k in range(KB):
                    tr = nc.tensor.transpose(b_vg[:, k * P:k * P + P], y[:, p, k * P:k * P + P], ident[:, :])
                tr.then_inc(S["yT_ps"], 1)

            def project_out(t, p):
                pe.wait_ge(S["yT_lo"], per(1, t))
                pe.wait_ge(S["qsT"], upto(t + 2))
                for k in range(KB):
                    mm = product3(b_qk[:, 0:E], [a[:, k, :] for a in yT], [w[:, k, :] for w in wo], k == 0, k == KB - 1)
                mm.then_inc(S["out_ps"], 1)

            def transpose_x2(t, p):
                pe.wait_ge(S["x2r"], per(1, t))
                pe.wait_ge(S["on"], upto(t + 1))
                wait(pe, S["x2_lo"], per(1, t - 1))
                for k in range(KB):
                    tr = nc.tensor.transpose(b_hT[:, k * P:k * P + P], x2r[:, p, k * P:k * P + P], ident[:, :])
                tr.then_inc(S["x2T_ps"], 1)

            def body(t, p, live):
                q = 1 - p
                if live(2): retain(t - 2, p)
                if live(2): state_update(t - 2, p)
                if live(1): transpose_qk(t - 1, q)
                if live(1): transpose_qs(t - 1, q)
                if live(0): transpose_h(t, p)
                if live(3): transpose_y(t - 3, q)
                if live(2): transpose_o(t - 2, p)
                if live(3): project_out(t - 3, q)
                if live(0): project(t, p)
                if live(1): scores(t - 1, q)
                if live(3): transpose_x2(t - 3, q)

            pipeline(nc.tensor, body)
        local.close()
        scopes.pop()


def mlp(nc, io, scopes, sb, sem, wait, alone, bank, ident, neghalf, eps, modb, h_all, x2T, wf1, wf2, h3T,
        rows, logits, order, chosen, before_tile, ebefore, dram, s_filled):
    with ExitStack() as local:
        scopes.append(local)
        b1, b2 = sb("b1", [P, FB]), sb("b2", [P, E])
        wr = sb("wr", [P, KB, NR])
        xt = sb("xt2", [P, 2, E])
        res = sb("res", [P, TPG, 3, E])
        RING = 4
        act1 = sb("act1", [P, 2, G])
        a1 = [sb(f"a1_{n}", [P, RING, G], F32R) for n in ("hi", "lo")]
        h3 = sb("h3", [P, TPG, E])
        mg = sb("mg", [P, 2, E])
        st6, mv, ve, rstd = sb("m_st6", [P, 2, 6]), sb("m_mv", [P, 2, 2]), sb("m_ve", [P, 2, 1]), sb("m_rstd", [P, 2, 1])
        xn, hm = sb("m_xn", [P, 2, E]), sb("m_hm", [P, E])
        hT32 = sb("hT32", [P, 2, KB, P])
        more, same = sb("more", [P, NX, NX]), sb("same", [P, NX, NX])
        place = sb("place", [P, 2, NX])
        fill, spare = sb("fill", [P, 4, ROW]), sb("spare", [P, 4], mybir.dt.int32)
        names = """zeros spare_in fill b2in wr_in x_in0 x_in1 res1 res2 res f_ps act a_hi a_lo fc2 mg x3
            st6 mv ve rstd xn hm h3 tr_ps h32 hi lo lg_ps lg more same tied place order chosen start before
            x3_out row_out0 row_out1 row_out2 row_out3 tab_in""".split()
        S = {n: sem("m_" + n) for n in names}
        block = local.enter_context(nc.Block())
        x_tiles = io["L0_attn_x"].rearrange("a (t p) e -> (a t) p e", p=P)
        hidden = [bank[n] for n in (0, 1, 2, 7)]
        outs = bank[3:5]
        b_tr, b_lg = bank[5], bank[6]
        SKEW = 2
        TAIL = FB - TPG

        def groups(eng, body):
            body(0, True)
            body(1, False)
            with eng.Fori(2, NG) as g:
                body(g, False)

        @block.sync
        def _(sp):
            sp.dma_start(b1[:, :], io["L0_attn_fc1_b"]).then_inc(S["b2in"], 16)
            sp.dma_start(b2[:, :], io["L0_attn_fc2_b"].partition_broadcast(P)).then_inc(S["b2in"], 16)
            sp.dma_start(wr[:, :, :], io["router_w"].rearrange("(k p) n -> p k n", p=P)).then_inc(S["wr_in"], 16)

            def load_x(t, p):
                wait(sp, S["res"], t - 1)
                sp.dma_start(xt[:, p, :], x_tiles[t, :, :]).then_inc(S[f"x_in{p}"], 16)

            def store(t, i):
                sp.wait_ge(S["x3"], per(1, t))
                sp.dma_start(x3_tiles[t, :, :], h_all[:, t, :]).then_inc(S["x3_out"], 16)
                sp.wait_ge(S["h3"], per(1, t))
                sp.dma_start(rows[:, t, 0:E], h3[:, i, :]).then_inc(S[f"row_out{i}"], 16)

            sp.dma_start(ebefore[:, :, :], io["t_before"]).then_inc(S["tab_in"], 16)
            sp.dma_start(spare[:, :], io["t_spare"]).then_inc(S["spare_in"], 16)
            x3_tiles = dram["x3_rows"].rearrange("(t p) e -> t p e", p=P)
            load_x(0, 0)
            load_x(1, 1)
            load_x(2, 0)
            load_x(3, 1)

            unused = dram["dispatched"].rearrange("(m r p) c -> m p r c", r=4, p=P)
            FILLS = ETILES // 4 // NG

            def fill_rows(g):
                for n in range(FILLS):
                    sp.dma_start(unused[g * FILLS + n, :, :, :], fill[:, :, :]).then_inc(s_filled, 16)

            sp.wait_ge(S["fill"], 1)
            def body(g, first):
                fill_rows(g)
                if not first:
                    for i in range(TPG):
                        store((g - 1) * TPG + i, i)
                        load_x(g * TPG + i, i % 2)

            groups(nc.sync, body)
            for i in range(TPG):
                store(NT - TPG + i, i)
            sp.wait_ge(s_filled, 16 * (ETILES // 4))
            sp.wait_ge(S["x3_out"], 16 * NT)
            for i in range(TPG):
                sp.wait_ge(S[f"row_out{i}"], 16 * NG)

        @block.gpsimd
        def _(pool):
            nc.gpsimd.memset(fill[:, :, :], 0.0).then_inc(S["zeros"], 1)
            pool.wait_ge(S["zeros"], 1)
            pool.wait_ge(S["spare_in"], 16)
            nc.gpsimd.tensor_copy(fill[:, :, E:E + 1].bitcast(mybir.dt.int32), spare[:, :].unsqueeze(2)).then_inc(S["fill"], 1)
            pool.wait_ge(S["b2in"], 32)

            def residual(g, i):
                t, p = g * TPG + i, i % 2
                wait(pool, S["x3"], per(1, t - TPG))
                nc.gpsimd.tensor_tensor(res[:, i, 0, :], h_all[:, t, :], b2[:, :], ALU.add).then_inc(S["res1"], 1)
                pool.wait_ge(S["res1"], per(1, t))
                nc.gpsimd.tensor_tensor(res[:, i, 1, :], res[:, i, 0, :], modb[:, 2, :], ALU.mult).then_inc(S["res2"], 1)
                pool.wait_ge(S["res2"], per(1, t))
                pool.wait_ge(S[f"x_in{p}"], (t - p) * 8 + 16)
                nc.gpsimd.tensor_tensor(res[:, i, 2, :], res[:, i, 1, :], xt[:, p, :], ALU.add).then_inc(S["res"], 1)

            def inverse_std(g, i):
                t, p = g * TPG + i, i % 2
                pool.wait_ge(S["ve"], per(1, t))
                nc.gpsimd.tensor_tensor(rstd[:, p, :], ve[:, p, :], neghalf[:, 0:1], ALU.pow).then_inc(S["rstd"], 1)

            def modulate(g, i):
                t, p = g * TPG + i, i % 2
                pool.wait_ge(S["xn"], per(1, t))
                nc.gpsimd.tensor_tensor(hm[:, :], xn[:, p, :], modb[:, 4, :], ALU.mult).then_inc(S["hm"], 1)
                pool.wait_ge(S["hm"], per(1, t))
                wait(pool, S["tr_ps"], per(1, t - TPG))
                wait(pool, S[f"row_out{i}"], g * 16)
                nc.gpsimd.tensor_tensor(h3[:, i, :], hm[:, :], modb[:, 3, :], ALU.add).then_inc(S["h3"], 1)

            def body(g, first):
                if not first:
                    for i in range(TPG):
                        inverse_std(g - 1, i)
                        modulate(g - 1, i)
                for i in range(TPG):
                    residual(g, i)

            groups(nc.gpsimd, body)
            for i in range(TPG):
                inverse_std(NG - 1, i)
                modulate(NG - 1, i)

        @block.scalar
        def _(act):
            act.wait_ge(S["b2in"], 32)

            def gelu(g, b):
                n = g * FB + b
                act.wait_ge(S["f_ps"], n + 1)
                wait(act, S["a_lo"], n - 1)
                nc.scalar.activation(act1[:, b % 2, :], hidden[b % RING][:, :], ACT.Gelu_apprx_tanh, bias=b1[:, b:b + 1]).then_inc(S["act"], 1)
                act.wait_ge(S["act"], n + 1)
                wait(act, S["fc2"], n - 3)
                nc.scalar.copy(a1[0][:, b % RING, :], act1[:, b % 2, :]).then_inc(S["a_hi"], 1)

            def evacuate(g, i):
                t, p = g * TPG + i, i % 2
                act.wait_ge(S["tr_ps"], per(1, t))
                wait(act, S["lo"], per(1, t - 2))
                wait(act, S["lg_ps"], per(1, t - 2))
                nc.scalar.copy(hT32[:, p, :, :], b_tr[:, 0:E]).then_inc(S["h32"], 1)
                act.wait_ge(S["h32"], per(1, t))
                nc.scalar.copy(h3T[0][:, :, bass.ds(t * P, P)], hT32[:, p, :, :]).then_inc(S["hi"], 1)

            def body(g, first):
                for b in range(FB):
                    gelu(g, b)
                    if not first and b >= TAIL:
                        evacuate(g - 1, b - TAIL)

            groups(nc.scalar, body)
            for i in range(TPG):
                evacuate(NG - 1, i)

        @block.vector
        def _(dve):
            nc.vector.memset(before_tile[:, 0, :], 0.0).then_inc(S["start"], 1)
            dve.wait_ge(S["start"], 1)
            dve.wait_ge(S["tab_in"], 16)

            def split(g, b):
                n = g * FB + b
                dve.wait_ge(S["a_hi"], n + 1)
                nc.vector.tensor_tensor(a1[1][:, b % RING, :], act1[:, b % 2, :], a1[0][:, b % RING, :].bitcast(F32), ALU.subtract).then_inc(S["a_lo"], 1)

            def gate(g, i):
                t, p = g * TPG + i, i % 2
                dve.wait_ge(S["fc2"], per(FB, g))
                nc.vector.tensor_tensor(mg[:, p, :], outs[i // 2][:, (i % 2) * E:(i % 2) * E + E], modb[:, 2, :], ALU.mult).then_inc(S["mg"], 1)
                dve.wait_ge(S["mg"], per(1, t))
                dve.wait_ge(S["res"], per(1, t))
                nc.vector.tensor_tensor(h_all[:, t, :], mg[:, p, :], res[:, i, 2, :], ALU.add).then_inc(S["x3"], 1)

            def stats(g, i):
                t, p = g * TPG + i, i % 2
                dve.wait_ge(S["x3"], per(1, t))
                alone(dve)
                nc.vector.bn_stats(st6[:, p, :], h_all[:, t, :]).then_inc(S["st6"], 1)
                dve.wait_ge(S["st6"], per(1, t))
                alone(dve)
                nc.vector.bn_aggr(mv[:, p, :], st6[:, p, :]).then_inc(S["mv"], 1)
                dve.wait_ge(S["mv"], per(1, t))
                nc.vector.tensor_scalar(ve[:, p, :], mv[:, p, 1:2], EPS, None, ALU.add).then_inc(S["ve"], 1)

            def normalise(g, i):
                t, p = g * TPG + i, i % 2
                dve.wait_ge(S["rstd"], per(1, t))
                wait(dve, S["hm"], per(1, t - 2))
                nc.vector.tensor_scalar(xn[:, p, :], h_all[:, t, :], mv[:, p, 0:1], rstd[:, p, :], ALU.subtract, ALU.mult).then_inc(S["xn"], 1)

            def low_part(g, i):
                t, p = g * TPG + i, i % 2
                dve.wait_ge(S["hi"], per(1, t))
                cols = bass.ds(t * P, P)
                nc.vector.tensor_tensor(h3T[1][:, :, cols], hT32[:, p, :, :], h3T[0][:, :, cols].bitcast(F32), ALU.subtract).then_inc(S["lo"], 1)
                dve.wait_ge(S["lg_ps"], per(1, t))
                nc.vector.tensor_copy(logits[:, t, :], b_lg[:, 0:NR]).then_inc(S["lg"], 1)
                dve.wait_ge(S["lg"], per(1, t))
                mine = logits[:, t, 0:NX].unsqueeze(2).broadcast_to([P, NX, NX])
                others = logits[:, t, 0:NX].unsqueeze(1).broadcast_to([P, NX, NX])
                nc.vector.tensor_tensor(more[:, :, :], others, mine, ALU.is_gt).then_inc(S["more"], 1)
                nc.vector.tensor_tensor(same[:, :, :], others, mine, ALU.is_equal).then_inc(S["same"], 1)
                dve.wait_ge(S["same"], per(1, t))
                nc.vector.tensor_tensor(same[:, :, :], same[:, :, :], ebefore[:, :, :], ALU.mult).then_inc(S["tied"], 1)
                dve.wait_ge(S["tied"], per(1, t))
                dve.wait_ge(S["more"], per(1, t))
                nc.vector.tensor_reduce(place[:, 0, :], more[:, :, :], AX.X, ALU.add).then_inc(S["place"], 1)
                nc.vector.tensor_reduce(place[:, 1, :], same[:, :, :], AX.X, ALU.add).then_inc(S["place"], 1)
                dve.wait_ge(S["place"], per(2, t))
                nc.vector.tensor_tensor(order[:, t, :], place[:, 0, :], place[:, 1, :], ALU.add).then_inc(S["order"], 1)
                dve.wait_ge(S["order"], per(1, t))
                nc.vector.tensor_scalar(chosen[:, t, :], order[:, t, :], TOPK - 0.5, None, ALU.is_lt).then_inc(S["chosen"], 1)
                dve.wait_ge(S["chosen"], per(1, t))
                wait(dve, S["before"], per(1, t - 1))
                nc.vector.tensor_tensor(before_tile[:, t + 1, :], before_tile[:, t, :], chosen[:, t, :], ALU.add).then_inc(S["before"], 1)

            def finish(g, i):
                stats(g, i)
                normalise(g, i)

            def body(g, first):
                for b in range(FB):
                    if not first and b == SKEW:
                        for i in range(TPG):
                            gate(g - 1, i)
                    split(g, b)
                    if not first and b >= SKEW and b < SKEW + TPG:
                        finish(g - 1, b - SKEW)
                    if not first and b >= TAIL:
                        low_part(g - 1, b - TAIL)

            groups(nc.vector, body)
            for i in range(TPG):
                gate(NG - 1, i)
            for i in range(TPG):
                finish(NG - 1, i)
                if i:
                    low_part(NG - 1, i - 1)
            low_part(NG - 1, TPG - 1)

        @block.tensor
        def _(pe):
            pe.wait_ge(S["wr_in"], 16)

            def first_product(g, b):
                n = g * FB + b
                wait(pe, S["act"], n - 3)
                cols = bass.ds(g * G, G)
                for k in range(KB):
                    m = slice(b * P, b * P + P)
                    for i, (wn, xn_) in enumerate(((0, 0), (0, 1), (1, 0))):
                        mm = nc.tensor.matmul(hidden[b % RING][:, :], wf1[wn][:, k, m], x2T[xn_][:, k, cols],
                                              start=(k == 0 and i == 0), stop=(k == KB - 1 and i == 2))
                mm.then_inc(S["f_ps"], 1)

            def second_product(g, b):
                n = g * FB + b
                pe.wait_ge(S["a_lo"], n + 1)
                if b == 0:
                    wait(pe, S["mg"], g * TPG)
                for i in range(TPG):
                    dst = outs[i // 2][:, (i % 2) * E:(i % 2) * E + E]
                    cols = slice(i * P, i * P + P)
                    for j, (an, wn) in enumerate(((0, 0), (0, 1), (1, 0))):
                        mm = nc.tensor.matmul(dst, a1[an][:, b % RING, cols], wf2[wn][:, b, :],
                                              start=(b == 0 and j == 0 and i % 2 == 0), stop=(b == FB - 1 and j == 2), skip_group_check=True)
                mm.then_inc(S["fc2"], 1)

            def transpose_h3(g, i):
                t = g * TPG + i
                pe.wait_ge(S["h3"], per(1, t))
                wait(pe, S["h32"], per(1, t - 1))
                for k in range(KB):
                    tr = nc.tensor.transpose(b_tr[:, k * P:k * P + P], h3[:, i, k * P:k * P + P], ident[:, :])
                tr.then_inc(S["tr_ps"], 1)

            def route(g, i):
                t, p = g * TPG + i, i % 2
                pe.wait_ge(S["h32"], per(1, t))
                wait(pe, S["lg"], per(1, t - 1))
                for k in range(KB):
                    mm = nc.tensor.matmul(b_lg[:, 0:NR], hT32[:, p, k, :], wr[:, k, :], start=(k == 0), stop=(k == KB - 1))
                mm.then_inc(S["lg_ps"], 1)

            def body(g, first):
                for b in range(FB):
                    first_product(g, b)
                    if b >= SKEW:
                        second_product(g, b - SKEW)
                    elif not first:
                        second_product(g - 1, FB - SKEW + b)
                    if not first and b >= TAIL:
                        transpose_h3(g - 1, b - TAIL)
                        route(g - 1, b - TAIL)

            groups(nc.tensor, body)
            for b in range(FB - SKEW, FB):
                second_product(NG - 1, b)
            for i in range(TPG):
                transpose_h3(NG - 1, i)
                route(NG - 1, i)
        scopes.pop()


def shared_and_dispatch(nc, io, scopes, sb, sem, wait, alone, bank, gb, weights, tile_expert, h3T, rows, logits,
                        order, chosen, before_tile, ebefore, wgu, dram, s_filled):
    INT = mybir.dt.int32
    NB = len(SBLOCKS)
    RING, SKEW = 3, 2
    with ExitStack() as local:
        scopes.append(local)
        wsg = [sb(f"wsg_{n}", [P, KB, 2 * SI], F32R) for n in ("hi", "lo")]
        wsd = [sb(f"wsd_{n}", [P, NB, E], F32R) for n in ("hi", "lo")]
        stage = sb("stage", [P, 2, KB, GU])
        hid = sb("hid", [P, 2, G])
        a1 = [sb(f"s_a1_{n}", [P, RING, G], F32R) for n in ("hi", "lo")]
        xt, x4 = sb("s_xt", [P, 2, E]), sb("s_x4", [P, 2, E])
        sgate = sb("sgate", [P, NT])
        later, ones = sb("later", [P, P]), sb("ones", [P, P])
        steps, tile_no = sb("steps", [P, NX]), sb("tile_no", [P, ETILES])
        dest = sb("dest", [P, TOPK, NT], INT)
        best, ez = sb("best", [P, NT]), sb("ez", [P, NT, NX])
        pick, slot = sb("pick", [P, NT, NX]), sb("slot", [P, TOPK, NT], INT)
        slot_e, slot32, cmp_ = ebefore, weights, pick
        used, base, end = sb("used", [P, NX]), sb("base", [P, NX]), sb("end", [P, NX])
        base_row = sb("base_row", [P, NX])
        ecount = sb("ecount", [1, ETILES])
        wsum, wrec = sb("wsum", [P, NT]), sb("wrec", [P, NT])
        names = """tab_in ones st_in0 st_in1 w_hi w_lo z_ps g_ps u_ps act hid a_hi a_lo fc2 x_in0 x_in1 sh x4 x4_out0 x4_out1
            chain exps rank_ps count_ps slots pad col tiles""".split()
        S = {n: sem("r_" + n) for n in names}
        s_sent = [sem(f"r_sent{t}") for t in range(NT)]
        block = local.enter_context(nc.Block())
        gate_b, up_b, outs, b_rank, b_count = bank[0:2], bank[2:4], bank[4:6], bank[6], bank[7]
        NCHUNKS = 7
        x3_tiles = dram["x3_rows"].rearrange("(t p) e -> t p e", p=P)
        x4_tiles = dram["x4_rows"].rearrange("(t p) e -> t p e", p=P)

        def groups(eng, body):
            body(0, True)
            body(1, False)
            with eng.Fori(2, NG) as g:
                body(g, False)

        def chunk(n):
            if n < 4:
                cols = slice(n * GU, n * GU + GU)
                return P, io["shared_gu"].rearrange("(k p) n -> p k n", p=P)[:, :, cols], stage[:, n % 2, :, :], [w[:, :, cols] for w in wsg]
            b = 2 * (n - 4)
            start, m = SBLOCKS[b]
            return (m, io["shared_d"][start:start + 2 * m, :].rearrange("(b p) n -> p b n", p=m),
                    stage[0:m, n % 2, :, 0:E], [w[0:m, b:b + 2, :] for w in wsd])

        def arrived(n, p):
            return ((n - p) * 8 + 16)

        def expert_chunk(e, p):
            return stage[:, p, :, :], [w[:, :, e, :] for w in wgu]

        @block.sync
        def _(sp):
            for dst, name in ((later, "t_later"), (steps, "t_steps"), (tile_no, "t_tiles"), (dest, "t_dest")):
                sp.dma_start(dst[tuple([slice(None)] * len(dst.shape))], io[name]).then_inc(S["tab_in"], 16)
            for n in range(NCHUNKS):
                m, src, st, _ = chunk(n)
                wait(sp, S["w_lo"], n - 1)
                sp.dma_start(st, src).then_inc(S[f"st_in{n % 2}"], 16)
            experts_gu = io["expert_gu"].rearrange("(k p) e n -> e p k n", p=P)

            def load_expert(e, i):
                wait(sp, S["w_lo"], NCHUNKS + e - 1)
                p = (NCHUNKS + i) % 2
                sp.dma_start(stage[:, p, :, :], experts_gu[e, :, :, :]).then_inc(S[f"st_in{p}"], 16)

            def load_x3(t, p):
                wait(sp, S["x4"], per(1, t - 2))
                sp.dma_start(xt[:, p, :], x3_tiles[t, :, :]).then_inc(S[f"x_in{p}"], 16)

            def store_x4(t, p):
                sp.wait_ge(S["x4"], per(1, t))
                sp.dma_start(x4_tiles[t, :, :], x4[:, p, :]).then_inc(S[f"x4_out{p}"], 16)

            def body(g, first):
                for i in range(TPG):
                    if not first and i == 2:
                        for n in range(TPG):
                            store_x4((g - 1) * TPG + n, n % 2)
                            load_x3((g - 1) * TPG + n + 2, n % 2)
                    load_expert(g * TPG + i, i)
                if first:
                    load_x3(0, 0)
                    load_x3(1, 1)

            groups(nc.sync, body)
            for i in range(TPG):
                store_x4(NT - TPG + i, i % 2)
                if i < 2:
                    load_x3(NT - 2 + i, i)
            for p in range(2):
                sp.wait_ge(S[f"x4_out{p}"], 16 * NT // 2)

        @block.gpsimd
        def _(pool):
            nc.gpsimd.memset(rows[:, :, E:ROW], 0.0).then_inc(S["pad"], 1)
            nc.gpsimd.memset(ones[:, :], 1.0).then_inc(S["ones"], 1)
            pool.wait_ge(S["pad"], 1)
            pool.wait_ge(s_filled, 16 * (ETILES // 4))
            for k in range(TOPK):
                for t in range(NT):
                    wait(pool, s_sent[t], 16 * k)
                if k == 0:
                    pool.wait_ge(S["tab_in"], 64)
                nc.gpsimd.tensor_copy(rows[:, :, E:E + 1].bitcast(INT), dest[:, k, :].unsqueeze(2)).then_inc(S["col"], 1)
                pool.wait_ge(S["col"], k + 1)
                pool.wait_ge(S["slots"], TOPK)
                for t in range(NT):
                    pool.indirect_dma_start(out=dram["dispatched"], out_offset=bass.IndirectOffsetOnAxis(ap=slot[:, k, t:t + 1], axis=0),
                                            in_=rows[:, t, :], in_offset=None).then_inc(s_sent[t], 16)
            for t in range(NT):
                pool.wait_ge(s_sent[t], 16 * TOPK)

        @block.scalar
        def _(act):
            def split(st, dst, n, p):
                act.wait_ge(S[f"st_in{p}"], arrived(n, p))
                nc.scalar.copy(dst[0], st).then_inc(S["w_hi"], 1)

            for n in range(NCHUNKS):
                _, _, st, dst = chunk(n)
                split(st, dst, n, n % 2)
            act.wait_ge(S["chain"], 2)
            nc.scalar.activation(ez[:, :, :], ez[:, :, :], ACT.Exp).then_inc(S["exps"], 1)
            nc.scalar.activation(sgate[:, :], logits[:, :, NX], ACT.Exp, scale=-1.0).then_inc(S["exps"], 1)

            def hidden(g, b):
                n, m = g * NB + b, SBLOCKS[b][1]
                act.wait_ge(S["g_ps"], n + 1)
                wait(act, S["a_lo"], n - 1)
                nc.scalar.activation(hid[0:m, b % 2, :], gate_b[b % 2][0:m, :], ACT.Silu).then_inc(S["act"], 1)
                act.wait_ge(S["hid"], n + 1)
                wait(act, S["fc2"], n - 2)
                nc.scalar.copy(a1[0][0:m, b % RING, :], hid[0:m, b % 2, :]).then_inc(S["a_hi"], 1)

            def body(g, first):
                for b in range(NB):
                    hidden(g, b)
                    if 1 <= b <= TPG:
                        p = (NCHUNKS + b - 1) % 2
                        st, dst = expert_chunk(g * TPG + b - 1, p)
                        split(st, dst, NCHUNKS + g * TPG + b - 1, p)

            groups(nc.scalar, body)

        @block.vector
        def _(dve):
            def low(st, dst, n):
                dve.wait_ge(S["w_hi"], n + 1)
                nc.vector.tensor_tensor(dst[1], st, dst[0].bitcast(F32), ALU.subtract).then_inc(S["w_lo"], 1)

            done = [0]

            def chain(ins):
                done[0] += 1
                ins.then_inc(S["chain"], 1)
                dve.wait_ge(S["chain"], done[0])

            chain(nc.vector.tensor_reduce(best[:, :], logits[:, :, 0:NX], AX.X, ALU.max))
            chain(nc.vector.tensor_tensor(ez[:, :, :], logits[:, :, 0:NX], best[:, :].unsqueeze(2).broadcast_to([P, NT, NX]), ALU.subtract))
            dve.wait_ge(S["tab_in"], 64)
            dve.wait_ge(S["count_ps"], 1)
            chain(nc.vector.tensor_copy(used[:, :], b_count[:, 0:NX]))
            chain(nc.vector.tensor_tensor(cmp_[:, :, :], used[:, :].unsqueeze(2).broadcast_to([P, NX, NX]),
                                          steps[:, :].unsqueeze(1).broadcast_to([P, NX, NX]), ALU.is_gt))
            chain(nc.vector.tensor_reduce(used[:, :], cmp_[:, :, :], AX.X, ALU.add))
            chain(nc.vector.tensor_tensor(cmp_[:, :, :], used[:, :].unsqueeze(1).broadcast_to([P, NX, NX]), ebefore[:, :, :], ALU.mult))
            chain(nc.vector.tensor_reduce(base[:, :], cmp_[:, :, :], AX.X, ALU.add))
            chain(nc.vector.tensor_scalar(base_row[:, :], base[:, :], float(P), None, ALU.mult))
            dve.wait_ge(S["rank_ps"], 1)
            chain(nc.vector.tensor_tensor(slot_e[:, :, :], b_rank[:, 0:NT * NX].rearrange("p (t e) -> p t e", e=NX),
                                          base_row[:, :].unsqueeze(1).broadcast_to([P, NT, NX]), ALU.add))

            def flat(x):
                return x[:, :, :].rearrange("p t e -> p (t e)")

            for k in range(TOPK):
                chain(nc.vector.scalar_tensor_tensor(flat(pick), flat(order), float(k), flat(slot_e), ALU.is_equal, ALU.mult))
                chain(nc.vector.tensor_reduce(slot32[:, k, :], pick[:, :, :], AX.X, ALU.add))
                nc.vector.tensor_copy(slot[:, k, :], slot32[:, k, :]).then_inc(S["slots"], 1)
            for n in range(NCHUNKS):
                _, _, st, dst = chunk(n)
                low(st, dst, n)
            chain(nc.vector.tensor_tensor(end[:, :], base[:, :], used[:, :], ALU.add))
            chain(nc.vector.tensor_scalar(ecount[:, :], tile_no[0:1, :], end[0:1, 0:1], None, ALU.is_ge))
            for e in range(1, NX):
                chain(nc.vector.scalar_tensor_tensor(ecount[:, :], tile_no[0:1, :], end[0:1, e:e + 1], ecount[:, :], ALU.is_ge, ALU.add))
            nc.vector.tensor_scalar(tile_expert[0:1, :], ecount[:, :], NX - 1.0, None, ALU.min).then_inc(S["tiles"], 1)
            dve.wait_ge(S["exps"], 2)
            for k in range(TOPK):
                chain(nc.vector.scalar_tensor_tensor(flat(pick), flat(order), float(k), flat(ez), ALU.is_equal, ALU.mult))
                chain(nc.vector.tensor_reduce(weights[:, k, :], pick[:, :, :], AX.X, ALU.add))
            chain(nc.vector.tensor_reduce(wsum[:, :], weights[:, :, :].rearrange("p k t -> p t k"), AX.X, ALU.add))
            chain(nc.vector.reciprocal(wrec[:, :], wsum[:, :]))
            chain(nc.vector.tensor_tensor(weights[:, :, :], weights[:, :, :], wrec[:, :].unsqueeze(1).broadcast_to([P, TOPK, NT]), ALU.mult))
            chain(nc.vector.tensor_scalar(sgate[:, :], sgate[:, :], 1.0, None, ALU.add))
            chain(nc.vector.reciprocal(sgate[:, :], sgate[:, :]))

            def hidden(g, b):
                n, m = g * NB + b, SBLOCKS[b][1]
                dve.wait_ge(S["act"], n + 1)
                dve.wait_ge(S["u_ps"], n + 1)
                nc.vector.tensor_tensor(hid[0:m, b % 2, :], hid[0:m, b % 2, :], up_b[b % 2][0:m, :], ALU.mult).then_inc(S["hid"], 1)
                dve.wait_ge(S["a_hi"], n + 1)
                wait(dve, S["fc2"], n - 2)
                nc.vector.tensor_tensor(a1[1][0:m, b % RING, :], hid[0:m, b % 2, :], a1[0][0:m, b % RING, :].bitcast(F32), ALU.subtract).then_inc(S["a_lo"], 1)

            def add_shared(g, i):
                t, p = g * TPG + i, i % 2
                dve.wait_ge(S["fc2"], per(NB, g))
                wait(dve, S[f"x4_out{p}"], (t - p) * 8)
                nc.vector.scalar_tensor_tensor(x4[:, p, :], outs[i // 2][:, (i % 2) * E:(i % 2) * E + E], sgate[:, bass.ds(t, 1)],
                                               gb[:, :], ALU.mult, ALU.mult).then_inc(S["sh"], 1)
                dve.wait_ge(S["sh"], per(1, t))
                dve.wait_ge(S[f"x_in{p}"], (t - p) * 8 + 16)
                nc.vector.tensor_tensor(x4[:, p, :], x4[:, p, :], xt[:, p, :], ALU.add).then_inc(S["x4"], 1)

            def body(g, first):
                for b in range(NB):
                    if not first and b == SKEW:
                        for i in range(TPG):
                            add_shared(g - 1, i)
                    hidden(g, b)
                    if 1 <= b <= TPG:
                        st, dst = expert_chunk(g * TPG + b - 1, (NCHUNKS + b - 1) % 2)
                        low(st, dst, NCHUNKS + g * TPG + b - 1)

            groups(nc.vector, body)
            for i in range(TPG):
                add_shared(NG - 1, i)

        @block.tensor
        def _(pe):
            pe.wait_ge(S["ones"], 1)
            pe.wait_ge(S["tab_in"], 64)
            nc.tensor.matmul(b_count[:, 0:NX], ones[:, :], before_tile[:, NT, :], start=True, stop=True).then_inc(S["count_ps"], 1)
            nc.tensor.matmul(b_rank[:, 0:NT * NX], ones[:, :], before_tile[:, 0:NT, :], start=True, stop=False)
            nc.tensor.matmul(b_rank[:, 0:NT * NX], later[:, :], chosen[:, :, :], start=False, stop=True).then_inc(S["rank_ps"], 1)

            def first_product(g, b):
                n = g * NB + b
                start, m = SBLOCKS[b]
                cols = bass.ds(g * G, G)
                for part, dst, done, free in ((0, gate_b, "g_ps", "act"), (SI, up_b, "u_ps", "hid")):
                    wait(pe, S[free], n - 1)
                    for k in range(KB):
                        for i, (wn, xn_) in enumerate(((0, 0), (0, 1), (1, 0))):
                            mm = nc.tensor.matmul(dst[b % 2][0:m, :], wsg[wn][:, k, part + start:part + start + m], h3T[xn_][:, k, cols],
                                                  start=(k == 0 and i == 0), stop=(k == KB - 1 and i == 2))
                    mm.then_inc(S[done], 1)

            def second_product(g, b):
                n, m = g * NB + b, SBLOCKS[b][1]
                pe.wait_ge(S["a_lo"], n + 1)
                if b == 0:
                    wait(pe, S["sh"], g * TPG)
                for i in range(TPG):
                    dst = outs[i // 2][:, (i % 2) * E:(i % 2) * E + E]
                    for j, (an, wn) in enumerate(((0, 0), (0, 1), (1, 0))):
                        mm = nc.tensor.matmul(dst, a1[an][0:m, b % RING, i * P:i * P + P], wsd[wn][0:m, b, :],
                                              start=(b == 0 and j == 0 and i % 2 == 0), stop=(b == NB - 1 and j == 2), skip_group_check=True)
                mm.then_inc(S["fc2"], 1)

            pe.wait_ge(S["w_lo"], NCHUNKS)

            def body(g, first):
                for b in range(NB):
                    first_product(g, b)
                    if b >= SKEW:
                        second_product(g, b - SKEW)
                    elif not first:
                        second_product(g - 1, NB - SKEW + b)

            groups(nc.tensor, body)
            for b in range(NB - SKEW, NB):
                second_product(NG - 1, b)
        scopes.pop()


def experts(nc, io, scopes, sb, sem, wait, alone, bank, ident, gb, weights, tile_expert, wgu, dram, out):
    INT = mybir.dt.int32
    XR, YR = 8, 4
    with ExitStack() as local:
        scopes.append(local)
        wda = [sb(f"wda_{n}", [P, NX, E], F32R) for n in ("hi", "lo")]
        wdb = [sb(f"wdb_{n}", [IT, NX, E], F32R) for n in ("hi", "lo")]
        stage = sb("d_stage", [P, 2, 4, E])
        xe = sb("xe", [P, XR, ROW])
        xT = [sb(f"xT_{n}", [P, 2, KB, P], F32R) for n in ("hi", "lo")]
        sg = sb("e_sg", [P, 2, I])
        hx = sb("hx", [P, 2, 2 * P])
        hT = [sb(f"e_hT_{n}", [P, 4, 2 * P], F32R) for n in ("hi", "lo")]
        yb = sb("yb", [P, YR, E])
        names = "st_in0 st_in1 w_hi w_lo zero xT_ps x_hi x_lo gu_ps sg hx hT_ps h_hi h_lo y_ps y".split()
        S = {n: sem("e_" + n) for n in names}
        s_in = [sem(f"e_in{r}") for r in range(XR)]
        s_sent = [sem(f"e_sent{r}") for r in range(YR)]
        t_bank, gu_bank, hT_bank, y_bank = bank[0:2], bank[2:4], bank[4:6], bank[6:8]
        dispatched = dram["dispatched"].rearrange("(j p) c -> j p c", p=P)
        NCH = 8
        LAG = 4

        def chunk(n):
            m, w, src = (P, wda, io["expert_d"][0:P]) if n < 4 else (IT, wdb, io["expert_d"][P:I])
            e = 4 * (n % 4)
            return src[:, e:e + 4, :], stage[0:m, n % 2, :, :], [x[:, e:e + 4, :] for x in w]

        def sent(j, r):
            return (j - r % YR) * (16 // YR) + 16

        def pipeline(eng, body):
            for t in range(XR):
                body(t, t % XR, lambda lag, t=t: t - lag >= 0)
            with eng.Fori(1, ETILES // XR) as j:
                for r in range(XR):
                    body(j * XR + r, r, lambda lag: True)
            for t in range(ETILES, ETILES + LAG):
                body(t, t % XR, lambda lag, t=t: t - lag < ETILES)

        with nc.Block() as block:
            @block.sync
            def _(sp):
                for n in range(NCH):
                    src, st, _ = chunk(n)
                    wait(sp, S["w_lo"], n - 1)
                    sp.dma_start(st, src).then_inc(S[f"st_in{n % 2}"], 16)

                def body(j, r, live):
                    if live(0):
                        wait(sp, s_sent[r % YR], sent(j - XR, r))
                        sp.dma_start(xe[:, r, :], dispatched[j, :, :]).then_inc(s_in[r], 16)

                pipeline(nc.sync, body)

            @block.gpsimd
            def _(pool):
                nc.gpsimd.memset(hx[:, :, :], 0.0).then_inc(S["zero"], 1)

                def send(j, r):
                    pool.wait_ge(S["y"], per(1, j))
                    alone(pool)
                    pool.indirect_dma_start(out=dram["results"], out_offset=bass.IndirectOffsetOnAxis(ap=xe[:, r, E:E + 1].bitcast(INT), axis=0),
                                            in_=yb[:, r % YR, :], in_offset=None).then_inc(s_sent[r % YR], 16)

                def body(j, r, live):
                    if live(LAG): send(j - LAG, (r - LAG) % XR)

                pipeline(nc.gpsimd, body)
                for r in range(YR):
                    pool.wait_ge(s_sent[r], 16 * ETILES // YR)

            @block.scalar
            def _(act):
                for n in range(NCH):
                    _, st, dst = chunk(n)
                    act.wait_ge(S[f"st_in{n % 2}"], (n // 2 + 1) * 16)
                    nc.scalar.copy(dst[0], st).then_inc(S["w_hi"], 1)

                def high_x(j, p):
                    act.wait_ge(S["xT_ps"], per(1, j))
                    wait(act, S["gu_ps"], per(1, j - 2))
                    nc.scalar.copy(xT[0][:, p, :, :], t_bank[p][:, 0:E]).then_inc(S["x_hi"], 1)

                def silu(j, p):
                    act.wait_ge(S["gu_ps"], per(1, j))
                    wait(act, S["hx"], per(1, j - 2))
                    nc.scalar.activation(sg[:, p, :], gu_bank[p][:, 0:I], ACT.Silu).then_inc(S["sg"], 1)

                def high_h(j, p, q):
                    act.wait_ge(S["hT_ps"], per(1, j))
                    wait(act, S["y_ps"], per(1, j - 4))
                    nc.scalar.copy(hT[0][:, q, :], hT_bank[p][:, 0:2 * P]).then_inc(S["h_hi"], 1)

                def body(j, r, live):
                    if live(0): high_x(j, r % 2)
                    if live(1): silu(j - 1, (r - 1) % 2)
                    if live(2): high_h(j - 2, r % 2, (r - 2) % 4)

                pipeline(nc.scalar, body)

            @block.vector
            def _(dve):
                for n in range(NCH):
                    _, st, dst = chunk(n)
                    dve.wait_ge(S["w_hi"], n + 1)
                    nc.vector.tensor_tensor(dst[1], st, dst[0].bitcast(F32), ALU.subtract).then_inc(S["w_lo"], 1)
                dve.wait_ge(S["zero"], 1)

                def low_x(j, p):
                    dve.wait_ge(S["x_hi"], per(1, j))
                    nc.vector.tensor_tensor(xT[1][:, p, :, :].rearrange("p k s -> p (k s)"), t_bank[p][:, 0:E],
                                            xT[0][:, p, :, :].bitcast(F32).rearrange("p k s -> p (k s)"), ALU.subtract).then_inc(S["x_lo"], 1)

                def product(j, p):
                    dve.wait_ge(S["sg"], per(1, j))
                    wait(dve, S["hT_ps"], per(1, j - 2))
                    nc.vector.tensor_tensor(hx[:, p, 0:I], sg[:, p, :], gu_bank[p][:, I:GU], ALU.mult).then_inc(S["hx"], 1)

                def low_h(j, p, q):
                    dve.wait_ge(S["h_hi"], per(1, j))
                    nc.vector.tensor_tensor(hT[1][:, q, :], hT_bank[p][:, 0:2 * P], hT[0][:, q, :].bitcast(F32), ALU.subtract).then_inc(S["h_lo"], 1)

                def result(j, r):
                    dve.wait_ge(S["y_ps"], per(1, j))
                    wait(dve, s_sent[r % YR], sent(j - YR, r))
                    nc.vector.tensor_tensor(yb[:, r % YR, :], y_bank[r % 2][:, 0:E], gb[:, :], ALU.mult).then_inc(S["y"], 1)

                def body(j, r, live):
                    if live(0): low_x(j, r % 2)
                    if live(1): product(j - 1, (r - 1) % 2)
                    if live(2): low_h(j - 2, r % 2, (r - 2) % 4)
                    if live(LAG): result(j - LAG, (r - LAG) % XR)

                pipeline(nc.vector, body)

            @block.tensor
            def _(pe):
                def transpose_x(j, r):
                    pe.wait_ge(s_in[r], (j - r) * (16 // XR) + 16)
                    wait(pe, S["x_lo"], per(1, j - 2))
                    for k in range(KB):
                        tr = nc.tensor.transpose(t_bank[r % 2][:, k * P:k * P + P], xe[:, r, k * P:k * P + P], ident[:, :])
                    tr.then_inc(S["xT_ps"], 1)

                expert_reg = [nc.tensor.alloc_register(f"expert{r}") for r in range(XR)]

                def load_expert(j, r):
                    nc.tensor.reg_load(expert_reg[r], tile_expert[0:1, bass.ds(j, 1)])

                def expert(r):
                    return nc.s_assert_within(nc.tensor.snap(expert_reg[r]), 0, NX - 1, skip_runtime_bounds_check_because="tile_expert is computed as at most NX - 1")

                def gate_up(j, p, e):
                    pe.wait_ge(S["x_lo"], per(1, j))
                    wait(pe, S["hx"], per(1, j - 2))
                    for k in range(KB):
                        for i, (xn_, wn) in enumerate(((0, 0), (0, 1), (1, 0))):
                            mm = nc.tensor.matmul(gu_bank[p][:, 0:GU], xT[xn_][:, p, k, :], wgu[wn][:, k, e, :],
                                                  start=(k == 0 and i == 0), stop=(k == KB - 1 and i == 2))
                    mm.then_inc(S["gu_ps"], 1)

                def transpose_h(j, p):
                    pe.wait_ge(S["hx"], per(1, j))
                    wait(pe, S["h_lo"], per(1, j - 2))
                    for k in range(2):
                        tr = nc.tensor.transpose(hT_bank[p][:, k * P:k * P + P], hx[:, p, k * P:k * P + P], ident[:, :])
                    tr.then_inc(S["hT_ps"], 1)

                def down(j, r, e):
                    p = r % 2
                    pe.wait_ge(S["h_lo"], per(1, j))
                    wait(pe, S["y"], per(1, j - 2))
                    for k, (m, w) in enumerate(((P, wda), (IT, wdb))):
                        for i, (hn, wn) in enumerate(((0, 0), (0, 1), (1, 0))):
                            mm = nc.tensor.matmul(y_bank[p][:, 0:E], hT[hn][0:m, r % 4, k * P:k * P + P], w[wn][0:m, e, :],
                                                  start=(k == 0 and i == 0), stop=(k == 1 and i == 2))
                    mm.then_inc(S["y_ps"], 1)

                pe.wait_ge(S["w_lo"], NCH)

                def body(j, r, live):
                    if live(0): load_expert(j, r)
                    if live(0): transpose_x(j, r)
                    if live(1): gate_up(j - 1, (r - 1) % 2, expert((r - 1) % XR))
                    if live(LAG): down(j - LAG, (r - LAG) % XR, expert((r - LAG) % XR))
                    if live(2): transpose_h(j - 2, r % 2)

                pipeline(nc.tensor, body)

        ys, x4, acc = sb("ys", [P, 2, TOPK, E]), sb("c_x4", [P, 2, E]), sb("acc", [P, 2, E])
        s_ys = [sem(f"c_ys{p}") for p in range(2)]
        s_sum, s_part = sem("c_sum"), sem("c_part")
        s_out = [sem(f"c_out{p}") for p in range(2)]
        res = dram["results"][0:N * TOPK, :].rearrange("(k t p) e -> t p k e", k=TOPK, p=P)
        x4_tiles = dram["x4_rows"].rearrange("(t p) e -> t p e", p=P)
        out_tiles = out.rearrange("a (t p) e -> (a t) p e", p=P)
        with nc.Block() as block:
            def pairs(eng, body):
                body(0, 0)
                body(1, 1)
                with eng.Fori(1, NT // 2) as j:
                    for p in range(2):
                        body(j * 2 + p, p)

            @block.sync
            def _(sp):
                def load(t, p):
                    wait(sp, s_sum, per(1, t - 2))
                    sp.dma_start(ys[:, p, :, :], res[t, :, :, :]).then_inc(s_ys[p], 16)
                    sp.dma_start(x4[:, p, :], x4_tiles[t, :, :]).then_inc(s_ys[p], 16)

                pairs(nc.sync, load)

            @block.scalar
            def _(act):
                def store(t, p):
                    act.wait_ge(s_sum, per(1, t))
                    act.dma_start(out_tiles[t, :, :], acc[:, p, :]).then_inc(s_out[p], 16)

                pairs(nc.scalar, store)
                for p in range(2):
                    act.wait_ge(s_out[p], 16 * NT // 2)

            @block.vector
            def _(dve):
                def combine(t, p):
                    dve.wait_ge(s_ys[p], (t - p) * 16 + 32)
                    wait(dve, s_out[p], (t - p) * 8)
                    for k in range(TOPK):
                        ins = nc.vector.scalar_tensor_tensor(acc[:, p, :], ys[:, p, k, :], weights[:, k, bass.ds(t, 1)],
                                                             x4[:, p, :] if k == 0 else acc[:, p, :], ALU.mult, ALU.add)
                        if k < TOPK - 1:
                            ins.then_inc(s_part, 1)
                            dve.wait_ge(s_part, t * (TOPK - 1) + k + 1)
                    ins.then_inc(s_sum, 1)

                pairs(nc.vector, combine)
        scopes.pop()


_INS = ['L0_attn_x', 'L0_attn_q_w', 'L0_attn_k_w', 'L0_attn_v_w', 'L0_attn_g_w', 'L0_attn_out_w', 'L0_attn_fc1_w',
        'L0_attn_fc1_b', 'L0_attn_fc2_w', 'L0_attn_fc2_b', 'L0_attn_retn_norm_w', 'L0_attn_final_norm_w', 'L0_c', 'L0_wmod']


def kernel(**inputs):
    import concourse.bacc as _bacc
    from concourse.bass_utils import run_bass_kernel_spmd as _run

    nc = _bacc.Bacc("TRN2", target_bir_lowering=False, num_devices=1)
    arrays = {name: np.ascontiguousarray(inputs[name]) for name in _INS}
    for name in ("L0_c", "L0_attn_retn_norm_w", "L0_attn_final_norm_w", "L0_attn_fc1_b"):
        arrays[name] = np.ascontiguousarray(arrays[name].reshape(-1, P).T)
    arrays["router_w"] = np.ascontiguousarray(np.concatenate([inputs["L0_ffn_gate_w"], inputs["L0_ffn_shared_gate_vec"]]).T)
    flat = lambda a: np.ascontiguousarray(a)
    arrays["expert_gu"] = flat(np.transpose(inputs["L0_ffn_expert_gate_up"], (2, 0, 1)))
    arrays["expert_d"] = flat(np.transpose(inputs["L0_ffn_expert_down"], (2, 0, 1)))
    arrays["shared_gu"] = flat(np.transpose(inputs["L0_ffn_shared_gate_up"]))
    arrays["shared_d"] = flat(np.transpose(inputs["L0_ffn_shared_down"]))
    arrays.update(shape_tables())
    io = {n: nc.dram_tensor(n, a.shape, mybir.dt.from_np(a.dtype), kind="ExternalInput").ap() for n, a in arrays.items()}
    out = nc.dram_tensor("out", (1, N, E), F32, kind="ExternalOutput").ap()
    build(nc, io, out)
    r = _run(nc, [arrays], core_ids=[0])
    return r.results[0]["out"]
```

```python
from contextlib import ExitStack

import numpy as np
import concourse.bass as bass
from concourse import mybir

F32 = mybir.dt.float32
F32R = mybir.dt.float32r
ALU = mybir.AluOpType
ACT = mybir.ActivationFunctionType
AX = mybir.AxisListType

P = 128
N = 2048
E = 256
KB = E // P
NT = N // P
H = 16
DH = E // H
PAIRS = H // 2
STRIP = 32
F = 1024
FB = F // P
NX = 16
NR = NX + 1
TOPK = 4
I = 176
IT = I - P
GU = 2 * I
SI = 704
SBLOCKS = [(0, 128), (128, 128), (256, 128), (384, 128), (512, 96), (608, 96)]
ETILES = N * TOPK // P + NX
ROW = E + 4
SPARE = N * TOPK
G = 512
NG = N // G
TPG = G // P
EPS = 1e-5
TINY = float(np.finfo(np.float32).tiny)


def shape_tables():
    f32 = np.float32
    angle = (f32(1.0) / f32(10000.0) ** np.linspace(0.0, 1.0, DH // 2, dtype=f32)).astype(f32)
    phase = (np.arange(N, dtype=f32)[:, None] * angle[None, :]).astype(f32)
    cos = np.repeat(np.cos(phase), 2, axis=1).astype(f32)
    sin = np.repeat(np.sin(phase), 2, axis=1).astype(f32)
    sin[:, 0::2] *= -1
    tiled = lambda a: np.ascontiguousarray(a.reshape(NT, P, -1).transpose(1, 0, 2)).astype(f32)
    log_gamma = np.log(f32(1.0) - f32(2.0) ** (f32(-5.0) - np.arange(H, dtype=f32))).astype(np.float64)
    s = np.arange(P)
    dist = s[None, :] - s[:, None]
    decay = np.where(dist[:, None, :] >= 0, np.exp(np.maximum(dist, 0)[:, None, :] * log_gamma[None, :, None]), 0.0)
    q_decay = np.exp((s[:, None] + 1) * log_gamma[None, :])
    v_decay = np.exp((P - 1 - s[:, None]) * log_gamma[None, :])
    norm = np.sqrt(np.cumsum(np.exp(np.arange(N)[:, None] * log_gamma[None, :]), axis=0))
    chunk = np.exp(P * log_gamma)
    same = (np.arange(P)[:, None] // DH == np.arange(H)[None, :] % (H // 2)).astype(f32)
    state_mask = np.broadcast_to(same[:, :, None], (P, H, DH + 1))
    state_decay = np.broadcast_to(chunk[None, :, None], (P, H, DH + 1))
    return {
        "t_cos": tiled(cos), "t_sin": tiled(sin), "t_norm": tiled(norm),
        "t_decay": decay.astype(f32).reshape(P, H * P), "t_qdecay": q_decay.astype(f32), "t_vdecay": v_decay.astype(f32),
        "t_smask": np.ascontiguousarray(state_mask).astype(f32), "t_sdecay": np.ascontiguousarray(state_decay).astype(f32),
        "t_ident": np.eye(P, dtype=f32),
        "t_before": np.ascontiguousarray(np.broadcast_to(np.tril(np.ones((NX, NX), f32), -1)[None], (P, NX, NX))),
        "t_later": np.triu(np.ones((P, P), f32), 1),
        "t_steps": np.ascontiguousarray(np.broadcast_to((P * np.arange(NX, dtype=f32))[None], (P, NX))),
        "t_tiles": np.ascontiguousarray(np.broadcast_to(np.arange(ETILES, dtype=f32)[None], (P, ETILES))),
        "t_dest": (np.arange(TOPK)[None, :, None] * N + np.arange(NT)[None, None, :] * P + s[:, None, None]).astype(np.int32),
        "t_spare": (SPARE + np.arange(4)[None, :] * P + s[:, None]).astype(np.int32),
    }


def per(count, t):
    return t * count + count


def upto(t):
    return min(t + 1, NT) if isinstance(t, int) else t + 1


def build(nc, io, out):
    ctx = ExitStack()
    dram = {n: nc.dram_tensor(n, shape, F32, kind="Internal").ap() for n, shape in (
        ("dispatched", (ETILES * P, ROW)), ("results", (N * TOPK + 4 * P, E)), ("x3_rows", (N, E)), ("x4_rows", (N, E)))}
    with ctx:
        scopes = [ctx]

        def sb(name, shape, dt=F32, side="left"):
            return scopes[-1].enter_context(nc.sbuf_tensor(name, shape, dt, side=side))

        phase_sems = []

        def sem(name):
            phase_sems.append(nc.alloc_semaphore(name))
            return phase_sems[-1]

        def release_sems():
            nc.clear_and_free_semaphores(phase_sems)
            nc.all_engine_barrier()
            phase_sems.clear()

        def alone(eng):
            eng.nop(nofuse=True)

        def wait(eng, s, value):
            if isinstance(value, int) and value <= 0:
                return
            eng.wait_ge(s, value)

        bank = [ctx.enter_context(nc.psum_tensor(f"bank{b}", [P, 512], F32)) for b in range(8)]

        ident = sb("ident", [P, P])
        neghalf, eps = sb("neghalf", [P, H]), sb("eps", [P, H])
        gb = sb("gb", [P, E])
        weights = sb("weights", [P, TOPK, NT])
        tile_expert = sb("tile_expert", [P, ETILES], mybir.dt.int32)
        s_filled = nc.alloc_semaphore("filled")
        s_down = nc.alloc_semaphore("down_in")

        late = ctx.enter_context(ExitStack())
        with ExitStack() as routed:
            with ExitStack() as attended:
                scopes.append(attended)
                modb = sb("modb", [P, 6, E])
                h_all = sb("h_all", [P, NT, E])
                x2T = [sb(f"x2T_{n}", [P, KB, N], F32R) for n in ("hi", "lo")]
                wf1 = [sb(f"wf1_{n}", [P, KB, F], F32R) for n in ("hi", "lo")]
                wf2 = [sb(f"wf2_{n}", [P, FB, E], F32R) for n in ("hi", "lo")]
                setup_and_attention(nc, io, scopes, sb, sem, wait, alone, bank, ident, neghalf, eps, modb, gb,
                                    h_all, x2T, wf1, wf2)
                release_sems()
                scopes.append(late)
                rows = sb("rows", [P, NT, ROW], side="right")
                scopes.pop()
                scopes.append(routed)
                h3T = [sb(f"h3T_{n}", [P, KB, N], F32R, side="right") for n in ("hi", "lo")]
                logits = sb("logits", [P, NT, NR], side="right")
                order = sb("order", [P, NT, NX], side="right")
                chosen = sb("chosen", [P, NT, NX], side="right")
                before_tile = sb("before_tile", [P, NT + 1, NX], side="right")
                ebefore = sb("ebefore", [P, NX, NX], side="right")
                wsg = [sb(f"wsg_{n}", [P, KB, 2 * SI], F32R, side="right") for n in ("hi", "lo")]
                scopes.pop()
                mlp(nc, io, scopes, sb, sem, wait, alone, bank, ident, neghalf, eps, modb, h_all, x2T, wf1, wf2, h3T,
                    rows, logits, order, chosen, before_tile, ebefore, wsg, dram, s_filled)
                release_sems()
                scopes.pop()
            wgu = [sb(f"wgu_{n}", [P, KB, NX, GU], F32R) for n in ("hi", "lo")]
            shared_and_dispatch(nc, io, scopes, sb, sem, wait, alone, bank, gb, weights, tile_expert, h3T, rows, logits,
                                order, chosen, before_tile, ebefore, wsg, wgu, dram, s_filled, s_down)
            release_sems()
        experts(nc, io, scopes, sb, sem, wait, alone, bank, ident, gb, tile_expert, wgu, rows, dram, s_down)
        release_sems()
        combine(nc, scopes, sb, sem, wait, weights, rows, dram, out)


def setup_and_attention(nc, io, scopes, sb, sem, wait, alone, bank, ident, neghalf, eps, modb, gb, h_all, x2T, wf1, wf2):
    with ExitStack() as local:
        scopes.append(local)
        cos, sin = sb("cos", [P, NT, DH]), sb("sin", [P, NT, DH])
        norm = sb("norm", [P, NT, H])
        decay = sb("decay", [P, H, P])
        qdecay, vdecay = sb("qdecay", [P, H]), sb("vdecay", [P, H])
        smask, sdecay = sb("smask", [P, H, DH + 1]), sb("sdecay", [P, H, DH + 1])
        rw, fw = sb("rw", [P, KB]), sb("fw", [P, KB])
        rwk = sb("rwk", [P, KB])
        ccol, scol = sb("ccol", [P, KB]), sb("scol", [P, KB])
        wmod = sb("wmod", [P, KB, 6 * E])
        sign = sb("sign", [P, E])
        rot1, rot2 = sb("rot1", [P, 2 * H, DH]), sb("rot2", [P, 2 * H, DH])
        wo32 = rot1[:, :, :].rearrange("p (k h) d -> p k (h d)", k=KB)
        probs = sb("probs", [P, H, P])
        wq32 = probs[:, :, :].rearrange("p (k n) s -> p k (n s)", k=KB)
        w1_32 = h_all[:, NT // 2:NT, :].rearrange("p (k n) e -> p k (n e)", k=KB)
        w2_32 = probs[:, :, :].rearrange("p (b n) s -> p b (n s)", b=FB)
        wq = [sb(f"wq_{n}", [P, KB, 4 * E], F32R) for n in ("hi", "lo")]
        wo = [sb(f"wo_{n}", [P, KB, E], F32R) for n in ("hi", "lo")]
        xt = sb("xt", [P, 2, E])
        st6, mv, ve, rstd = sb("st6", [P, 2, 6]), sb("mv", [P, 2, 2]), sb("ve", [P, 2, 1]), sb("rstd", [P, 2, 1])
        xn, hm = sb("xn", [P, 2, E]), sb("hm", [P, E])
        junk = sign
        ssq, ssq2 = sb("ssq", [P, 2, 1]), sb("ssq2", [P, 2, 1])
        mse, mse2 = sb("mse", [P, 2, 1]), sb("mse2", [P, 2, 1])
        rms, rms2 = sb("rms", [P, 2, 1]), sb("rms2", [P, 2, 1])
        hr, x2r = sb("hr", [P, 2, E]), sb("x2r", [P, 2, E])
        hT = [sb(f"hT_{n}", [P, 2, KB, P], F32R) for n in ("hi", "lo")]
        qk = sb("qk", [P, 2, 2 * H, DH])
        qk2 = sb("qk2", [P, 2 * H, 4, DH], F32R)
        q_parts, k_parts = qk2[:, 0:H, :, :], qk2[:, H:2 * H, :, :]
        HI, LO = (q_parts[:, :, 0:2, :], k_parts[:, :, 0::2, :]), (q_parts[:, :, 2:4, :], k_parts[:, :, 1::2, :])

        def twice(heads):
            return heads.unsqueeze(2).broadcast_to([P, H, 2, DH])

        qs = sb("qs", [P, E])
        vpad = sb("vpad", [P, 2, H, STRIP])
        vs = sb("vs", [P, 2, H, DH + 1])
        sg = sb("sg", [P, 2, E])
        qbd = sb("qbd", [P, PAIRS, 2 * P], F32R)
        kT = sb("kT", [P, PAIRS, P], F32R)
        qsT = sb("qsT", [P, KB, P])
        state = sb("state", [P, H, STRIP])
        state_new, state_old = sb("state_new", [P, H, DH + 1]), sb("state_old", [P, H, DH + 1])
        oT = sb("oT", [P, 4, P])
        rabs, den, rden = sb("rabs", [P, H]), sb("den", [P, H]), sb("rden", [P, H])
        on, osq, og = sb("on", [P, H, DH]), sb("osq", [P, H, DH]), sb("og", [P, H, DH])
        oms, omse, orms = sb("oms", [P, H]), sb("omse", [P, H]), sb("orms", [P, H])
        y = sb("y", [P, 2, E])
        yT = [sb(f"yT_{n}", [P, KB, P], F32R) for n in ("hi", "lo")]

        b_hT, b_qk, b_vg, b_o = bank[0], bank[1], bank[2], bank[7]
        b_s = bank[3:7]

        names = """rwk wq_in wo_in w1_in w2_in wq_hi wq_lo wo_hi wo_lo w1_hi w1_lo w2_ga w2_hi w2_lo eps tables decay_in vecs wmod_in x_in0 x_in1 silu_c mod_ps mod_sb sgn gates prep init
            st6 mv ve rstd xn hm h ssq mse rms hr hT_ps hT_hi hT_lo qk_ps vg_ps rope qk qk_hi qk_lo qs v sg vs
            qT_ps kT_ps q_ev k_ev qsT_ps qsT sc_ps probs inter o_ps st_ps st_new st_old state oT oTT_ps
            rabs den rden on osq og oms omse orms y yT_ps yT_hi yT_lo out_ps x2 ssq2 mse2 rms2 x2r x2T_ps x2_hi x2_lo""".split()
        S = {n: sem("s_" + n) for n in names}

        block = local.enter_context(nc.Block())
        x_tiles = io["L0_attn_x"].rearrange("a (t p) e -> (a t) p e", p=P)
        LAGS = 3

        def pipeline(eng, body):
            for t in range(6):
                body(t, t % 2, lambda lag, t=t: t - lag >= 0)
            with eng.Fori(3, NT // 2) as j:
                for p in range(2):
                    body(j * 2 + p, p, lambda lag: True)
            for t in range(NT, NT + LAGS):
                body(t, t % 2, lambda lag, t=t: t - lag < NT)

        @block.sync
        def _(sp):
            def load_x(t, p):
                wait(sp, S["xn"], per(1, t - 2))
                sp.dma_start(xt[:, p, :], x_tiles[t, :, :]).then_inc(S[f"x_in{p}"], 16)

            sp.dma_start(ccol[:, :], io["L0_c"]).then_inc(S["vecs"], 16)
            sp.dma_start(rw[:, :], io["L0_attn_retn_norm_w"]).then_inc(S["vecs"], 16)
            sp.dma_start(fw[:, :], io["L0_attn_final_norm_w"]).then_inc(S["vecs"], 16)
            sp.dma_start(wmod[:, :, :], io["L0_wmod"].rearrange("(k p) n -> p k n", p=P)).then_inc(S["wmod_in"], 16)
            load_x(0, 0)
            load_x(1, 1)
            for n, w in enumerate(("q", "k", "v", "g")):
                sp.dma_start(wq32[:, :, n * E:(n + 1) * E], io[f"L0_attn_{w}_w"].rearrange("(k p) n -> p k n", p=P)).then_inc(S["wq_in"], 16)
            sp.dma_start(wo32[:, :, :], io["L0_attn_out_w"].rearrange("(k p) n -> p k n", p=P)).then_inc(S["wo_in"], 16)
            sp.dma_start(decay[:, :, :], io["t_decay"].rearrange("p (h s) -> p h s", h=H)).then_inc(S["decay_in"], 16)
            sp.wait_ge(S["wq_lo"], 3 * KB)
            sp.dma_start(w2_32, io["L0_attn_fc2_w"].rearrange("(k p) n -> p k n", p=P)).then_inc(S["w2_in"], 16)
            sp.dma_start(w1_32[:, :, :], io["L0_attn_fc1_w"].rearrange("(k p) n -> p k n", p=P)).then_inc(S["w1_in"], 16)

            with sp.Fori(1, NT // 2) as j:
                load_x(j * 2, 0)
                load_x(j * 2 + 1, 1)

        TABLES = [(ident, "t_ident"), (cos, "t_cos"), (sin, "t_sin"), (norm, "t_norm"), (qdecay, "t_qdecay"),
                  (vdecay, "t_vdecay"), (smask, "t_smask"), (sdecay, "t_sdecay")]
        ALL_TABLES, PREP = 16 * len(TABLES), 6
        QKVG = [(k, cols, scale) for k in range(KB) for cols, scale in ((slice(0, E), rw), (slice(E, 2 * E), rwk), (slice(2 * E, 4 * E), rw))]

        @block.scalar
        def _(act):
            for dst, name in TABLES:
                src = io[name]
                act.dma_start(dst[tuple([slice(None)] * len(dst.shape))], src).then_inc(S["tables"], 16)
            act.wait_ge(S["vecs"], 48)
            nc.scalar.activation(scol[:, :], ccol[:, :], ACT.Silu).then_inc(S["silu_c"], 1)
            for c in range(3):
                act.wait_ge(S["mod_ps"], c + 1)
                nc.scalar.copy(modb[:, 2 * c:2 * c + 2, :], bank[c][:, :]).then_inc(S["mod_sb"], 1)
            act.wait_ge(S["wq_in"], 64)
            act.wait_ge(S["rwk"], 1)
            for k, cols, scale in QKVG:
                nc.scalar.activation(wq[0][:, k, cols], wq32[:, k, cols], ACT.Identity, scale=scale[:, k:k + 1]).then_inc(S["wq_hi"], 1)
            act.wait_ge(S["init"], 1)
            act.wait_ge(S["prep"], PREP)

            def high_weights(t):
                if t == 0:
                    act.wait_ge(S["wo_in"], 16)
                    nc.scalar.copy(wo[0][:, :, :], wo32[:, :, :]).then_inc(S["wo_hi"], 1)
                if t == 1:
                    act.wait_ge(S["w2_ga"], 1)
                    nc.scalar.copy(wf2[0][:, :, :], w2_32).then_inc(S["w2_hi"], 1)
                if t == 3:
                    act.wait_ge(S["w1_in"], 16)
                    for k in range(KB):
                        nc.scalar.activation(wf1[0][:, k, :], w1_32[:, k, :], ACT.Identity, scale=fw[:, k:k + 1]).then_inc(S["w1_hi"], 1)

            def square_h(t, p):
                act.wait_ge(S["h"], per(1, t))
                wait(act, S["mse"], per(1, t - 2))
                nc.scalar.activation(junk[:, :], h_all[:, t, :], ACT.Square, scale=E ** -0.5, accum_out=ssq[:, p, :]).then_inc(S["ssq"], 1)

            def split_hT(t, p):
                act.wait_ge(S["hT_ps"], per(1, t))
                wait(act, S["vg_ps"], per(1, t - 2))
                nc.scalar.copy(hT[0][:, p, :, :], b_hT[:, 0:E]).then_inc(S["hT_hi"], 1)

            def split_qk(t, p):
                act.wait_ge(S["qk"], per(1, t))
                wait(act, S["kT_ps"], per(2, t - 1))
                for n in range(2):
                    nc.scalar.copy(HI[n], twice(qk[:, p, n * H:n * H + H, :])).then_inc(S["qk_hi"], 1)

            def value_gate(t, p):
                act.wait_ge(S["vg_ps"], per(1, t))
                wait(act, S["o_ps"], per(1, t - 2))
                wait(act, S["vs"], per(1, t - 2))
                nc.scalar.copy(vpad[:, p, :, 0:DH], b_vg[:, 0:E].rearrange("p (h d) -> p h d", d=DH)).then_inc(S["v"], 1)
                wait(act, S["og"], per(1, t - 2))
                nc.scalar.activation(sg[:, p, :], b_vg[:, E:2 * E], ACT.Silu).then_inc(S["sg"], 1)

            def evacuate_q(t, p):
                wait(act, S["sc_ps"], per(4, t - 1))
                for b in range(2):
                    act.wait_ge(S["qT_ps"], per(2, t) - 1 + b)
                    for half in range(2):
                        rows = slice(64 * half, 64 * half + 64)
                        nc.scalar.copy(qbd[rows, 4 * b:4 * b + 4, P * half:P * half + P],
                                       b_s[b][rows, :].rearrange("p (j s) -> p j s", s=P)).then_inc(S["q_ev"], 1)

            def evacuate_qsT(t, p):
                act.wait_ge(S["qsT_ps"], per(1, t))
                wait(act, S["inter"], per(1, t - 1))
                nc.scalar.copy(qsT[:, :, :], b_qk[:, 0:E]).then_inc(S["qsT"], 1)

            def evacuate_oT(t, p):
                act.wait_ge(S["o_ps"], per(1, t))
                wait(act, S["oTT_ps"], per(1, t - 1))
                nc.scalar.copy(oT[:, :, :], b_o[:, :]).then_inc(S["oT"], 1)

            def square_o(t, p):
                act.wait_ge(S["on"], per(1, t))
                wait(act, S["oms"], per(1, t - 1))
                nc.scalar.activation(osq[:, :, :], on[:, :, :], ACT.Square, scale=DH ** -0.5).then_inc(S["osq"], 1)

            def split_yT(t, p):
                act.wait_ge(S["yT_ps"], per(1, t))
                wait(act, S["out_ps"], per(1, t - 1))
                nc.scalar.copy(yT[0][:, :, :], b_vg[:, 0:E]).then_inc(S["yT_hi"], 1)

            def square_x2(t, p):
                act.wait_ge(S["x2"], per(1, t))
                wait(act, S["mse2"], per(1, t - 2))
                nc.scalar.activation(junk[:, :], h_all[:, t, :], ACT.Square, scale=E ** -0.5, accum_out=ssq2[:, p, :]).then_inc(S["ssq2"], 1)

            def split_x2T(t, p):
                act.wait_ge(S["x2T_ps"], per(1, t))
                nc.scalar.copy(x2T[0][:, :, bass.ds(t * P, P)], b_hT[:, 0:E].rearrange("p (k s) -> p k s", s=P)).then_inc(S["x2_hi"], 1)

            def body(t, p, live):
                q = 1 - p
                if isinstance(t, int):
                    high_weights(t)
                if live(1): value_gate(t - 1, q)
                if live(1): split_qk(t - 1, q)
                if live(0): square_h(t, p)
                if live(2): evacuate_oT(t - 2, p)
                if live(1): evacuate_q(t - 1, q)
                if live(0): split_hT(t, p)
                if live(3): split_yT(t - 3, q)
                if live(1): evacuate_qsT(t - 1, q)
                if live(3): square_x2(t - 3, q)
                if live(2): square_o(t - 2, p)
                if live(3): split_x2T(t - 3, q)

            pipeline(nc.scalar, body)

        @block.gpsimd
        def _(pool):
            nc.gpsimd.memset(neghalf[:, :], -0.5).then_inc(S["prep"], 1)
            nc.gpsimd.memset(eps[:, :], EPS).then_inc(S["eps"], 1)
            nc.gpsimd.memset(vpad[:, :, :, :], 0.0).then_inc(S["prep"], 1)
            nc.gpsimd.memset(state[:, :, :], 0.0).then_inc(S["prep"], 1)
            pool.wait_ge(S["eps"], 1)
            pool.wait_ge(S["prep"], 3)
            nc.gpsimd.memset(vpad[:, :, :, DH:DH + 1], 1.0).then_inc(S["prep"], 1)
            pool.wait_ge(S["tables"], ALL_TABLES)
            for p in range(2):
                nc.gpsimd.tensor_copy(vs[:, p, :, DH:DH + 1], vdecay[:, :].unsqueeze(2)).then_inc(S["prep"], 1)
            pool.wait_ge(S["prep"], PREP)
            pool.wait_ge(S["mod_sb"], 3)
            pool.wait_ge(S["sgn"], 1)

            def rms_scale(src, ready, tmp, tmp_name, dst, dst_name, t, p, reader):
                pool.wait_ge(S[ready], per(1, t))
                nc.gpsimd.tensor_tensor(tmp, src, eps[:, 0:tmp.shape[1]], ALU.add).then_inc(S[tmp_name], 1)
                pool.wait_ge(S[tmp_name], per(1, t))
                wait(pool, S[reader], per(1, t - 2))
                nc.gpsimd.tensor_tensor(dst, tmp, neghalf[:, 0:tmp.shape[1]], ALU.pow).then_inc(S[dst_name], 1)

            def rstd_x(t, p):
                pool.wait_ge(S["ve"], per(1, t))
                nc.gpsimd.tensor_tensor(rstd[:, p, :], ve[:, p, :], neghalf[:, 0:1], ALU.pow).then_inc(S["rstd"], 1)

            def modulate(t, p):
                pool.wait_ge(S["xn"], per(1, t))
                wait(pool, S["h"], per(1, t - 1))
                nc.gpsimd.tensor_tensor(hm[:, :], xn[:, p, :], modb[:, 1, :], ALU.mult).then_inc(S["hm"], 1)
                pool.wait_ge(S["hm"], per(1, t))
                nc.gpsimd.tensor_tensor(h_all[:, t, :], hm[:, :], modb[:, 0, :], ALU.add).then_inc(S["h"], 1)

            def rms_h(t, p):
                rms_scale(ssq[:, p, :], "ssq", mse[:, p, :], "mse", rms[:, p, :], "rms", t, p, "hr")

            def rope_add(t, p):
                pool.wait_ge(S["rope"], per(3, t))
                wait(pool, S["st_ps"], per(1, t - 2))
                nc.gpsimd.tensor_tensor(qk[:, p, :, :], rot1[:, :, :], rot2[:, :, :], ALU.add).then_inc(S["qk"], 1)

            def decay_q(t, p):
                pool.wait_ge(S["qk"], per(1, t))
                wait(pool, S["qsT_ps"], per(1, t - 1))
                nc.gpsimd.tensor_tensor(qs[:, :].rearrange("p (h d) -> p h d", d=DH), qk[:, p, 0:H, :],
                                        qdecay[:, :].unsqueeze(2).broadcast_to([P, H, DH]), ALU.mult).then_inc(S["qs"], 1)

            def decay_v(t, p):
                pool.wait_ge(S["v"], per(1, t))
                wait(pool, S["st_ps"], per(1, t - 2))
                nc.gpsimd.tensor_tensor(vs[:, p, :, 0:DH], vpad[:, p, :, 0:DH],
                                        vdecay[:, :].unsqueeze(2).broadcast_to([P, H, DH]), ALU.mult).then_inc(S["vs"], 1)

            def decay_state(t, p):
                wait(pool, S["state"], per(1, t - 1))
                nc.gpsimd.tensor_tensor(state_old[:, :, :], state[:, :, 0:DH + 1], sdecay[:, :, :], ALU.mult).then_inc(S["st_old"], 1)

            def gate_o(t, p):
                pool.wait_ge(S["on"], per(1, t))
                pool.wait_ge(S["sg"], per(1, t))
                wait(pool, S["y"], per(1, t - 1))
                nc.gpsimd.tensor_tensor(og[:, :, :], on[:, :, :], sg[:, p, :].rearrange("p (h d) -> p h d", d=DH), ALU.mult).then_inc(S["og"], 1)

            def rms_o(t, p):
                pool.wait_ge(S["oms"], per(1, t))
                nc.gpsimd.tensor_tensor(omse[:, :], oms[:, :], eps[:, :], ALU.add).then_inc(S["omse"], 1)
                pool.wait_ge(S["omse"], per(1, t))
                wait(pool, S["y"], per(1, t - 1))
                nc.gpsimd.tensor_tensor(orms[:, :], omse[:, :], neghalf[:, :], ALU.pow).then_inc(S["orms"], 1)

            def scale_o(t, p):
                pool.wait_ge(S["orms"], per(1, t))
                pool.wait_ge(S["og"], per(1, t))
                wait(pool, S["yT_ps"], per(1, t - 2))
                nc.gpsimd.tensor_tensor(y[:, p, :].rearrange("p (h d) -> p h d", d=DH), og[:, :, :],
                                        orms[:, :].unsqueeze(2).broadcast_to([P, H, DH]), ALU.mult).then_inc(S["y"], 1)

            def rms_x2(t, p):
                rms_scale(ssq2[:, p, :], "ssq2", mse2[:, p, :], "mse2", rms2[:, p, :], "rms2", t, p, "x2r")

            def body(t, p, live):
                q = 1 - p
                if isinstance(t, int) and t == 5:
                    pool.wait_ge(S["w1_lo"], KB)
                if live(0): rstd_x(t, p)
                if live(1): rope_add(t - 1, q)
                if live(1): decay_v(t - 1, q)
                if live(0): modulate(t, p)
                if live(2): decay_state(t - 2, p)
                if live(0): rms_h(t, p)
                if live(1): decay_q(t - 1, q)
                if live(2): gate_o(t - 2, p)
                if live(3): rms_x2(t - 3, q)
                if live(2): rms_o(t - 2, p)
                if live(2): scale_o(t - 2, p)

            pipeline(nc.gpsimd, body)

        @block.vector
        def _(dve):
            count = {}

            def step(name, ins):
                count[name] = count.get(name, 0) + 1
                ins.then_inc(S[name], 1)
                dve.wait_ge(S[name], count[name])

            dve.wait_ge(S["vecs"], 48)
            nc.vector.tensor_scalar(rwk[:, :], rw[:, :], float(DH) ** -0.5, None, ALU.mult).then_inc(S["rwk"], 1)
            nc.vector.memset(qbd[:, :, :].bitcast(F32), 0.0).then_inc(S["init"], 1)
            dve.wait_ge(S["mod_sb"], 3)
            ca1 = modb[:, 1, :]
            step("sgn", nc.vector.tensor_scalar(ca1, ca1, 1.0, None, ALU.add))
            for g, gated in ((modb[:, 2, :], modb[:, 2, :]), (modb[:, 5, :], gb[:, :])):
                step("sgn", nc.vector.tensor_scalar(sign[:, :], g, 0.0, 2.0, ALU.is_ge, ALU.mult))
                step("sgn", nc.vector.tensor_scalar(sign[:, :], sign[:, :], 1.0, None, ALU.subtract))
                step("sgn", nc.vector.tensor_tensor(g, g, sign[:, :], ALU.mult))
                step("gates", nc.vector.scalar_tensor_tensor(gated, g, 0.25, sign[:, :], ALU.max, ALU.mult))
            nc.vector.tensor_scalar(modb[:, 4, :], modb[:, 4, :], 1.0, None, ALU.add).then_inc(S["gates"], 1)
            for n, (k, cols, scale) in enumerate(QKVG):
                dve.wait_ge(S["wq_hi"], n + 1)
                nc.vector.scalar_tensor_tensor(wq[1][:, k, cols], wq32[:, k, cols], scale[:, k:k + 1], wq[0][:, k, cols].bitcast(F32),
                                               ALU.mult, ALU.subtract).then_inc(S["wq_lo"], 1)
            dve.wait_ge(S["tables"], ALL_TABLES)
            dve.wait_ge(S["prep"], PREP)

            def low_weights(t):
                if t == 0:
                    dve.wait_ge(S["wo_hi"], 1)
                    nc.vector.tensor_tensor(wo[1][:, :, :], wo32[:, :, :], wo[0][:, :, :].bitcast(F32), ALU.subtract).then_inc(S["wo_lo"], 1)
                if t == 1:
                    dve.wait_ge(S["w2_in"], 16)
                    dve.wait_ge(S["gates"], 1)
                    nc.vector.tensor_tensor(w2_32, w2_32, modb[:, 2, :].unsqueeze(1).broadcast_to([P, FB, E]), ALU.mult).then_inc(S["w2_ga"], 1)
                    dve.wait_ge(S["w2_hi"], 1)
                    nc.vector.tensor_tensor(wf2[1][:, :, :], w2_32, wf2[0][:, :, :].bitcast(F32), ALU.subtract).then_inc(S["w2_lo"], 1)
                if t == 2:
                    dve.wait_ge(S["decay_in"], 16)
                if t == 3:
                    for k in range(KB):
                        dve.wait_ge(S["w1_hi"], k + 1)
                        nc.vector.scalar_tensor_tensor(wf1[1][:, k, :], w1_32[:, k, :], fw[:, k:k + 1], wf1[0][:, k, :].bitcast(F32),
                                                       ALU.mult, ALU.subtract).then_inc(S["w1_lo"], 1)

            def stats(t, p):
                dve.wait_ge(S[f"x_in{p}"], (t - p) * 8 + 16)
                nc.vector.bn_stats(st6[:, p, :], xt[:, p, :]).then_inc(S["st6"], 1)
                dve.wait_ge(S["st6"], per(1, t))
                alone(dve)
                nc.vector.bn_aggr(mv[:, p, :], st6[:, p, :]).then_inc(S["mv"], 1)
                dve.wait_ge(S["mv"], per(1, t))
                wait(dve, S["rstd"], per(1, t - 2))
                nc.vector.tensor_scalar(ve[:, p, :], mv[:, p, 1:2], EPS, None, ALU.add).then_inc(S["ve"], 1)

            def normalise(t, p):
                dve.wait_ge(S["rstd"], per(1, t))
                wait(dve, S["hm"], per(1, t - 2))
                nc.vector.tensor_scalar(xn[:, p, :], xt[:, p, :], mv[:, p, 0:1], rstd[:, p, :], ALU.subtract, ALU.mult).then_inc(S["xn"], 1)

            def scale_h(t, p):
                dve.wait_ge(S["rms"], per(1, t))
                wait(dve, S["hT_ps"], per(1, t - 2))
                nc.vector.tensor_scalar(hr[:, p, :], h_all[:, t, :], rms[:, p, :], None, ALU.mult).then_inc(S["hr"], 1)

            def split_hT(t, p):
                dve.wait_ge(S["hT_hi"], per(1, t))
                wait(dve, S["vg_ps"], per(1, t - 2))
                nc.vector.tensor_tensor(hT[1][:, p, :, :].rearrange("p k s -> p (k s)"), b_hT[:, 0:E],
                                        hT[0][:, p, :, :].bitcast(F32).rearrange("p k s -> p (k s)"), ALU.subtract).then_inc(S["hT_lo"], 1)

            def rope(t, p):
                dve.wait_ge(S["qk_ps"], per(1, t))
                wait(dve, S["qk"], per(1, t - 1))
                heads = b_qk[:, :].rearrange("p (h d) -> p h d", d=DH)
                odd_even = b_qk[:, :].rearrange("p (h d two) -> p h d two", d=DH // 2, two=2)
                r2 = rot2[:, :, :].rearrange("p h (d two) -> p h d two", two=2)
                nc.vector.tensor_tensor(rot1[:, :, :], heads, cos[:, t, :].unsqueeze(1).broadcast_to([P, 2 * H, DH]), ALU.mult).then_inc(S["rope"], 1)
                sn = sin[:, t, :].rearrange("p (d two) -> p d two", two=2)
                for e in range(2):
                    nc.vector.tensor_tensor(r2[:, :, :, e], odd_even[:, :, :, 1 - e],
                                            sn[:, :, e].unsqueeze(1).broadcast_to([P, 2 * H, DH // 2]), ALU.mult).then_inc(S["rope"], 1)

            def split_qk(t, p):
                for n in range(2):
                    dve.wait_ge(S["qk_hi"], per(2, t) - 1 + n)
                    nc.vector.tensor_tensor(LO[n], twice(qk[:, p, n * H:n * H + H, :]), HI[n].bitcast(F32), ALU.subtract).then_inc(S["qk_lo"], 1)

            def evacuate_k(t, p):
                wait(dve, S["sc_ps"], per(4, t - 1))
                for b in range(2):
                    dve.wait_ge(S["kT_ps"], per(2, t) - 1 + b)
                    nc.vector.tensor_copy(kT[:, 4 * b:4 * b + 4, :], b_s[2 + b][:, :].rearrange("p (j s) -> p j s", s=P)).then_inc(S["k_ev"], 1)

            def mask(t, p):
                wait(dve, S["o_ps"], per(1, t - 1))
                for b in range(4):
                    dve.wait_ge(S["sc_ps"], per(4, t) - 3 + b)
                    nc.vector.tensor_tensor(probs[:, 4 * b:4 * b + 4, :], b_s[b][:, :].rearrange("p (h s) -> p h s", s=P),
                                            decay[:, 4 * b:4 * b + 4, :], ALU.mult).then_inc(S["probs"], 1)

            def update_state(t, p):
                dve.wait_ge(S["st_ps"], per(1, t))
                nc.vector.tensor_tensor(state_new[:, :, :], b_vg[:, 0:H * (DH + 1)].rearrange("p (h d) -> p h d", d=DH + 1),
                                        smask[:, :, :], ALU.mult).then_inc(S["st_new"], 1)
                dve.wait_ge(S["st_new"], per(1, t))
                dve.wait_ge(S["st_old"], per(1, t))
                dve.wait_ge(S["inter"], per(1, t))
                nc.vector.tensor_tensor(state[:, :, 0:DH + 1], state_new[:, :, :], state_old[:, :, :], ALU.add).then_inc(S["state"], 1)

            def normalise_o(t, p):
                dve.wait_ge(S["oTT_ps"], per(1, t))
                o = b_hT[:, :].rearrange("p (h d) -> p h d", d=STRIP)
                nc.vector.tensor_reduce(rabs[:, :], o[:, :, DH:DH + 1], AX.X, ALU.max, apply_absolute_value=True).then_inc(S["rabs"], 1)
                dve.wait_ge(S["rabs"], per(1, t))
                nc.vector.tensor_tensor(den[:, :], rabs[:, :], norm[:, t, :], ALU.max).then_inc(S["den"], 1)
                dve.wait_ge(S["den"], per(1, t))
                nc.vector.reciprocal(rden[:, :], den[:, :]).then_inc(S["rden"], 1)
                dve.wait_ge(S["rden"], per(1, t))
                wait(dve, S["og"], per(1, t - 1))
                wait(dve, S["osq"], per(1, t - 1))
                nc.vector.tensor_tensor(on[:, :, :], o[:, :, 0:DH], rden[:, :].unsqueeze(2).broadcast_to([P, H, DH]), ALU.mult).then_inc(S["on"], 1)

            def mean_square_o(t, p):
                dve.wait_ge(S["osq"], per(1, t))
                wait(dve, S["omse"], per(1, t - 1))
                nc.vector.tensor_reduce(oms[:, :], osq[:, :, :], AX.X, ALU.add).then_inc(S["oms"], 1)

            def split_yT(t, p):
                dve.wait_ge(S["yT_hi"], per(1, t))
                wait(dve, S["out_ps"], per(1, t - 1))
                nc.vector.tensor_tensor(yT[1][:, :, :].rearrange("p k s -> p (k s)"), b_vg[:, 0:E],
                                        yT[0][:, :, :].bitcast(F32).rearrange("p k s -> p (k s)"), ALU.subtract).then_inc(S["yT_lo"], 1)

            def residual(t, p):
                dve.wait_ge(S["out_ps"], per(1, t))
                nc.vector.tensor_tensor(h_all[:, t, :], b_qk[:, 0:E], h_all[:, t, :], ALU.add).then_inc(S["x2"], 1)

            def scale_x2(t, p):
                dve.wait_ge(S["rms2"], per(1, t))
                wait(dve, S["x2T_ps"], per(1, t - 2))
                nc.vector.tensor_scalar(x2r[:, p, :], h_all[:, t, :], rms2[:, p, :], None, ALU.mult).then_inc(S["x2r"], 1)

            def split_x2T(t, p):
                dve.wait_ge(S["x2_hi"], per(1, t))
                cols = bass.ds(t * P, P)
                nc.vector.tensor_tensor(x2T[1][:, :, cols], b_hT[:, 0:E].rearrange("p (k s) -> p k s", s=P),
                                        x2T[0][:, :, cols].bitcast(F32), ALU.subtract).then_inc(S["x2_lo"], 1)

            def body(t, p, live):
                q = 1 - p
                if isinstance(t, int):
                    low_weights(t)
                if live(0): stats(t, p)
                if live(1): rope(t - 1, q)
                if live(0): normalise(t, p)
                if live(2): mask(t - 2, p)
                if live(1): split_qk(t - 1, q)
                if live(2): update_state(t - 2, p)
                if live(0): scale_h(t, p)
                if live(1): evacuate_k(t - 1, q)
                if live(0): split_hT(t, p)
                if live(3): split_yT(t - 3, q)
                if live(2): normalise_o(t - 2, p)
                if live(3): residual(t - 3, q)
                if live(2): mean_square_o(t - 2, p)
                if live(3): scale_x2(t - 3, q)
                if live(3): split_x2T(t - 3, q)

            pipeline(nc.vector, body)

        @block.tensor
        def _(pe):
            pe.wait_ge(S["silu_c"], 1)
            pe.wait_ge(S["wmod_in"], 16)
            for c in range(3):
                for k in range(KB):
                    mm = nc.tensor.matmul(bank[c][:, :], scol[:, k:k + 1].broadcast_to([P, P]), wmod[:, k, 512 * c:512 * c + 512],
                                          start=(k == 0), stop=(k == KB - 1))
                mm.then_inc(S["mod_ps"], 1)
            pe.wait_ge(S["mod_sb"], 3)
            pe.wait_ge(S["wq_lo"], 3 * KB)
            pe.wait_ge(S["tables"], ALL_TABLES)
            pe.wait_ge(S["prep"], PREP)

            def product3(dst, lhs, rhs, start, stop):
                nc.tensor.matmul(dst, lhs[0], rhs[0], start=start, stop=False)
                nc.tensor.matmul(dst, lhs[0], rhs[1], start=False, stop=False)
                return nc.tensor.matmul(dst, lhs[1], rhs[0], start=False, stop=stop)

            def transpose_h(t, p):
                pe.wait_ge(S["hr"], per(1, t))
                wait(pe, S["hT_lo"], per(1, t - 1))
                wait(pe, S["x2_lo"], per(1, t - 4))
                wait(pe, S["on"], per(1, t - 3))
                for k in range(KB):
                    tr = nc.tensor.transpose(b_hT[:, k * P:k * P + P], hr[:, p, k * P:k * P + P], ident[:, :])
                tr.then_inc(S["hT_ps"], 1)

            def project(t, p):
                pe.wait_ge(S["hT_lo"], per(1, t))
                wait(pe, S["rope"], per(3, t - 1))
                wait(pe, S["qsT"], per(1, t - 1))
                wait(pe, S["x2"], per(1, t - 3))
                for k in range(KB):
                    mm = product3(b_qk[:, :], [a[:, p, k, :] for a in hT], [w[:, k, 0:512] for w in wq], k == 0, k == KB - 1)
                mm.then_inc(S["qk_ps"], 1)
                wait(pe, S["sg"], per(1, t - 1))
                wait(pe, S["st_new"], per(1, t - 2))
                wait(pe, S["yT_lo"], per(1, t - 3))
                for k in range(KB):
                    mm = product3(b_vg[:, :], [a[:, p, k, :] for a in hT], [w[:, k, 512:1024] for w in wq], k == 0, k == KB - 1)
                mm.then_inc(S["vg_ps"], 1)

            def transpose_qk(t, p):
                wait(pe, S["probs"], per(4, t - 1))
                for n, done in enumerate(("qT_ps", "kT_ps")):
                    pe.wait_ge(S["qk_lo"], per(2, t) - 1 + n)
                    for j in range(PAIRS):
                        src = qk2[:, n * H + 2 * j:n * H + 2 * j + 2, :, :].bitcast(F32).rearrange("p h part d -> p (h part d)")
                        tr = nc.tensor.transpose(b_s[2 * n + j // 4][:, (j % 4) * P:(j % 4) * P + P], src, ident[:, :])
                        if j % 4 == 3:
                            tr.then_inc(S[done], 1)

            def transpose_qs(t, p):
                pe.wait_ge(S["qs"], per(1, t))
                pe.wait_ge(S["rope"], per(3, t))
                for k in range(KB):
                    tr = nc.tensor.transpose(b_qk[:, k * P:k * P + P], qs[:, k * P:k * P + P], ident[:, :])
                tr.then_inc(S["qsT_ps"], 1)

            def scores(t, p):
                pe.wait_ge(S["q_ev"], per(4, t))
                pe.wait_ge(S["k_ev"], per(2, t))
                for b in range(4):
                    for j in (2 * b, 2 * b + 1):
                        mm = nc.tensor.matmul(b_s[b][:, (j % 2) * 2 * P:(j % 2) * 2 * P + 2 * P], kT[:, j, :], qbd[:, j, :], start=True, stop=True)
                    mm.then_inc(S["sc_ps"], 1)

            def retain(t, p):
                wait(pe, S["oT"], per(1, t - 1))
                pe.wait_ge(S["qsT"], per(1, t))
                wait(pe, S["state"], per(1, t - 1))
                for g in range(4):
                    mm = nc.tensor.matmul(b_o[:, g * P:g * P + P], state[:, 4 * g:4 * g + 4, :], qsT[:, g // 2, :],
                                          start=(g == 0), stop=(g == 3), skip_group_check=True)
                mm.then_inc(S["inter"], 1)
                pe.wait_ge(S["v"], per(1, t))
                for h in range(H):
                    if h % 4 == 0:
                        pe.wait_ge(S["probs"], per(4, t) - 3 + h // 4)
                    r = STRIP * (h % 4)
                    mm = nc.tensor.matmul(b_o[r:r + STRIP, (h // 4) * P:(h // 4) * P + P], vpad[:, p, h, :], probs[:, h, :],
                                          start=False, stop=(h == H - 1), skip_group_check=True)
                mm.then_inc(S["o_ps"], 1)

            def state_update(t, p):
                pe.wait_ge(S["vs"], per(1, t))
                pe.wait_ge(S["sg"], upto(t + 1))
                for a in range(2):
                    mm = nc.tensor.matmul(b_vg[:, a * 8 * (DH + 1):(a + 1) * 8 * (DH + 1)],
                                          qk[:, p, H + 8 * a:H + 8 * a + 8, :], vs[:, p, 8 * a:8 * a + 8, :], start=True, stop=True)
                mm.then_inc(S["st_ps"], 1)

            def transpose_o(t, p):
                pe.wait_ge(S["oT"], per(1, t))
                pe.wait_ge(S["hT_lo"], upto(t + 2))
                wait(pe, S["x2_lo"], per(1, t - 2))
                for g in range(4):
                    tr = nc.tensor.transpose(b_hT[:, g * P:g * P + P], oT[:, g, :], ident[:, :])
                tr.then_inc(S["oTT_ps"], 1)

            def transpose_y(t, p):
                pe.wait_ge(S["y"], per(1, t))
                pe.wait_ge(S["st_new"], upto(t + 1))
                for k in range(KB):
                    tr = nc.tensor.transpose(b_vg[:, k * P:k * P + P], y[:, p, k * P:k * P + P], ident[:, :])
                tr.then_inc(S["yT_ps"], 1)

            def project_out(t, p):
                pe.wait_ge(S["yT_lo"], per(1, t))
                pe.wait_ge(S["qsT"], upto(t + 2))
                for k in range(KB):
                    mm = product3(b_qk[:, 0:E], [a[:, k, :] for a in yT], [w[:, k, :] for w in wo], k == 0, k == KB - 1)
                mm.then_inc(S["out_ps"], 1)

            def transpose_x2(t, p):
                pe.wait_ge(S["x2r"], per(1, t))
                pe.wait_ge(S["on"], upto(t + 1))
                wait(pe, S["x2_lo"], per(1, t - 1))
                for k in range(KB):
                    tr = nc.tensor.transpose(b_hT[:, k * P:k * P + P], x2r[:, p, k * P:k * P + P], ident[:, :])
                tr.then_inc(S["x2T_ps"], 1)

            def body(t, p, live):
                q = 1 - p
                if isinstance(t, int) and t == LAGS:
                    pe.wait_ge(S["wo_lo"], 1)
                if live(2): state_update(t - 2, p)
                if live(2): retain(t - 2, p)
                if live(1): transpose_qk(t - 1, q)
                if live(1): transpose_qs(t - 1, q)
                if live(0): transpose_h(t, p)
                if live(3): transpose_y(t - 3, q)
                if live(1): scores(t - 1, q)
                if live(2): transpose_o(t - 2, p)
                if live(3): project_out(t - 3, q)
                if live(3): transpose_x2(t - 3, q)
                if live(0): project(t, p)

            pipeline(nc.tensor, body)
        local.close()
        scopes.pop()


def mlp(nc, io, scopes, sb, sem, wait, alone, bank, ident, neghalf, eps, modb, h_all, x2T, wf1, wf2, h3T,
        rows, logits, order, chosen, before_tile, ebefore, wsg, dram, s_filled):
    with ExitStack() as local:
        scopes.append(local)
        b1, b2 = sb("b1", [P, FB]), sb("b2", [P, E])
        wr = sb("wr", [P, KB, NR])
        xt = sb("xt2", [P, TPG, E])
        res = sb("res", [P, TPG, E])
        RING = 4
        act1 = sb("act1", [P, 2, G])
        a1 = [sb(f"a1_{n}", [P, RING, G], F32R) for n in ("hi", "lo")]
        early = sb("early", [P, (TPG + 2) * E])
        h3 = early[:, 0:TPG * E].rearrange("p (t e) -> p t e", e=E)
        versus = early[:, TPG * E:(TPG + 2) * E].rearrange("p (t e x) -> p t e x", t=2, x=NX)
        stage = early[:, 0:2 * KB * GU].rearrange("p (c k n) -> p c k n", c=2, k=KB)
        st6, mv, ve, rstd = sb("m_st6", [P, 2, 6]), sb("m_mv", [P, 2, 2]), sb("m_ve", [P, 2, 1]), sb("m_rstd", [P, 2, 1])
        xn = sb("m_xn", [P, 2, E])
        hT32 = sb("hT32", [P, 2, KB, P])
        fill, spare = sb("fill", [P, 4, ROW]), sb("spare", [P, 4], mybir.dt.int32)
        names = """st_in0 st_in1 w_hi w_lo zeros spare_in fill gab xb b2in wr_in x_in0 x_in1 x_in2 x_in3 res1 res2 res f_ps act a_hi a_lo fc2 x3
            st6 mv ve rstd xn hm h3 tr_ps h32 hi lo lg_ps lg versus ahead order chosen start before
            x3_out row_out0 row_out1 row_out2 row_out3 tab_in""".split()
        S = {n: sem("m_" + n) for n in names}
        block = local.enter_context(nc.Block())
        x_tiles = io["L0_attn_x"].rearrange("a (t p) e -> (a t) p e", p=P)
        hidden = [bank[n] for n in (0, 1, 2, 7)]
        outs = bank[3:5]
        b_tr, b_lg = bank[5], bank[6]
        SKEW = 2
        TAIL = FB - TPG

        SCH = 2 * SI // GU

        def chunk(n):
            cols = slice(n * GU, n * GU + GU)
            return stage[:, n % 2, :, :], [w[:, :, cols] for w in wsg]

        def groups(eng, body):
            body(0, True)
            body(1, False)
            with eng.Fori(2, NG) as g:
                body(g, False)

        @block.sync
        def _(sp):
            sp.dma_start(b1[:, :], io["L0_attn_fc1_b"]).then_inc(S["b2in"], 16)
            sp.dma_start(b2[:, :], io["L0_attn_fc2_b"].partition_broadcast(P)).then_inc(S["b2in"], 16)
            sp.dma_start(wr[:, :, :], io["router_w"].rearrange("(k p) n -> p k n", p=P)).then_inc(S["wr_in"], 16)

            def load_x(g, i):
                wait(sp, S["res"], (g - 1) * TPG + i + 1)
                sp.dma_start(xt[:, i, :], x_tiles[g * TPG + i, :, :]).then_inc(S[f"x_in{i}"], 16)

            def store(t, i):
                sp.wait_ge(S["x3"], per(1, t))
                sp.dma_start(x3_tiles[t, :, :], h_all[:, t, :]).then_inc(S["x3_out"], 16)
                sp.wait_ge(S["h3"], per(1, t))
                sp.dma_start(rows[:, t, 0:E], h3[:, i, :]).then_inc(S[f"row_out{i}"], 16)

            sp.dma_start(ebefore[:, :, :], io["t_before"]).then_inc(S["tab_in"], 16)
            sp.dma_start(spare[:, :], io["t_spare"]).then_inc(S["spare_in"], 16)
            x3_tiles = dram["x3_rows"].rearrange("(t p) e -> t p e", p=P)
            for i in range(TPG):
                load_x(0, i)

            unused = dram["dispatched"].rearrange("(m r p) c -> m p r c", r=4, p=P)
            FILLS = ETILES // 4 // NG

            def fill_rows(g):
                for n in range(FILLS):
                    sp.dma_start(unused[g * FILLS + n, :, :, :], fill[:, :, :]).then_inc(s_filled, 16)

            sp.wait_ge(S["fill"], 1)
            def load_shared(n):
                wait(sp, S["w_lo"], n - 1)
                sp.dma_start(stage[:, n % 2, :, :], io["shared_gu"].rearrange("(k p) n -> p k n", p=P)[:, :, n * GU:n * GU + GU]).then_inc(S[f"st_in{n % 2}"], 16)

            for n in range(SCH):
                load_shared(n)

            def body(g, first):
                fill_rows(g)
                if not first:
                    for i in range(TPG):
                        load_x(g, i)
                    for i in range(TPG):
                        store((g - 1) * TPG + i, i)

            groups(nc.sync, body)
            for i in range(TPG):
                store(NT - TPG + i, i)
            sp.wait_ge(s_filled, 16 * (ETILES // 4))
            sp.wait_ge(S["x3_out"], 16 * NT)
            for i in range(TPG):
                sp.wait_ge(S[f"row_out{i}"], 16 * NG)

        @block.gpsimd
        def _(pool):
            nc.gpsimd.memset(fill[:, :, :], 0.0).then_inc(S["zeros"], 1)
            pool.wait_ge(S["zeros"], 1)
            pool.wait_ge(S["spare_in"], 16)
            nc.gpsimd.tensor_copy(fill[:, :, E:E + 1].bitcast(mybir.dt.int32), spare[:, :].unsqueeze(2)).then_inc(S["fill"], 1)
            pool.wait_ge(S["b2in"], 32)

            def gate_x2(g, i):
                t = g * TPG + i
                wait(pool, S["x3"], per(1, t - TPG))
                nc.gpsimd.tensor_tensor(res[:, i, :], h_all[:, t, :], modb[:, 2, :], ALU.mult).then_inc(S["res1"], 1)

            def residual(g, i):
                t = g * TPG + i
                pool.wait_ge(S["res1"], per(1, t))
                pool.wait_ge(S["xb"], per(1, t))
                nc.gpsimd.tensor_tensor(res[:, i, :], res[:, i, :], xt[:, i, :], ALU.add).then_inc(S["res"], 1)

            def add_bias(g, i):
                pool.wait_ge(S[f"x_in{i}"], g * 16 + 16)
                nc.gpsimd.tensor_tensor(xt[:, i, :], xt[:, i, :], b2[:, :], ALU.add).then_inc(S["xb"], 1)

            def inverse_std(g, i):
                t, p = g * TPG + i, i % 2
                pool.wait_ge(S["ve"], per(1, t))
                nc.gpsimd.tensor_tensor(rstd[:, p, :], ve[:, p, :], neghalf[:, 0:1], ALU.pow).then_inc(S["rstd"], 1)

            def modulate(g, i):
                t, p = g * TPG + i, i % 2
                pool.wait_ge(S["xn"], per(1, t))
                nc.gpsimd.tensor_tensor(xn[:, p, :], xn[:, p, :], modb[:, 4, :], ALU.mult).then_inc(S["hm"], 1)
                pool.wait_ge(S["hm"], per(1, t))
                wait(pool, S["tr_ps"], per(1, t - TPG))
                wait(pool, S[f"row_out{i}"], g * 16)
                nc.gpsimd.tensor_tensor(h3[:, i, :], xn[:, p, :], modb[:, 3, :], ALU.add).then_inc(S["h3"], 1)

            nc.gpsimd.tensor_tensor(b2[:, :], b2[:, :], modb[:, 2, :], ALU.mult).then_inc(S["gab"], 1)
            pool.wait_ge(S["gab"], 1)

            def body(g, first):
                for i in range(TPG):
                    add_bias(g, i)
                if not first:
                    for i in range(TPG):
                        inverse_std(g - 1, i)
                        modulate(g - 1, i)
                        gate_x2(g, i)
                else:
                    for i in range(TPG):
                        gate_x2(g, i)
                for i in range(TPG):
                    residual(g, i)

            groups(nc.gpsimd, body)
            for i in range(TPG):
                inverse_std(NG - 1, i)
                modulate(NG - 1, i)

        @block.scalar
        def _(act):
            act.wait_ge(S["b2in"], 32)

            def gelu(g, b):
                n = g * FB + b
                act.wait_ge(S["f_ps"], n + 1)
                wait(act, S["a_lo"], n - 1)
                nc.scalar.activation(act1[:, b % 2, :], hidden[b % RING][:, :], ACT.Gelu_apprx_tanh, bias=b1[:, b:b + 1]).then_inc(S["act"], 1)
                act.wait_ge(S["act"], n + 1)
                wait(act, S["fc2"], n - 3)
                nc.scalar.copy(a1[0][:, b % RING, :], act1[:, b % 2, :]).then_inc(S["a_hi"], 1)

            def evacuate(g, i):
                t, p = g * TPG + i, i % 2
                act.wait_ge(S["tr_ps"], per(1, t))
                wait(act, S["lo"], per(1, t - 2))
                wait(act, S["lg_ps"], per(1, t - 2))
                nc.scalar.copy(hT32[:, p, :, :], b_tr[:, 0:E]).then_inc(S["h32"], 1)
                act.wait_ge(S["h32"], per(1, t))
                nc.scalar.copy(h3T[0][:, :, bass.ds(t * P, P)], hT32[:, p, :, :]).then_inc(S["hi"], 1)

            def body(g, first):
                for b in range(FB):
                    gelu(g, b)
                    if first and b < SCH:
                        st, dst = chunk(b)
                        act.wait_ge(S[f"st_in{b % 2}"], (b // 2 + 1) * 16)
                        nc.scalar.copy(dst[0], st).then_inc(S["w_hi"], 1)
                    if not first and b >= TAIL:
                        evacuate(g - 1, b - TAIL)

            groups(nc.scalar, body)
            for i in range(TPG):
                evacuate(NG - 1, i)

        @block.vector
        def _(dve):
            nc.vector.memset(before_tile[:, 0, :], 0.0).then_inc(S["start"], 1)
            dve.wait_ge(S["start"], 1)
            dve.wait_ge(S["tab_in"], 16)

            def split(g, b):
                n = g * FB + b
                dve.wait_ge(S["a_hi"], n + 1)
                nc.vector.tensor_tensor(a1[1][:, b % RING, :], act1[:, b % 2, :], a1[0][:, b % RING, :].bitcast(F32), ALU.subtract).then_inc(S["a_lo"], 1)

            def add_residual(g, i):
                t = g * TPG + i
                dve.wait_ge(S["fc2"], per(FB, g))
                dve.wait_ge(S["res"], per(1, t))
                nc.vector.tensor_tensor(h_all[:, t, :], outs[i // 2][:, (i % 2) * E:(i % 2) * E + E], res[:, i, :], ALU.add).then_inc(S["x3"], 1)

            def stats(g, i):
                t, p = g * TPG + i, i % 2
                dve.wait_ge(S["x3"], per(1, t))
                alone(dve)
                nc.vector.bn_stats(st6[:, p, :], h_all[:, t, :]).then_inc(S["st6"], 1)
                dve.wait_ge(S["st6"], per(1, t))
                alone(dve)
                nc.vector.bn_aggr(mv[:, p, :], st6[:, p, :]).then_inc(S["mv"], 1)
                dve.wait_ge(S["mv"], per(1, t))
                nc.vector.tensor_scalar(ve[:, p, :], mv[:, p, 1:2], EPS, None, ALU.add).then_inc(S["ve"], 1)

            def normalise(g, i):
                t, p = g * TPG + i, i % 2
                dve.wait_ge(S["rstd"], per(1, t))
                wait(dve, S["h3"], per(1, t - 2))
                nc.vector.tensor_scalar(xn[:, p, :], h_all[:, t, :], mv[:, p, 0:1], rstd[:, p, :], ALU.subtract, ALU.mult).then_inc(S["xn"], 1)

            def low_part(g, i):
                t, p = g * TPG + i, i % 2
                dve.wait_ge(S["hi"], per(1, t))
                cols = bass.ds(t * P, P)
                nc.vector.tensor_tensor(h3T[1][:, :, cols], hT32[:, p, :, :], h3T[0][:, :, cols].bitcast(F32), ALU.subtract).then_inc(S["lo"], 1)

            def keep_logits(g, i):
                t = g * TPG + i
                dve.wait_ge(S["lg_ps"], per(1, t))
                nc.vector.tensor_copy(logits[:, t, :], b_lg[:, 0:NR]).then_inc(S["lg"], 1)

            def compare(g, h):
                t, u = g * TPG + 2 * h, g * 2 + h
                two = bass.ds(t, 2)
                dve.wait_ge(S["lg"], t + 2)
                nc.vector.tensor_tensor(versus[:, :, :, :], logits[:, two, 0:NX].unsqueeze(2).broadcast_to([P, 2, NX, NX]),
                                        logits[:, two, 0:NX].unsqueeze(3).broadcast_to([P, 2, NX, NX]), ALU.subtract).then_inc(S["versus"], 1)
                dve.wait_ge(S["versus"], u + 1)
                nc.vector.scalar_tensor_tensor(versus[:, :, :, :], ebefore[:, :, :].unsqueeze(1).broadcast_to([P, 2, NX, NX]), -TINY,
                                               versus[:, :, :, :], ALU.mult, ALU.is_lt).then_inc(S["ahead"], 1)

            def choose(g, h):
                t, u = g * TPG + 2 * h, g * 2 + h
                two = bass.ds(t, 2)
                dve.wait_ge(S["ahead"], u + 1)
                nc.vector.tensor_reduce(order[:, two, :], versus[:, :, :, :], AX.X, ALU.add).then_inc(S["order"], 1)
                dve.wait_ge(S["order"], u + 1)
                nc.vector.tensor_scalar(chosen[:, two, :], order[:, two, :], TOPK - 0.5, None, ALU.is_lt).then_inc(S["chosen"], 1)
                dve.wait_ge(S["chosen"], u + 1)
                for n in range(2):
                    wait(dve, S["before"], t + n)
                    nc.vector.tensor_tensor(before_tile[:, bass.ds(t + n + 1, 1), :], before_tile[:, bass.ds(t + n, 1), :],
                                            chosen[:, bass.ds(t + n, 1), :], ALU.add).then_inc(S["before"], 1)

            def finish(g, i):
                if i < TPG:
                    stats(g, i)
                if i:
                    normalise(g, i - 1)

            def body(g, first):
                for b in range(FB):
                    if first and 0 < b <= SCH:
                        st, dst = chunk(b - 1)
                        dve.wait_ge(S["w_hi"], b)
                        nc.vector.tensor_tensor(dst[1], st, dst[0].bitcast(F32), ALU.subtract).then_inc(S["w_lo"], 1)
                    if not first and b == SKEW:
                        for i in range(TPG):
                            add_residual(g - 1, i)
                    split(g, b)
                    if not first and b >= SKEW and b <= SKEW + TPG:
                        finish(g - 1, b - SKEW)
                    if not first and b >= TAIL:
                        low_part(g - 1, b - TAIL)
                    if not first and b > TAIL:
                        keep_logits(g - 1, b - TAIL - 1)
                    if not first and b == FB - 2:
                        compare(g - 1, 0)
                    if not first and b == FB - 1:
                        choose(g - 1, 0)
                    if b == 0 and not (isinstance(g, int) and g < 2):
                        keep_logits(g - 2, TPG - 1)
                        compare(g - 2, 1)
                    if b == 1 and not (isinstance(g, int) and g < 2):
                        choose(g - 2, 1)

            groups(nc.vector, body)
            for i in range(TPG):
                add_residual(NG - 1, i)
            for i in range(TPG + 1):
                finish(NG - 1, i)
                if i == 1:
                    keep_logits(NG - 2, TPG - 1)
                    compare(NG - 2, 1)
                if i == 2:
                    choose(NG - 2, 1)
            for i in range(TPG):
                low_part(NG - 1, i)
                keep_logits(NG - 1, i)

        @block.tensor
        def _(pe):
            pe.wait_ge(S["wr_in"], 16)

            def first_product(g, b):
                n = g * FB + b
                wait(pe, S["act"], n - 3)
                cols = bass.ds(g * G, G)
                for k in range(KB):
                    m = slice(b * P, b * P + P)
                    for i, (wn, xn_) in enumerate(((0, 0), (0, 1), (1, 0))):
                        mm = nc.tensor.matmul(hidden[b % RING][:, :], wf1[wn][:, k, m], x2T[xn_][:, k, cols],
                                              start=(k == 0 and i == 0), stop=(k == KB - 1 and i == 2))
                mm.then_inc(S["f_ps"], 1)

            def second_product(g, b):
                n = g * FB + b
                pe.wait_ge(S["a_lo"], n + 1)
                if b == 0:
                    wait(pe, S["x3"], g * TPG)
                for i in range(TPG):
                    dst = outs[i // 2][:, (i % 2) * E:(i % 2) * E + E]
                    cols = slice(i * P, i * P + P)
                    for j, (an, wn) in enumerate(((0, 0), (0, 1), (1, 0))):
                        mm = nc.tensor.matmul(dst, a1[an][:, b % RING, cols], wf2[wn][:, b, :],
                                              start=(b == 0 and j == 0 and i % 2 == 0), stop=(b == FB - 1 and j == 2), skip_group_check=True)
                mm.then_inc(S["fc2"], 1)

            def transpose_h3(g, i):
                t = g * TPG + i
                pe.wait_ge(S["h3"], per(1, t))
                wait(pe, S["h32"], per(1, t - 1))
                for k in range(KB):
                    tr = nc.tensor.transpose(b_tr[:, k * P:k * P + P], h3[:, i, k * P:k * P + P], ident[:, :])
                tr.then_inc(S["tr_ps"], 1)

            def route(g, i):
                t, p = g * TPG + i, i % 2
                pe.wait_ge(S["h32"], per(1, t))
                wait(pe, S["lg"], per(1, t - 1))
                for k in range(KB):
                    mm = nc.tensor.matmul(b_lg[:, 0:NR], hT32[:, p, k, :], wr[:, k, :], start=(k == 0), stop=(k == KB - 1))
                mm.then_inc(S["lg_ps"], 1)

            def body(g, first):
                for b in range(FB):
                    first_product(g, b)
                    if b >= SKEW:
                        second_product(g, b - SKEW)
                    elif not first:
                        second_product(g - 1, FB - SKEW + b)
                    if b == 0 and not (isinstance(g, int) and g < 2):
                        route(g - 2, TPG - 1)
                    if not first and b > TAIL:
                        route(g - 1, b - TAIL - 1)
                    if not first and b >= TAIL:
                        transpose_h3(g - 1, b - TAIL)

            groups(nc.tensor, body)
            for b in range(FB - SKEW, FB):
                second_product(NG - 1, b)
            route(NG - 2, TPG - 1)
            for i in range(TPG):
                transpose_h3(NG - 1, i)
                route(NG - 1, i)
        scopes.pop()


def shared_and_dispatch(nc, io, scopes, sb, sem, wait, alone, bank, gb, weights, tile_expert, h3T, rows, logits,
                        order, chosen, before_tile, ebefore, wsg, wgu, dram, s_filled, s_down):
    INT = mybir.dt.int32
    NB = len(SBLOCKS)
    RING, SKEW = 3, 2
    with ExitStack() as local:
        scopes.append(local)
        wsd = [sb(f"wsd_{n}", [P, NB, E], F32R) for n in ("hi", "lo")]
        stage = sb("stage", [P, 2, KB, GU])
        hid = sb("hid", [P, 2, G])
        a1 = [sb(f"s_a1_{n}", [P, RING, G], F32R) for n in ("hi", "lo")]
        x4, sh = sb("s_x4", [P, TPG, E]), sb("sh", [P, 2, E])
        sgate = sb("sgate", [P, NT])
        later, ones = sh[:, 0, 0:P], sh[:, 0, P:2 * P]
        versus = sh[:, 1, :].rearrange("p (e x) -> p e x", x=NX)
        steps, tile_no = sb("steps", [P, NX]), sb("tile_no", [P, ETILES])
        dest = sb("dest", [P, TOPK, NT], INT)
        best = sb("best", [P, NT])
        pick, slot = sb("pick", [P, NT, NX]), sb("slot", [P, TOPK, NT], INT)
        slot_e, slot32, cmp_, ez = ebefore, weights, pick, chosen
        used, base, end = sb("used", [P, NX]), sb("base", [P, NX]), sb("end", [P, NX])
        base_row = sb("base_row", [P, NX])
        ecount = sb("ecount", [1, ETILES])
        wsum, wrec = sb("wsum", [P, NT]), sb("wrec", [P, NT])
        names = """tab_in ones st_in0 st_in1 w_hi w_lo z_ps g_ps u_ps act hid a_hi a_lo fc2 x_in0 x_in1 x_in2 x_in3 sh x4 x4_out0 x4_out1 x4_out2 x4_out3
            chain ez exps rank_ps count_ps slots pad col tiles""".split()
        S = {n: sem("r_" + n) for n in names}
        s_sent = [sem(f"r_sent{t}") for t in range(NT)]
        block = local.enter_context(nc.Block())
        gate_b, up_b, b_rank, b_count = bank[0:2], bank[2:4], bank[6], bank[7]
        outs = [bank[4:6], bank[6:8]]
        NCHUNKS = 3
        x3_tiles = dram["x3_rows"].rearrange("(t p) e -> t p e", p=P)
        x4_tiles = dram["x4_rows"].rearrange("(t p) e -> t p e", p=P)

        def groups(eng, body):
            body(0, 0)
            body(1, 1)
            with eng.Fori(1, NG // 2) as j:
                for q in range(2):
                    body(j * 2 + q, q)

        def chunk(n):
            b = 2 * n
            start, m = SBLOCKS[b]
            return (io["shared_d"][start:start + 2 * m, :].rearrange("(b p) n -> p b n", p=m),
                    stage[0:m, n % 2, :, 0:E], [w[0:m, b:b + 2, :] for w in wsd])

        def arrived(n, p):
            return ((n - p) * 8 + 16)

        def expert_chunk(e, p):
            return stage[:, p, :, :], [w[:, :, e, :] for w in wgu]

        @block.sync
        def _(sp):
            for dst, name in ((later, "t_later"), (steps, "t_steps"), (tile_no, "t_tiles"), (dest, "t_dest")):
                sp.dma_start(dst[tuple([slice(None)] * len(dst.shape))], io[name]).then_inc(S["tab_in"], 16)
            for n in range(NCHUNKS):
                src, st, _ = chunk(n)
                wait(sp, S["w_lo"], n - 1)
                sp.dma_start(st, src).then_inc(S[f"st_in{n % 2}"], 16)
            experts_gu = io["expert_gu"].rearrange("(k p) e n -> e p k n", p=P)

            def load_expert(e, i):
                wait(sp, S["w_lo"], NCHUNKS + e - 1)
                p = (NCHUNKS + i) % 2
                sp.dma_start(stage[:, p, :, :], experts_gu[e, :, :, :]).then_inc(S[f"st_in{p}"], 16)

            def load_x3(g, i):
                wait(sp, S[f"x4_out{i}"], g * 16)
                sp.dma_start(x4[:, i, :], x3_tiles[g * TPG + i, :, :]).then_inc(S[f"x_in{i}"], 16)

            def store_x4(g, i):
                sp.wait_ge(S["x4"], g * TPG + i + 1)
                sp.dma_start(x4_tiles[g * TPG + i, :, :], x4[:, i, :]).then_inc(S[f"x4_out{i}"], 16)


            def body(g, q):
                first = isinstance(g, int) and g == 0
                for i in range(TPG):
                    if not first and i == 2:
                        for n in range(TPG):
                            store_x4(g - 1, n)
                    load_expert(g * TPG + i, i)
                for i in range(TPG):
                    load_x3(g, i)

            groups(nc.sync, body)
            for t in range(NT):
                sp.wait_ge(s_sent[t], 16 * TOPK)
            sp.dma_start(rows[:, :, 0:E], io["expert_d"][0:P]).then_inc(s_down, 16)
            for i in range(TPG):
                store_x4(NG - 1, i)
            for i in range(TPG):
                sp.wait_ge(S[f"x4_out{i}"], 16 * NG)

        @block.gpsimd
        def _(pool):
            nc.gpsimd.memset(rows[:, :, E:ROW], 0.0).then_inc(S["pad"], 1)
            nc.gpsimd.memset(ones[:, :], 1.0).then_inc(S["ones"], 1)
            pool.wait_ge(S["pad"], 1)
            pool.wait_ge(s_filled, 16 * (ETILES // 4))
            for k in range(TOPK):
                for t in range(NT):
                    wait(pool, s_sent[t], 16 * k)
                if k == 0:
                    pool.wait_ge(S["tab_in"], 64)
                nc.gpsimd.tensor_copy(rows[:, :, E:E + 1].bitcast(INT), dest[:, k, :].unsqueeze(2)).then_inc(S["col"], 1)
                pool.wait_ge(S["col"], k + 1)
                pool.wait_ge(S["slots"], TOPK)
                for t in range(NT):
                    pool.indirect_dma_start(out=dram["dispatched"], out_offset=bass.IndirectOffsetOnAxis(ap=slot[:, k, t:t + 1], axis=0),
                                            in_=rows[:, t, :], in_offset=None).then_inc(s_sent[t], 16)
            for t in range(NT):
                pool.wait_ge(s_sent[t], 16 * TOPK)

        @block.scalar
        def _(act):
            def split(st, dst, n, p):
                act.wait_ge(S[f"st_in{p}"], arrived(n, p))
                nc.scalar.copy(dst[0], st).then_inc(S["w_hi"], 1)

            def exponentials():
                act.wait_ge(S["ez"], 1)
                nc.scalar.activation(ez[:, :, :], ez[:, :, :], ACT.Exp).then_inc(S["exps"], 1)
                nc.scalar.activation(sgate[:, :], logits[:, :, NX], ACT.Exp, scale=-1.0).then_inc(S["exps"], 1)

            def high_down(n):
                _, st, dst = chunk(n)
                split(st, dst, n, n % 2)

            high_down(0)
            high_down(1)

            def hidden(g, b):
                n, m = g * NB + b, SBLOCKS[b][1]
                act.wait_ge(S["g_ps"], n + 1)
                wait(act, S["a_lo"], n - 1)
                nc.scalar.activation(hid[0:m, b % 2, :], gate_b[b % 2][0:m, :], ACT.Silu).then_inc(S["act"], 1)
                act.wait_ge(S["hid"], n + 1)
                wait(act, S["fc2"], n - 2)
                nc.scalar.copy(a1[0][0:m, b % RING, :], hid[0:m, b % 2, :]).then_inc(S["a_hi"], 1)

            def body(g, q):
                for b in range(NB):
                    hidden(g, b)
                    if isinstance(g, int) and g == 0 and b == 1:
                        high_down(2)
                    if isinstance(g, int) and g == 0 and b == NB - 1:
                        exponentials()
                    if 1 <= b <= TPG:
                        p = (NCHUNKS + b - 1) % 2
                        st, dst = expert_chunk(g * TPG + b - 1, p)
                        split(st, dst, NCHUNKS + g * TPG + b - 1, p)

            groups(nc.scalar, body)

        @block.vector
        def _(dve):
            def low(st, dst, n):
                dve.wait_ge(S["w_hi"], n + 1)
                nc.vector.tensor_tensor(dst[1], st, dst[0].bitcast(F32), ALU.subtract).then_inc(S["w_lo"], 1)

            done = [0]

            def chain(ins):
                done[0] += 1
                ins.then_inc(S["chain"], 1)
                dve.wait_ge(S["chain"], done[0])

            def flat(x):
                return x[:, :, :].rearrange("p t e -> p (t e)")

            def choose(t):
                chain(nc.vector.tensor_tensor(versus[:, :, :], logits[:, t, 0:NX].unsqueeze(1).broadcast_to([P, NX, NX]),
                                              logits[:, t, 0:NX].unsqueeze(2).broadcast_to([P, NX, NX]), ALU.subtract))
                chain(nc.vector.scalar_tensor_tensor(versus[:, :, :], ebefore[:, :, :], -TINY, versus[:, :, :], ALU.mult, ALU.is_lt))
                chain(nc.vector.tensor_reduce(order[:, t, :], versus[:, :, :], AX.X, ALU.add))
                chain(nc.vector.tensor_scalar(chosen[:, t, :], order[:, t, :], TOPK - 0.5, None, ALU.is_lt))
                chain(nc.vector.tensor_tensor(before_tile[:, t + 1, :], before_tile[:, t, :], chosen[:, t, :], ALU.add))

            def bases():
                dve.wait_ge(S["tab_in"], 64)
                dve.wait_ge(S["count_ps"], 1)
                chain(nc.vector.tensor_copy(used[:, :], b_count[:, 0:NX]))
                chain(nc.vector.tensor_tensor(cmp_[:, :, :], used[:, :].unsqueeze(2).broadcast_to([P, NX, NX]),
                                              steps[:, :].unsqueeze(1).broadcast_to([P, NX, NX]), ALU.is_gt))
                chain(nc.vector.tensor_reduce(used[:, :], cmp_[:, :, :], AX.X, ALU.add))
                chain(nc.vector.tensor_tensor(cmp_[:, :, :], used[:, :].unsqueeze(1).broadcast_to([P, NX, NX]), ebefore[:, :, :], ALU.mult))
                chain(nc.vector.tensor_reduce(base[:, :], cmp_[:, :, :], AX.X, ALU.add))
                chain(nc.vector.tensor_scalar(base_row[:, :], base[:, :], float(P), None, ALU.mult))
                dve.wait_ge(S["rank_ps"], 1)
                chain(nc.vector.tensor_tensor(slot_e[:, :, :], b_rank[:, 0:NT * NX].rearrange("p (t e) -> p t e", e=NX),
                                              base_row[:, :].unsqueeze(1).broadcast_to([P, NT, NX]), ALU.add))

            def slots(k):
                chain(nc.vector.scalar_tensor_tensor(flat(pick), flat(order), float(k), flat(slot_e), ALU.is_equal, ALU.mult))
                chain(nc.vector.tensor_reduce(slot32[:, k, :], pick[:, :, :], AX.X, ALU.add))
                nc.vector.tensor_copy(slot[:, k, :], slot32[:, k, :]).then_inc(S["slots"], 1)

            def less_best():
                chain(nc.vector.tensor_reduce(best[:, :], logits[:, :, 0:NX], AX.X, ALU.max))
                nc.vector.tensor_tensor(ez[:, :, :], logits[:, :, 0:NX], best[:, :].unsqueeze(2).broadcast_to([P, NT, NX]), ALU.subtract).then_inc(S["ez"], 1)

            def experts_of_tiles(part):
                if part == 0:
                    chain(nc.vector.tensor_tensor(end[:, :], base[:, :], used[:, :], ALU.add))
                    chain(nc.vector.tensor_scalar(ecount[:, :], tile_no[0:1, :], end[0:1, 0:1], None, ALU.is_ge))
                for e in range(max(1, part * NX // 4), (part + 1) * NX // 4):
                    chain(nc.vector.scalar_tensor_tensor(ecount[:, :], tile_no[0:1, :], end[0:1, e:e + 1], ecount[:, :], ALU.is_ge, ALU.add))
                if part == 3:
                    nc.vector.tensor_scalar(tile_expert[0:1, :], ecount[:, :], NX - 1.0, None, ALU.min).then_inc(S["tiles"], 1)

            def shared_gate():
                dve.wait_ge(S["exps"], 2)
                chain(nc.vector.tensor_scalar(sgate[:, :], sgate[:, :], 1.0, None, ALU.add))
                chain(nc.vector.reciprocal(sgate[:, :], sgate[:, :]))

            def weigh(k):
                chain(nc.vector.scalar_tensor_tensor(flat(pick), flat(order), float(k), flat(ez), ALU.is_equal, ALU.mult))
                chain(nc.vector.tensor_reduce(weights[:, k, :], pick[:, :, :], AX.X, ALU.add))

            def share():
                chain(nc.vector.tensor_reduce(wsum[:, :], weights[:, :, :].rearrange("p k t -> p t k"), AX.X, ALU.add))
                chain(nc.vector.reciprocal(wrec[:, :], wsum[:, :]))
                chain(nc.vector.tensor_tensor(weights[:, :, :], weights[:, :, :], wrec[:, :].unsqueeze(1).broadcast_to([P, TOPK, NT]), ALU.mult))

            def low_down(n):
                _, st, dst = chunk(n)
                low(st, dst, n)

            choose(NT - 4)
            low_down(0)
            low_down(1)

            def hidden(g, b):
                n, m = g * NB + b, SBLOCKS[b][1]
                dve.wait_ge(S["act"], n + 1)
                dve.wait_ge(S["u_ps"], n + 1)
                nc.vector.tensor_tensor(hid[0:m, b % 2, :], hid[0:m, b % 2, :], up_b[b % 2][0:m, :], ALU.mult).then_inc(S["hid"], 1)
                dve.wait_ge(S["a_hi"], n + 1)
                wait(dve, S["fc2"], n - 2)
                nc.vector.tensor_tensor(a1[1][0:m, b % RING, :], hid[0:m, b % 2, :], a1[0][0:m, b % RING, :].bitcast(F32), ALU.subtract).then_inc(S["a_lo"], 1)

            def add_shared(g, i, q):
                t, p = g * TPG + i, i % 2
                dve.wait_ge(S["fc2"], per(NB, g))
                wait(dve, S["x4"], per(1, t - 2))
                nc.vector.scalar_tensor_tensor(sh[:, p, :], outs[q][i // 2][:, (i % 2) * E:(i % 2) * E + E], sgate[:, bass.ds(t, 1)],
                                               gb[:, :], ALU.mult, ALU.mult).then_inc(S["sh"], 1)
                dve.wait_ge(S["sh"], per(1, t))
                dve.wait_ge(S[f"x_in{i}"], g * 16 + 16)
                nc.vector.tensor_tensor(x4[:, i, :], sh[:, p, :], x4[:, i, :], ALU.add).then_inc(S["x4"], 1)

            def route(g, b):
                if g == 0 and b == 0:
                    choose(NT - 2)
                    choose(NT - 1)
                elif g == 0 and b == 1:
                    low_down(2)
                    bases()
                elif g == 0 and b in (2, 3):
                    slots(2 * b - 4)
                    slots(2 * b - 3)
                elif g == 0 and b == 4:
                    less_best()
                elif g == 1 and b == 0:
                    shared_gate()
                elif g == 1 and b < 5:
                    experts_of_tiles(b - 1)
                    weigh(b - 1)
                elif g == 1:
                    share()

            def body(g, q):
                for b in range(NB):
                    if b == SKEW and not (isinstance(g, int) and g == 0):
                        for i in range(TPG):
                            add_shared(g - 1, i, 1 - q)
                    if isinstance(g, int) and g == 0 and b == 0:
                        choose(NT - 3)
                    hidden(g, b)
                    if isinstance(g, int):
                        route(g, b)
                    if 1 <= b <= TPG:
                        st, dst = expert_chunk(g * TPG + b - 1, (NCHUNKS + b - 1) % 2)
                        low(st, dst, NCHUNKS + g * TPG + b - 1)

            groups(nc.vector, body)
            for i in range(TPG):
                add_shared(NG - 1, i, (NG - 1) % 2)

        @block.tensor
        def _(pe):
            def count():
                pe.wait_ge(S["ones"], 1)
                pe.wait_ge(S["tab_in"], 64)
                pe.wait_ge(S["chain"], 5 * TPG)
                nc.tensor.matmul(b_count[:, 0:NX], ones[:, :], before_tile[:, NT, :], start=True, stop=True).then_inc(S["count_ps"], 1)
                nc.tensor.matmul(b_rank[:, 0:NT * NX], ones[:, :], before_tile[:, 0:NT, :], start=True, stop=False)
                nc.tensor.matmul(b_rank[:, 0:NT * NX], later[:, :], chosen[:, :, :], start=False, stop=True).then_inc(S["rank_ps"], 1)

            def first_product(g, b):
                n = g * NB + b
                start, m = SBLOCKS[b]
                cols = bass.ds(g * G, G)
                for part, dst, done, free in ((0, gate_b, "g_ps", "act"), (SI, up_b, "u_ps", "hid")):
                    wait(pe, S[free], n - 1)
                    for k in range(KB):
                        for i, (wn, xn_) in enumerate(((0, 0), (0, 1), (1, 0))):
                            mm = nc.tensor.matmul(dst[b % 2][0:m, :], wsg[wn][:, k, part + start:part + start + m], h3T[xn_][:, k, cols],
                                                  start=(k == 0 and i == 0), stop=(k == KB - 1 and i == 2))
                    mm.then_inc(S[done], 1)

            def second_product(g, b, q):
                n, m = g * NB + b, SBLOCKS[b][1]
                if isinstance(g, int) and g == 0:
                    pe.wait_ge(S["w_lo"], b // 2 + 1)
                pe.wait_ge(S["a_lo"], n + 1)
                if b == 0:
                    wait(pe, S["sh"], (g - 1) * TPG)
                    if isinstance(g, int) and g == 1:
                        pe.wait_ge(S["slots"], 1)
                for i in range(TPG):
                    dst = outs[q][i // 2][:, (i % 2) * E:(i % 2) * E + E]
                    for j, (an, wn) in enumerate(((0, 0), (0, 1), (1, 0))):
                        mm = nc.tensor.matmul(dst, a1[an][0:m, b % RING, i * P:i * P + P], wsd[wn][0:m, b, :],
                                              start=(b == 0 and j == 0 and i % 2 == 0), stop=(b == NB - 1 and j == 2), skip_group_check=True)
                mm.then_inc(S["fc2"], 1)

            def body(g, q):
                for b in range(NB):
                    first_product(g, b)
                    if isinstance(g, int) and g == 0 and b == 2:
                        count()
                    if b >= SKEW:
                        second_product(g, b - SKEW, q)
                    elif not (isinstance(g, int) and g == 0):
                        second_product(g - 1, NB - SKEW + b, 1 - q)

            groups(nc.tensor, body)
            for b in range(NB - SKEW, NB):
                second_product(NG - 1, b, (NG - 1) % 2)
        scopes.pop()


def experts(nc, io, scopes, sb, sem, wait, alone, bank, ident, gb, tile_expert, wgu, rows, dram, s_down):
    INT = mybir.dt.int32
    XR, YR = 8, 4
    with ExitStack() as local:
        scopes.append(local)
        wda = [sb(f"wda_{n}", [P, NX, E], F32R) for n in ("hi", "lo")]
        wdb = [sb(f"wdb_{n}", [IT, NX, E], F32R) for n in ("hi", "lo")]
        stage = sb("d_stage", [P, 2, 4, E])
        xe = sb("xe", [P, XR, ROW])
        xT = [sb(f"xT_{n}", [P, 2, KB, P], F32R) for n in ("hi", "lo")]
        sg = sb("e_sg", [P, 2, I])
        hx = sb("hx", [P, 2, 2 * P])
        hT = [sb(f"e_hT_{n}", [P, 4, 2 * P], F32R) for n in ("hi", "lo")]
        yb = sb("yb", [P, YR, E])
        names = "x4_in st_in0 st_in1 w_hi w_lo zero xT_ps x_hi x_lo gu_ps sg hx hT_ps h_hi h_lo y_ps y".split()
        S = {n: sem("e_" + n) for n in names}
        s_in = [sem(f"e_in{r}") for r in range(XR)]
        s_sent = [sem(f"e_sent{r}") for r in range(YR)]
        t_bank, gu_bank, hT_bank, y_bank = bank[0:2], bank[2:4], bank[4:6], bank[6:8]
        dispatched = dram["dispatched"].rearrange("(j p) c -> j p c", p=P)
        NCH = 8
        LAG = 4

        def chunk(n):
            e = 4 * (n % 4)
            if n < 4:
                return rows[:, e:e + 4, 0:E], [x[:, e:e + 4, :] for x in wda]
            return stage[0:IT, n % 2, :, :], [x[:, e:e + 4, :] for x in wdb]

        def sent(j, r):
            return (j - r % YR) * (16 // YR) + 16

        def pipeline(eng, body):
            for t in range(XR):
                body(t, t % XR, lambda lag, t=t: t - lag >= 0)
            with eng.Fori(1, ETILES // XR) as j:
                for r in range(XR):
                    body(j * XR + r, r, lambda lag: True)
            for t in range(ETILES, ETILES + LAG):
                body(t, t % XR, lambda lag, t=t: t - lag < ETILES)

        with nc.Block() as block:
            @block.sync
            def _(sp):
                def load_down(n):
                    if n >= 6:
                        sp.wait_ge(S["w_lo"], n - 1)
                    sp.dma_start(chunk(n)[0], io["expert_d"][P:I, 4 * (n - 4):4 * (n - 4) + 4, :]).then_inc(S[f"st_in{n % 2}"], 16)

                load_down(4)
                load_down(5)

                def body(j, r, live):
                    if live(0):
                        wait(sp, s_sent[r % YR], sent(j - XR, r))
                        sp.dma_start(xe[:, r, :], dispatched[j, :, :]).then_inc(s_in[r], 16)
                    if isinstance(j, int) and j in (2, 3):
                        load_down(j + 4)
                    if isinstance(j, int) and j == XR - 1:
                        sp.wait_ge(S["w_lo"], 4)
                        sp.dma_start(rows[:, :, 0:E], dram["x4_rows"].rearrange("(t p) e -> p t e", p=P)).then_inc(S["x4_in"], 16)

                pipeline(nc.sync, body)
                sp.wait_ge(S["x4_in"], 16)

            @block.gpsimd
            def _(pool):
                nc.gpsimd.memset(hx[:, :, :], 0.0).then_inc(S["zero"], 1)

                def send(j, r):
                    pool.wait_ge(S["y"], per(1, j))
                    alone(pool)
                    pool.indirect_dma_start(out=dram["results"], out_offset=bass.IndirectOffsetOnAxis(ap=xe[:, r, E:E + 1].bitcast(INT), axis=0),
                                            in_=yb[:, r % YR, :], in_offset=None).then_inc(s_sent[r % YR], 16)

                def body(j, r, live):
                    if live(LAG): send(j - LAG, (r - LAG) % XR)

                pipeline(nc.gpsimd, body)
                for r in range(YR):
                    pool.wait_ge(s_sent[r], 16 * ETILES // YR)

            @block.scalar
            def _(act):
                def high_w(n):
                    if n < 4:
                        act.wait_ge(s_down, 16)
                    else:
                        act.wait_ge(S[f"st_in{n % 2}"], (n // 2 - 1) * 16)
                    st, dst = chunk(n)
                    nc.scalar.copy(dst[0], st).then_inc(S["w_hi"], 1)

                def high_x(j, p):
                    act.wait_ge(S["xT_ps"], per(1, j))
                    wait(act, S["gu_ps"], per(1, j - 2))
                    nc.scalar.copy(xT[0][:, p, :, :], t_bank[p][:, 0:E]).then_inc(S["x_hi"], 1)

                def silu(j, p):
                    act.wait_ge(S["gu_ps"], per(1, j))
                    wait(act, S["hx"], per(1, j - 2))
                    nc.scalar.activation(sg[:, p, :], gu_bank[p][:, 0:I], ACT.Silu).then_inc(S["sg"], 1)

                def high_h(j, p, q):
                    act.wait_ge(S["hT_ps"], per(1, j))
                    wait(act, S["y_ps"], per(1, j - 4))
                    nc.scalar.copy(hT[0][:, q, :], hT_bank[p][:, 0:2 * P]).then_inc(S["h_hi"], 1)

                def body(j, r, live):
                    if isinstance(j, int) and j < 4:
                        high_w(2 * j)
                        high_w(2 * j + 1)
                    if live(0): high_x(j, r % 2)
                    if live(1): silu(j - 1, (r - 1) % 2)
                    if live(2): high_h(j - 2, r % 2, (r - 2) % 4)

                pipeline(nc.scalar, body)

            @block.vector
            def _(dve):
                def low_w(n):
                    dve.wait_ge(S["w_hi"], n + 1)
                    st, dst = chunk(n)
                    nc.vector.tensor_tensor(dst[1], st, dst[0].bitcast(F32), ALU.subtract).then_inc(S["w_lo"], 1)

                dve.wait_ge(S["zero"], 1)

                def low_x(j, p):
                    dve.wait_ge(S["x_hi"], per(1, j))
                    nc.vector.tensor_tensor(xT[1][:, p, :, :].rearrange("p k s -> p (k s)"), t_bank[p][:, 0:E],
                                            xT[0][:, p, :, :].bitcast(F32).rearrange("p k s -> p (k s)"), ALU.subtract).then_inc(S["x_lo"], 1)

                def product(j, p):
                    dve.wait_ge(S["sg"], per(1, j))
                    wait(dve, S["hT_ps"], per(1, j - 2))
                    nc.vector.tensor_tensor(hx[:, p, 0:I], sg[:, p, :], gu_bank[p][:, I:GU], ALU.mult).then_inc(S["hx"], 1)

                def low_h(j, p, q):
                    dve.wait_ge(S["h_hi"], per(1, j))
                    nc.vector.tensor_tensor(hT[1][:, q, :], hT_bank[p][:, 0:2 * P], hT[0][:, q, :].bitcast(F32), ALU.subtract).then_inc(S["h_lo"], 1)

                def result(j, r):
                    dve.wait_ge(S["y_ps"], per(1, j))
                    wait(dve, s_sent[r % YR], sent(j - YR, r))
                    nc.vector.tensor_tensor(yb[:, r % YR, :], y_bank[r % 2][:, 0:E], gb[:, :], ALU.mult).then_inc(S["y"], 1)

                def body(j, r, live):
                    if isinstance(j, int) and j < 4:
                        low_w(2 * j)
                        low_w(2 * j + 1)
                    if live(0): low_x(j, r % 2)
                    if live(1): product(j - 1, (r - 1) % 2)
                    if live(2): low_h(j - 2, r % 2, (r - 2) % 4)
                    if live(LAG): result(j - LAG, (r - LAG) % XR)

                pipeline(nc.vector, body)

            @block.tensor
            def _(pe):
                def transpose_x(j, r):
                    pe.wait_ge(s_in[r], (j - r) * (16 // XR) + 16)
                    wait(pe, S["x_lo"], per(1, j - 2))
                    for k in range(KB):
                        tr = nc.tensor.transpose(t_bank[r % 2][:, k * P:k * P + P], xe[:, r, k * P:k * P + P], ident[:, :])
                    tr.then_inc(S["xT_ps"], 1)

                expert_reg = [nc.tensor.alloc_register(f"expert{r}") for r in range(XR)]

                def load_expert(j, r):
                    nc.tensor.reg_load(expert_reg[r], tile_expert[0:1, bass.ds(j, 1)])

                def expert(r):
                    return nc.s_assert_within(nc.tensor.snap(expert_reg[r]), 0, NX - 1, skip_runtime_bounds_check_because="tile_expert is computed as at most NX - 1")

                def gate_up(j, p, e):
                    pe.wait_ge(S["x_lo"], per(1, j))
                    wait(pe, S["hx"], per(1, j - 2))
                    for k in range(KB):
                        for i, (xn_, wn) in enumerate(((0, 0), (0, 1), (1, 0))):
                            mm = nc.tensor.matmul(gu_bank[p][:, 0:GU], xT[xn_][:, p, k, :], wgu[wn][:, k, e, :],
                                                  start=(k == 0 and i == 0), stop=(k == KB - 1 and i == 2))
                    mm.then_inc(S["gu_ps"], 1)

                def transpose_h(j, p):
                    pe.wait_ge(S["hx"], per(1, j))
                    wait(pe, S["h_lo"], per(1, j - 2))
                    for k in range(2):
                        tr = nc.tensor.transpose(hT_bank[p][:, k * P:k * P + P], hx[:, p, k * P:k * P + P], ident[:, :])
                    tr.then_inc(S["hT_ps"], 1)

                def down(j, r, e):
                    p = r % 2
                    pe.wait_ge(S["h_lo"], per(1, j))
                    wait(pe, S["y"], per(1, j - 2))
                    for k, (m, w) in enumerate(((P, wda), (IT, wdb))):
                        for i, (hn, wn) in enumerate(((0, 0), (0, 1), (1, 0))):
                            mm = nc.tensor.matmul(y_bank[p][:, 0:E], hT[hn][0:m, r % 4, k * P:k * P + P], w[wn][0:m, e, :],
                                                  start=(k == 0 and i == 0), stop=(k == 1 and i == 2))
                    mm.then_inc(S["y_ps"], 1)

                def body(j, r, live):
                    if live(0): load_expert(j, r)
                    if live(0): transpose_x(j, r)
                    if live(1): gate_up(j - 1, (r - 1) % 2, expert((r - 1) % XR))
                    if isinstance(j, int) and j == LAG:
                        pe.wait_ge(S["w_lo"], NCH)
                    if live(LAG): down(j - LAG, (r - LAG) % XR, expert((r - LAG) % XR))
                    if live(2): transpose_h(j - 2, r % 2)

                pipeline(nc.tensor, body)

        scopes.pop()


def combine(nc, scopes, sb, sem, wait, weights, rows, dram, out):
    R = 4
    with ExitStack() as local:
        scopes.append(local)
        ys, acc = sb("ys", [P, R, TOPK, E]), sb("acc", [P, R, E])
        s_ys = [sem(f"c_ys{r}") for r in range(R)]
        s_out = [sem(f"c_out{r}") for r in range(R)]
        s_sum = [sem(f"c_sum{k}") for k in range(TOPK)]
        res = dram["results"][0:N * TOPK, :].rearrange("(k t p) e -> t p k e", k=TOPK, p=P)
        out_tiles = out.rearrange("a (t p) e -> (a t) p e", p=P)
        with nc.Block() as block:
            def rounds(eng, body):
                body(0)
                with eng.Fori(1, NT // R) as j:
                    body(j * R)

            @block.sync
            def _(sp):
                def load(t):
                    for r in range(R):
                        wait(sp, s_sum[TOPK - 1], t + r - R + 1)
                        sp.dma_start(ys[:, r, :, :], res[t + r, :, :, :]).then_inc(s_ys[r], 16)

                rounds(nc.sync, load)

            @block.scalar
            def _(act):
                def store(t):
                    for r in range(R):
                        act.wait_ge(s_sum[TOPK - 1], t + r + 1)
                        act.dma_start(out_tiles[t + r, :, :], acc[:, r, :]).then_inc(s_out[r], 16)

                rounds(nc.scalar, store)
                for r in range(R):
                    act.wait_ge(s_out[r], 16 * NT // R)

            @block.vector
            def _(dve):
                def add(t, r, k):
                    if k == 0:
                        dve.wait_ge(s_ys[r], t * 4 + 16)
                        wait(dve, s_out[r], t * 4)
                    else:
                        dve.wait_ge(s_sum[k - 1], t + r + 1)
                    nc.vector.scalar_tensor_tensor(acc[:, r, :], ys[:, r, k, :], weights[:, k, bass.ds(t + r, 1)],
                                                   rows[:, t + r, 0:E] if k == 0 else acc[:, r, :], ALU.mult, ALU.add).then_inc(s_sum[k], 1)

                def sum_round(t):
                    for r in range(0, R, 2):
                        for k in range(TOPK):
                            add(t, r, k)
                            add(t, r + 1, k)

                rounds(nc.vector, sum_round)
        scopes.pop()


_INS = ['L0_attn_x', 'L0_attn_q_w', 'L0_attn_k_w', 'L0_attn_v_w', 'L0_attn_g_w', 'L0_attn_out_w', 'L0_attn_fc1_w',
        'L0_attn_fc1_b', 'L0_attn_fc2_w', 'L0_attn_fc2_b', 'L0_attn_retn_norm_w', 'L0_attn_final_norm_w', 'L0_c', 'L0_wmod']


def kernel(**inputs):
    import concourse.bacc as _bacc
    from concourse.bass_utils import run_bass_kernel_spmd as _run

    nc = _bacc.Bacc("TRN2", target_bir_lowering=False, num_devices=1)
    arrays = {name: np.ascontiguousarray(inputs[name]) for name in _INS}
    for name in ("L0_c", "L0_attn_retn_norm_w", "L0_attn_final_norm_w", "L0_attn_fc1_b"):
        arrays[name] = np.ascontiguousarray(arrays[name].reshape(-1, P).T)
    arrays["router_w"] = np.ascontiguousarray(np.concatenate([inputs["L0_ffn_gate_w"], inputs["L0_ffn_shared_gate_vec"]]).T)
    flat = lambda a: np.ascontiguousarray(a)
    arrays["expert_gu"] = flat(np.transpose(inputs["L0_ffn_expert_gate_up"], (2, 0, 1)))
    arrays["expert_d"] = flat(np.transpose(inputs["L0_ffn_expert_down"], (2, 0, 1)))
    arrays["shared_gu"] = flat(np.transpose(inputs["L0_ffn_shared_gate_up"]))
    arrays["shared_d"] = flat(np.transpose(inputs["L0_ffn_shared_down"]))
    arrays.update(shape_tables())
    io = {n: nc.dram_tensor(n, a.shape, mybir.dt.from_np(a.dtype), kind="ExternalInput").ap() for n, a in arrays.items()}
    out = nc.dram_tensor("out", (1, N, E), F32, kind="ExternalOutput").ap()
    build(nc, io, out)
    r = _run(nc, [arrays], core_ids=[0])
    return r.results[0]["out"]
```
